# Optimizing a Trainium2 kernel written in Bass

```python
import numpy as np
import jax
import jax.numpy as jnp

def _softmax(x, axis=-1):
    return jax.nn.softmax(x, axis=axis)

def _gelu(x):
    return jax.nn.gelu(x, approximate=True)

def _silu(x):
    return jax.nn.silu(x)

def _sigmoid(x):
    return jax.nn.sigmoid(x)

def _layernorm(x, axis=-1, eps=1e-05):
    m = jnp.mean(x, axis=axis, keepdims=True)
    v = jnp.var(x, axis=axis, keepdims=True)
    return (x - m) / jnp.sqrt(v + eps)

def _scatter_add(tgt, idx, src, axis=0):
    return tgt.at[idx].add(src)

def _segment_sum(src, seg, n):
    return jax.ops.segment_sum(src, seg, n)
kernel_name = 'mk_cond_seq_d1_seqx_r4_e9ce3f'

def setup_inputs(seed: int=0):
    np.random.seed(seed)
    _w = jnp.asarray

    def _rec_inputs():
        import jax
        import jax.numpy as jnp
        _rk = jax.random.key(seed)
        x = 1.648e-05 + 1 * jax.random.normal(jax.random.fold_in(_rk, 1), (2, 1024, 288), jnp.float32)
        _lenS = 1024 - jax.random.randint(jax.random.fold_in(_rk, 7), (2,), 0, max(1, 1024 // 4) + 1, jnp.int32)
        _lenS2 = 1024 - jax.random.randint(jax.random.fold_in(_rk, 8), (2,), 0, max(1, 1024 // 4) + 1, jnp.int32)
        cond_1152 = 0.00914911 + 1.00357 * jax.random.normal(jax.random.fold_in(_rk, 11), (2, 288), jnp.float32)
        return (x, cond_1152)
    x, cond_1152 = _rec_inputs()

    def _L0_cond_setup():
        import jax, jax.numpy as jnp
        import numpy as np
        NUM_HEADS = 16
        NUM_EXPERTS = 4
        TOP_K = 2
        LN_EPS = 1e-06

        def _ln(h):
            mu = jnp.mean(h, axis=-1, keepdims=True)
            var = jnp.var(h, axis=-1, keepdims=True)
            return (h - mu) * jax.lax.rsqrt(var + LN_EPS)

        def _modulate(h, shift, scale):
            return h * (1.0 + scale[:, None, :]) + shift[:, None, :]
        key = jax.random.key(seed)
        ks = jax.random.split(key, 12)
        B, N, C = (8, 256, 288)
        H = 4 * C
        E = NUM_EXPERTS
        s = 0.02
        return {'x': jax.random.normal(ks[0], (B, N, C), jnp.float32), 'c': jax.random.normal(ks[1], (B, C), jnp.float32), 'w_adaln': jax.random.normal(ks[2], (C, 6 * C), jnp.float32) * s, 'b_adaln': jnp.zeros((6 * C,), jnp.float32), 'w_qkv': jax.random.normal(ks[3], (C, 3 * C), jnp.float32) * s, 'b_qkv': jnp.zeros((3 * C,), jnp.float32), 'w_proj': jax.random.normal(ks[4], (C, C), jnp.float32) * s, 'b_proj': jnp.zeros((C,), jnp.float32), 'w_gate': jax.random.normal(ks[5], (C, E), jnp.float32) * s, 'w1': jax.random.normal(ks[6], (E, C, H), jnp.float32) * s, 'b1': jnp.zeros((E, H), jnp.float32), 'w2': jax.random.normal(ks[7], (E, H, C), jnp.float32) * s, 'b2': jnp.zeros((E, C), jnp.float32)}
    _L0_cond_all = _L0_cond_setup()
    _L0_cond_in = {k: v for k, v in _L0_cond_all.items() if k in ('w_adaln', 'b_adaln', 'w_qkv', 'b_qkv', 'w_proj', 'b_proj', 'w_gate', 'w1', 'b1', 'w2', 'b2')}
    del _L0_cond_all
    return {'x': x, 'cond_1152': cond_1152, 'L0_cond_w_adaln': _L0_cond_in['w_adaln'], 'L0_cond_b_adaln': _L0_cond_in['b_adaln'], 'L0_cond_w_qkv': _L0_cond_in['w_qkv'], 'L0_cond_b_qkv': _L0_cond_in['b_qkv'], 'L0_cond_w_proj': _L0_cond_in['w_proj'], 'L0_cond_b_proj': _L0_cond_in['b_proj'], 'L0_cond_w_gate': _L0_cond_in['w_gate'], 'L0_cond_w1': _L0_cond_in['w1'], 'L0_cond_b1': _L0_cond_in['b1'], 'L0_cond_w2': _L0_cond_in['w2'], 'L0_cond_b2': _L0_cond_in['b2']}

def reference(x, cond_1152, L0_cond_w_adaln, L0_cond_b_adaln, L0_cond_w_qkv, L0_cond_b_qkv, L0_cond_w_proj, L0_cond_b_proj, L0_cond_w_gate, L0_cond_w1, L0_cond_b1, L0_cond_w2, L0_cond_b2):
    import jax
    import jax.numpy as jnp

    def _L0_cond_ref(x, c, w_adaln, b_adaln, w_qkv, b_qkv, w_proj, b_proj, w_gate, w1, b1, w2, b2):
        import jax, jax.numpy as jnp
        import numpy as np
        NUM_HEADS = 16
        NUM_EXPERTS = 4
        TOP_K = 2
        LN_EPS = 1e-06

        def _ln(h):
            mu = jnp.mean(h, axis=-1, keepdims=True)
            var = jnp.var(h, axis=-1, keepdims=True)
            return (h - mu) * jax.lax.rsqrt(var + LN_EPS)

        def _modulate(h, shift, scale):
            return h * (1.0 + scale[:, None, :]) + shift[:, None, :]
        B, N, C = x.shape
        nh = NUM_HEADS
        hd = C // nh
        mod = jax.nn.silu(c) @ w_adaln + b_adaln
        sh_msa, sc_msa, g_msa, sh_mlp, sc_mlp, g_mlp = jnp.split(mod, 6, axis=-1)
        h = _modulate(_ln(x), sh_msa, sc_msa)
        qkv = (h @ w_qkv + b_qkv).reshape(B, N, 3, nh, hd).transpose(2, 0, 3, 1, 4)
        q, k, v = (qkv[0], qkv[1], qkv[2])
        attn = jax.nn.softmax(jnp.einsum('bhqd,bhkd->bhqk', q, k) * hd ** (-0.5), axis=-1)
        o = jnp.einsum('bhqk,bhkd->bhqd', attn, v).transpose(0, 2, 1, 3).reshape(B, N, C)
        o = o @ w_proj + b_proj
        x = x + g_msa[:, None, :] * o
        xn = _modulate(_ln(x), sh_mlp, sc_mlp)
        xf = xn.reshape(-1, C)
        gate_logits = xf @ w_gate
        topk_logits, topk_idx = jax.lax.top_k(gate_logits, TOP_K)
        gates = jax.nn.softmax(topk_logits, axis=-1)
        cw = jnp.sum(jax.nn.one_hot(topk_idx, NUM_EXPERTS, dtype=xf.dtype) * gates[..., None], axis=1)
        hmid = jax.nn.gelu(jnp.einsum('tc,ech->eth', xf, w1) + b1[:, None, :], approximate=True)
        eo = jnp.einsum('eth,ehc->etc', hmid, w2) + b2[:, None, :]
        moe = jnp.einsum('te,etc->tc', cw, eo).reshape(B, N, C)
        return x + g_mlp[:, None, :] * moe
    x = _L0_cond_ref(x, cond_1152, L0_cond_w_adaln, L0_cond_b_adaln, L0_cond_w_qkv, L0_cond_b_qkv, L0_cond_w_proj, L0_cond_b_proj, L0_cond_w_gate, L0_cond_w1, L0_cond_b1, L0_cond_w2, L0_cond_b2)
    return x

_drawn_inputs = setup_inputs


def setup_inputs(seed=0):
    import zlib

    import numpy as np

    out = dict(_drawn_inputs(seed))
    spreads = {'L0_cond_b_adaln': (0.0, 0.428),
     'L0_cond_b_qkv': (0.0, 0.8),
     'L0_cond_b_proj': (0.0, 0.339),
     'L0_cond_b1': (0.0, 0.8),
     'L0_cond_b2': (0.0, 0.525)}
    factors = {'L0_cond_w_qkv': 8.0,
     'L0_cond_w_proj': 5.351,
     'L0_cond_w_gate': 2.874,
     'L0_cond_w1': 2.695}
    for name, (base, spread) in spreads.items():
        noise = np.random.default_rng([zlib.crc32(name.encode()), seed]).standard_normal(out[name].shape)
        drawn = base * np.exp(spread * noise) if base else spread * noise
        out[name] = jnp.asarray(drawn.astype(out[name].dtype))
    for name, factor in factors.items():
        out[name] = (out[name] * factor).astype(out[name].dtype)
    return out
```

```python
from contextlib import ExitStack

import concourse.bass as bass
from concourse import mybir

ALU = mybir.AluOpType
ACT = mybir.ActivationFunctionType
AX = mybir.AxisListType
F32 = mybir.dt.float32
F32R = mybir.dt.float32r

P = 128
B, N, C = 2, 1024, 288
T = B * N
NT = T // P
NH, HD = 16, 18
HP = 32
HA = HD + 1
GH = 4
NG = NH // GH
GG = B * NG
GC = GH * HD
HALF = N // 2
KT = N // P
QT = HALF // P
MOD = 6 * C
NE, H = 4, 1152
HT = H // P
CH = 512
NCH = T // CH
TCH = CH // P
REM = C - 2 * P
LN_EPS = 1e-6
SCALE = HD ** -0.5
SH_MSA, SC_MSA = 0, C
G_MSA, SH_MLP, SC_MLP, G_MLP = 0, C, 2 * C, 3 * C

PRODUCTS = [(0, 0, 0, 0), (0, 1, 0, 1), (0, 2, 0, 2), (0, 0, 1, 0), (0, 1, 1, 1), (1, 0, 0, 0), (1, 1, 0, 1)]


def f32(ap):
    return ap.bitcast(F32)


def split_weights(eng, hi, lo, raw, done):
    n = done[1]
    eng.tensor_copy(hi, raw).then_inc(done[0], 1)
    eng.wait_ge(done[0], n + 1)
    eng.tensor_tensor(lo, raw[:, 0:2], f32(hi[:, 0:2]), ALU.subtract).then_inc(done[0], 1)
    for i, q in enumerate((1, 3)):
        s = slice(q * HP, q * HP + REM)
        eng.wait_ge(done[0], n + 2 + i)
        eng.tensor_tensor(hi[s, 2], raw[s, 2], f32(hi[s, 2]), ALU.subtract).then_inc(done[0], 1)
    eng.wait_ge(done[0], n + 4)


def load_rows(eng, dst, w, sem):
    eng.dma_start(dst[:, 0:2], w[0:2 * P].rearrange("(k p) n -> p k n", p=P)).then_inc(sem, 16)
    for q in range(4):
        eng.dma_start(dst[q * HP:q * HP + REM, 2], w[2 * P:C]).then_inc(sem, 16)


LOADS = 5


def build_kernel(nc, x, cond, w_adaln, b_adaln, w_qkv, b_qkv, w_proj, b_proj, w_gate, w1, b1, w2, b2, out):
    outer = ExitStack()

    def sb(stack, name, shape, dt=F32):
        return stack.enter_context(nc.sbuf_tensor(name, shape, dt))

    def pb(stack, name, shape, dt=F32):
        return stack.enter_context(nc.psum_tensor(name, shape, dt))

    def sem(stack, name):
        return stack.enter_context(nc.semaphore(name))

    o_dram = nc.dram_tensor("o_scratch", (GG, 2, P, QT * GC), F32, kind="Internal").ap()
    xt = x.rearrange("b (t p) c -> p (b t) c", p=P)
    ot = out.rearrange("b (t p) c -> p (b t) c", p=P)

    outer.enter_context(nc.allow_non_contiguous_dma(reason="biases and the condition are laid out by column"))
    with outer:
        x_hi = sb(outer, "x_hi", [P, 3, T], F32R)
        x_lo = sb(outer, "x_lo", [P, 2, T], F32R)
        mod_late = sb(outer, "mod_late", [P, B, 4 * C])
        ident = sb(outer, "ident", [P, P])
        half_neg = sb(outer, "half_neg", [P, NT])

        setup_and_attention = ExitStack()
        with setup_and_attention:
            v_aug = sb(setup_and_attention, "v_aug", [P, NT, NH, HA])
            setup(nc, sb, pb, sem, xt, cond, w_adaln, b_adaln, w_qkv, b_qkv, x_hi, x_lo, mod_late, ident, half_neg, v_aug)
            attention(nc, sb, pb, sem, w_qkv, b_qkv, x_hi, x_lo, ident, v_aug, o_dram)
        experts(nc, sb, pb, sem, xt, ot, o_dram, w_proj, b_proj, w_gate, w1, b1, w2, b2, x_hi, x_lo, mod_late, ident,
                half_neg)


def setup(nc, sb, pb, sem, xt, cond, w_adaln, b_adaln, w_qkv, b_qkv, x_hi, x_lo, mod_late, ident, half_neg, v_aug):
    ctx = ExitStack()
    KC, KN = 96, 3
    MN = MOD // 6
    with ctx:
        mod_early = sb(ctx, "mod_early", [P, B, 2 * C])
        x_in = sb(ctx, "x_in", [P, NT, C])
        cond_t = sb(ctx, "cond_t", [KC, KN, B])
        sig = sb(ctx, "sig", [KC, KN, B])
        silu = sb(ctx, "silu", [KC, KN, B])
        silu_b = sb(ctx, "silu_b", [KC, KN, B, P])
        wa = sb(ctx, "wa", [KC, KN, MOD])
        ba = sb(ctx, "ba", [P, MOD])
        bv = sb(ctx, "bv", [P, C])
        wv_raw = sb(ctx, "wv_raw", [P, 3, C])
        wv_hi = sb(ctx, "wv_hi", [P, 3, C], F32R)
        wv_lo = sb(ctx, "wv_lo", [P, 2, C], F32R)
        stats = sb(ctx, "stats", [P, NT, 6])
        mv = sb(ctx, "mv", [P, NT, 2])
        veps = sb(ctx, "veps", [P, NT])
        rstd = sb(ctx, "rstd", [P, NT])
        xn = sb(ctx, "xn", [P, 2, C])
        xm = sb(ctx, "xm", [P, 2, C])
        h = sb(ctx, "h", [P, 2, 3 * P])

        mod_ps = [pb(ctx, f"mod_ps{i}", [P, 512]) for i in range(4)]
        t_ps = [pb(ctx, f"t_ps{i}", [P, 3, P]) for i in range(2)]
        v_ps = [pb(ctx, f"v_ps{i}", [P, 512]) for i in range(2)]

        x_ld = [sem(ctx, f"x_ld{i}") for i in range(NT // 4)]
        cond_ld = sem(ctx, "cond_ld")
        wa_ld = sem(ctx, "wa_ld")
        ba_ld = sem(ctx, "ba_ld")
        bv_ld = sem(ctx, "bv_ld")
        wv_ld = sem(ctx, "wv_ld")
        const_ok = sem(ctx, "const_ok")
        wv_ok = sem(ctx, "wv_ok")
        exp_ok = sem(ctx, "exp_ok")
        silu_step = sem(ctx, "silu_step")
        silu_ok = sem(ctx, "silu_ok")
        mod_mm = sem(ctx, "mod_mm")
        mod_ok = sem(ctx, "mod_ok")
        stat_step = sem(ctx, "stat_step")
        veps_ok = sem(ctx, "veps_ok")
        rstd_ok = sem(ctx, "rstd_ok")
        xn_ok = sem(ctx, "xn_ok")
        xm_ok = sem(ctx, "xm_ok")
        h_ok = sem(ctx, "h_ok")
        rem_ok = sem(ctx, "rem_ok")
        t_ok = sem(ctx, "t_ok")
        hi_ok = sem(ctx, "hi_ok")
        lo_ok = sem(ctx, "lo_ok")
        v_mm = sem(ctx, "v_mm")
        v_ok = sem(ctx, "v_ok")

        block = ctx.enter_context(nc.Block())

        @block.sync
        def _(sp):
            for b in range(B):
                sp.dma_start(cond_t[:, :, b], cond[b].rearrange("(k p) -> p k", p=KC)).then_inc(cond_ld, 16)
            for k in range(KN):
                sp.dma_start(wa[:, k], w_adaln[k * KC:(k + 1) * KC]).then_inc(wa_ld, 16)
            for i in range(0, NT, 4):
                sp.dma_start(x_in[:, i:i + 4], xt[:, i:i + 4]).then_inc(x_ld[i // 4], 16)

        @block.gpsimd
        def _(pool):
            nc.gpsimd.memset(ident[:], 0.0).then_inc(const_ok, 1)
            nc.gpsimd.memset(half_neg[:], -0.5).then_inc(const_ok, 1)
            pool.wait_ge(const_ok, 2)
            nc.gpsimd.affine_select(out=ident[:], in_=ident[:], compare_op=ALU.not_equal, fill=1.0, base=0,
                                    pattern=[[-1, P]], channel_multiplier=1).then_inc(const_ok, 1)
            pool.wait_ge(wv_ld, 16 * LOADS)
            split_weights(pool, wv_hi[:], wv_lo[:], wv_raw[:], (wv_ok, 0))
            pool.wait_ge(veps_ok, 1)
            nc.gpsimd.tensor_tensor(rstd[:], veps[:], half_neg[:], ALU.pow).then_inc(rstd_ok, 1)
            for t in range(NT):
                pool.wait_ge(xm_ok, t + 1)
                if t >= 2:
                    pool.wait_ge(t_ok, t - 1)
                    pool.wait_ge(rem_ok, t - 1)
                b = t // KT
                nc.gpsimd.tensor_tensor(h[:, t % 2, 0:C], xm[:, t % 2], mod_early[:, b, SH_MSA:SH_MSA + C],
                                        ALU.add).then_inc(h_ok, 1)

        @block.scalar
        def _(act):
            load_rows(act, wv_raw, w_qkv[:, 2 * C:3 * C], wv_ld)
            act.dma_start(ba[:], b_adaln.rearrange("(a n) -> a n", a=1).broadcast_to([P, MOD])).then_inc(ba_ld, 16)
            act.dma_start(bv[:], b_qkv[2 * C:3 * C].rearrange("(a n) -> a n", a=1).broadcast_to([P, C]))\
               .then_inc(bv_ld, 16)
            act.wait_ge(cond_ld, 32)
            nc.scalar.activation(sig[:], cond_t[:], ACT.Exp, scale=-1.0).then_inc(exp_ok, 1)
            for t in range(NT):
                act.wait_ge(h_ok, t + 1)
                rem = h[:, t % 2, 2 * P:C].unsqueeze(1).broadcast_to([P, 3, REM])
                nc.scalar.copy(h[:, t % 2, C:3 * P].rearrange("p (q c) -> p q c", q=3), rem).then_inc(rem_ok, 1)
                act.wait_ge(t_ok, t + 1)
                nc.scalar.copy(x_hi[:, :, t * P:(t + 1) * P], t_ps[t % 2][:]).then_inc(hi_ok, 1)

        @block.vector
        def _(dve):
            nc.vector.memset(v_aug[:, :, :, HD:HA], 1.0)
            dve.wait_ge(exp_ok, 1)
            nc.vector.tensor_scalar(sig[:], sig[:], 1.0, None, ALU.add).then_inc(silu_step, 1)
            dve.wait_ge(silu_step, 1)
            nc.vector.reciprocal(sig[:], sig[:]).then_inc(silu_step, 1)
            dve.wait_ge(silu_step, 2)
            nc.vector.tensor_tensor(silu[:], cond_t[:], sig[:], ALU.mult).then_inc(silu_step, 1)
            dve.wait_ge(silu_step, 3)
            for k in range(KN):
                nc.vector.tensor_copy(silu_b[:, k], silu[:, k].unsqueeze(2).broadcast_to([KC, B, P]))\
                  .then_inc(silu_ok, 1)
            for t in range(NT):
                dve.wait_ge(x_ld[t // 4], 16)
                nc.vector.bn_stats(stats[:, t], x_in[:, t]).then_inc(stat_step, 1)
            for t in range(NT):
                dve.wait_ge(stat_step, t + 1)
                nc.vector.bn_aggr(mv[:, t], stats[:, t]).then_inc(stat_step, 1)
            dve.wait_ge(stat_step, 2 * NT)
            nc.vector.tensor_scalar(veps[:], mv[:, :, 1], LN_EPS, None, ALU.add).then_inc(veps_ok, 1)
            dve.wait_ge(ba_ld, 16)
            for i in range(6 * B):
                b, j = i // 6, i % 6
                dve.wait_ge(mod_mm, i + 1)
                dst = mod_early[:, b, j * MN:(j + 1) * MN] if j < 2 else mod_late[:, b, (j - 2) * MN:(j - 1) * MN]
                nc.vector.tensor_tensor(dst, mod_ps[i % 4][:, 0:MN], ba[:, j * MN:(j + 1) * MN], ALU.add)\
                  .then_inc(mod_ok, 1)
            dve.wait_ge(mod_ok, 6 * B)
            for m, s in ((mod_early, SC_MSA), (mod_late, SC_MLP)):
                nc.vector.tensor_scalar(m[:, :, s:s + C], m[:, :, s:s + C], 1.0, None, ALU.add).then_inc(mod_ok, 1)
            dve.wait_ge(mod_ok, 6 * B + 2)
            dve.wait_ge(rstd_ok, 1)
            dve.wait_ge(bv_ld, 16)

            def normalise(t):
                nc.vector.tensor_scalar(xn[:, t % 2], x_in[:, t], mv[:, t, 0:1], rstd[:, t:t + 1],
                                        ALU.subtract, ALU.mult).then_inc(xn_ok, 1)
                dve.wait_ge(xn_ok, t + 1)
                if t >= 2:
                    dve.wait_ge(h_ok, t - 1)
                nc.vector.tensor_tensor(xm[:, t % 2], xn[:, t % 2], mod_early[:, t // KT, SC_MSA:SC_MSA + C],
                                        ALU.mult).then_inc(xm_ok, 1)

            def low_parts(t):
                s = slice(t * P, (t + 1) * P)
                dve.wait_ge(hi_ok, t + 1)
                nc.vector.tensor_tensor(x_lo[:, :, s], t_ps[t % 2][:, 0:2], f32(x_hi[:, 0:2, s]), ALU.subtract)
                nc.vector.tensor_tensor(x_hi[2 * HP:P, 2, s], t_ps[t % 2][2 * HP:P, 2], f32(x_hi[2 * HP:P, 2, s]),
                                        ALU.subtract).then_inc(lo_ok, 1)

            def values(t):
                dve.wait_ge(v_mm, t + 1)
                nc.vector.tensor_tensor(v_aug[:, t, :, 0:HD], v_ps[t % 2][:, 0:C].rearrange("p (h d) -> p h d", d=HD),
                                        bv[:].rearrange("p (h d) -> p h d", d=HD), ALU.add).then_inc(v_ok, 1)

            for t in range(NT + 2):
                if t < NT:
                    normalise(t)
                if 1 <= t <= NT:
                    low_parts(t - 1)
                if t >= 2:
                    values(t - 2)

        @block.tensor
        def _(pe):
            pe.wait_ge(silu_ok, KN)
            pe.wait_ge(wa_ld, 16 * KN)
            for i in range(6 * B):
                b, j = i // 6, i % 6
                if i >= 4:
                    pe.wait_ge(mod_ok, i - 3)
                for k in range(KN):
                    mm = nc.tensor.matmul(mod_ps[i % 4][:, 0:MN], silu_b[:, k, b], wa[:, k, j * MN:(j + 1) * MN],
                                          start=(k == 0), stop=(k == KN - 1))
                mm.then_inc(mod_mm, 1)
            pe.wait_ge(const_ok, 3)
            pe.wait_ge(wv_ok, 4)

            def transposes(t):
                pe.wait_ge(rem_ok, t + 1)
                if t >= 2:
                    pe.wait_ge(lo_ok, t - 1)
                for k in range(3):
                    mm = nc.tensor.transpose(t_ps[t % 2][:, k], h[:, t % 2, k * P:(k + 1) * P], ident[:])
                mm.then_inc(t_ok, 1)

            def values(t):
                pe.wait_ge(lo_ok, t + 1)
                if t >= 2:
                    pe.wait_ge(v_ok, t - 1)
                for i, (xs, xk, ws, wk) in enumerate(PRODUCTS):
                    mm = nc.tensor.matmul(v_ps[t % 2][:, 0:C], (x_hi, x_lo)[xs][:, xk, t * P:(t + 1) * P],
                                          (wv_hi, wv_lo)[ws][:, wk], start=(i == 0), stop=(i == 6))
                mm.then_inc(v_mm, 1)

            for t in range(NT + 1):
                if t < NT:
                    transposes(t)
                if t >= 1:
                    values(t - 1)


STEPS = 2 * KT
MAX_TILES = {s: range(3 * (s - 4), min(3 * (s - 4) + 3, 24)) for s in range(4, 12)}
MAX_TILES |= {s: range(24 + 2 * (s - 12), 24 + 2 * (s - 12) + 2) for s in range(12, 16)}
PROJ_UNIT = {6: 0, 8: 1, 10: 2, 13: 3}
ROWS_LAST = 2
ROWS_NEXT = 11
OUT_FIRST = 9


def attention(nc, sb, pb, sem, w_qkv, b_qkv, x_hi, x_lo, ident, v_aug, o_dram):
    ctx = ExitStack()
    with ctx:
        wqk_raw = sb(ctx, "wqk_raw", [P, 3, 2, GC])
        wqk_hi = sb(ctx, "wqk_hi", [P, 3, 2, GH, HP], F32R)
        wqk_lo = sb(ctx, "wqk_lo", [P, 2, 2, GH, HP], F32R)
        bqk = sb(ctx, "bqk", [P, GG, 2])
        proj_f = sb(ctx, "proj_f", [P, 2, HALF])
        parts = sb(ctx, "parts", [P, 4, 2, HALF], F32R)
        Q_LO, Q_HI, K_HI, K_LO = range(4)
        rows_dram = nc.dram_tensor("rows_scratch", (GG, 2, 2, GH * QT, P), F32, kind="Internal").ap()
        stack = [sb(ctx, f"stack{i}", [3 * HP, GH, 2, 2, HALF], F32R) for i in range(2)]
        negmax = sb(ctx, "negmax", [P, 2, 2, GH * QT])
        rows_hi = sb(ctx, "rows_hi", [GH * QT, 2, P], F32R)
        rows_lo = sb(ctx, "rows_lo", [GH * QT, 2, P], F32R)
        probs = sb(ctx, "probs", [P, 2, GH, HALF])
        o_sb = sb(ctx, "o_sb", [P, 2, HALF])
        rsum = sb(ctx, "rsum", [P, 2, QT * GH])
        o_norm = sb(ctx, "o_norm", [P, 2, QT * GH, HD])

        s_ps = [pb(ctx, f"s_ps{i}", [P, HALF]) for i in range(2)]
        m_ps = [pb(ctx, f"m_ps{i}", [P, N]) for i in range(2)]
        o_ps = pb(ctx, "o_ps", [P, HALF])
        misc = pb(ctx, "misc", [P, HALF])

        zero_ok = sem(ctx, "zero_ok")
        bias_zero = sem(ctx, "bias_zero")
        bias_ld = sem(ctx, "bias_ld")
        w_ld = sem(ctx, "w_ld")
        w_split = sem(ctx, "w_split")
        proj_mm = sem(ctx, "proj_mm")
        proj_f_ok = sem(ctx, "proj_f_ok")
        parts_ok = sem(ctx, "parts_ok")
        stack_ld = sem(ctx, "stack_ld")
        max_mm = sem(ctx, "max_mm")
        max_free = sem(ctx, "max_free")
        rows_mm = sem(ctx, "rows_mm")
        rows_step = sem(ctx, "rows_step")
        rows_ld = [sem(ctx, f"rows_ld{i}") for i in range(2)]
        rows_st = [sem(ctx, f"rows_st{i}") for i in range(2)]
        score_mm = sem(ctx, "score_mm")
        exp_free = sem(ctx, "exp_free")
        pv_free = sem(ctx, "pv_free")
        o_evac = sem(ctx, "o_evac")
        out_mm = sem(ctx, "out_mm")
        rsum_ok = sem(ctx, "rsum_ok")
        out_ok = sem(ctx, "out_ok")
        out_st = [sem(ctx, f"out_st{i}") for i in range(2)]

        block = ctx.enter_context(nc.Block())

        def groups(body):
            for g in range(GG):
                body(g, g % 2, g + 1 < GG, g + 2 < GG)

        def max_tile(m):
            return m // 16, (m // QT) % GH, m % QT

        @block.sync
        def _(sp):
            def load_w(g):
                if g >= 1:
                    sp.wait_ge(w_split, 4 * g)
                c = (g % NG) * GC
                for k in range(2):
                    sp.dma_start(wqk_raw[:, k], w_qkv[k * P:(k + 1) * P, 0:2 * C]
                                 .rearrange("p (a n) -> p a n", a=2)[:, :, c:c + GC]).then_inc(w_ld, 16)
                for q in range(4):
                    sp.dma_start(wqk_raw[q * HP:q * HP + REM, 2], w_qkv[2 * P:C, 0:2 * C]
                                 .rearrange("p (a n) -> p a n", a=2)[:, :, c:c + GC]).then_inc(w_ld, 16)

            def load_stack(g, s):
                sp.wait_ge(parts_ok, 8 * (g + 1))
                if g >= 2:
                    sp.wait_ge(score_mm, 64 * (g - 1))
                for h in range(GH):
                    for q, kinds in enumerate((slice(Q_HI, K_HI + 1), slice(Q_HI, K_LO + 1, 2), slice(Q_LO, K_HI + 1, 2))):
                        sp.dma_start(f32(stack[s][q * HP:q * HP + HA, h]).rearrange("p a b n -> p a (b n)"),
                                     f32(parts[h * HP:h * HP + HA, kinds]).rearrange("p a b n -> p a (b n)"))\
                          .then_inc(stack_ld, 16)

            def load_rows_of_max(g, s, half):
                n = 2 * g + half
                sp.wait_ge(rows_step, 2 * (n + 1))
                for part, rows in enumerate((rows_hi, rows_lo)):
                    sp.dma_start(rows_dram[g, half, part], f32(rows[:, half])).then_inc(rows_st[half], 16)
                sp.wait_ge(rows_st[half], 32 * (g + 1))
                for part, q in enumerate((0, 2)):
                    sp.dma_start(f32(stack[s][q * HP + HD:q * HP + HA, :, 0, half]),
                                 rows_dram[g, half, part].rearrange("(a h t) n -> a h (t n)", a=1, h=GH))\
                      .then_inc(rows_ld[half], 16)

            def store(g, half):
                n = 2 * g + half
                sp.wait_ge(out_ok, n + 1)
                sp.dma_start(o_dram[g, half], o_norm[:, half].rearrange("p t d -> p (t d)")).then_inc(out_st[half], 16)

            sp.wait_ge(bias_zero, 1)
            for h in range(GH):
                for a in range(2):
                    for b in range(B):
                        sp.dma_start(bqk[h * HP:h * HP + HD, b * NG:(b + 1) * NG, a],
                                     b_qkv[a * C:(a + 1) * C].rearrange("(g h d) -> h d g", h=GH, d=HD)[h])\
                          .then_inc(bias_ld, 16)
            load_w(0)
            load_w(1)
            sp.wait_ge(zero_ok, 4)
            load_stack(0, 0)
            load_w(2)
            load_rows_of_max(0, 0, 0)

            def group(g, s, has_next, has_after):
                if has_next:
                    load_stack(g + 1, 1 - s)
                load_rows_of_max(g, s, 1)
                store(g, 0)
                if has_after and g + 3 < GG:
                    load_w(g + 3)
                if has_next:
                    load_rows_of_max(g + 1, 1 - s, 0)
                store(g, 1)

            groups(group)
            for half in range(2):
                sp.wait_ge(out_st[half], 16 * GG)

        @block.gpsimd
        def _(pool):
            nc.gpsimd.memset(bqk[:, :, 0], 0.0)
            nc.gpsimd.memset(bqk[:, :, 1], 1.0).then_inc(bias_zero, 1)
            nc.gpsimd.memset(f32(wqk_hi[:]), 0.0).then_inc(bias_zero, 1)
            nc.gpsimd.memset(f32(wqk_lo[:]), 0.0).then_inc(bias_zero, 1)
            pool.wait_ge(bias_zero, 3)

            def split_w(g):
                pool.wait_ge(w_ld, 16 * 6 * (g + 1))
                if g >= 1:
                    pool.wait_ge(proj_mm, 4 * g)
                hi = wqk_hi[:, :, :, :, 0:HD].rearrange("p k a h d -> p (k a) h d")
                lo = wqk_lo[:, :, :, :, 0:HD].rearrange("p k a h d -> p (k a) h d")
                raw = wqk_raw[:].rearrange("p k a (h d) -> p (k a) h d", d=HD)
                nc.gpsimd.tensor_copy(hi, raw).then_inc(w_split, 1)
                pool.wait_ge(w_split, 4 * g + 1)
                nc.gpsimd.tensor_tensor(lo, raw[:, 0:4], f32(hi[:, 0:4]), ALU.subtract).then_inc(w_split, 1)
                for i, q in enumerate((1, 3)):
                    r = slice(q * HP, q * HP + REM)
                    pool.wait_ge(w_split, 4 * g + 2 + i)
                    nc.gpsimd.tensor_tensor(hi[r, 4:6], raw[r, 4:6], f32(hi[r, 4:6]), ALU.subtract).then_inc(w_split, 1)
                pool.wait_ge(w_split, 4 * g + 4)

            def split_unit(g, u):
                n = 4 * g + u
                half, a = u // 2, u % 2
                hi, lo = parts[:, (Q_HI, K_HI)[a], half], parts[:, (Q_LO, K_LO)[a], half]
                pool.wait_ge(proj_f_ok, n + 1)
                if u == 0:
                    pool.wait_ge(stack_ld, 16 * 12 * g)
                nc.gpsimd.tensor_copy(hi, proj_f[:, u % 2]).then_inc(parts_ok, 1)
                pool.wait_ge(parts_ok, 2 * n + 1)
                nc.gpsimd.tensor_tensor(lo, proj_f[:, u % 2], f32(hi), ALU.subtract).then_inc(parts_ok, 1)

            split_w(0)
            for g in range(2):
                for u in range(4):
                    split_unit(g, u)
                split_w(g + 1)

            def group(g, s, has_next, has_after):
                if has_after:
                    for u in range(4):
                        split_unit(g + 2, u)
                    if g + 3 < GG:
                        split_w(g + 3)

            groups(group)

        @block.scalar
        def _(act):
            act.sem_inc(exp_free, 2)
            act.wait_ge(bias_ld, 16 * 16)

            def project(g, u):
                n = 4 * g + u
                a = u % 2
                act.wait_ge(proj_mm, n + 1)
                if n >= 2:
                    act.wait_ge(parts_ok, 2 * (n - 1))
                nc.scalar.activation(proj_f[:, u % 2], misc[:], ACT.Identity, bias=bqk[:, g, a:a + 1])\
                  .then_inc(proj_f_ok, 1)

            def out_of_bank(g, half):
                n = 2 * g + half
                act.wait_ge(pv_free, 2 + 16 * g + KT * (half + 1))
                if n >= 2:
                    act.wait_ge(out_mm, n - 1)
                nc.scalar.copy(o_sb[:, half], o_ps[:]).then_inc(o_evac, 1)

            for g in range(2):
                for u in range(4):
                    project(g, u)

            def group(g, s, has_next, has_after):
                for st in range(STEPS):
                    for h in range(GH):
                        n = 64 * g + 4 * st + h
                        act.wait_ge(score_mm, n + 1)
                        if h == 0:
                            act.wait_ge(pv_free, 16 * g + st + 1)
                        nc.scalar.activation(probs[:, st % 2, h], s_ps[h % 2][:],
                                             ACT.Exp, scale=SCALE).then_inc(exp_free, 1)
                    if st == KT:
                        out_of_bank(g, 0)
                    if has_after and st in PROJ_UNIT:
                        project(g + 2, PROJ_UNIT[st])
                out_of_bank(g, 1)

            groups(group)

        @block.vector
        def _(dve):
            for i in range(2):
                nc.vector.memset(f32(stack[i][:, 0:2].rearrange("p h a b n -> p (h a b n)")), 0.0).then_inc(zero_ok, 1)
                nc.vector.memset(f32(stack[i][:, 2:4].rearrange("p h a b n -> p (h a b n)")), 0.0).then_inc(zero_ok, 1)
            nc.vector.memset(o_ps[:], 0.0).then_inc(zero_ok, 1)
            dve.sem_inc(max_free, 2)

            def maximum(g, m):
                half = m // 16
                n = 32 * g + m
                dve.wait_ge(max_mm, n + 1)
                nc.vector.tensor_reduce(negmax[:, half, g % 2, m % 16:m % 16 + 1],
                                        m_ps[m % 2][:], AX.X, ALU.max, negate=True).then_inc(max_free, 1)

            def rows(g, half):
                n = 2 * g + half
                dve.wait_ge(rows_mm, n + 1)
                if g >= 1:
                    dve.wait_ge(rows_ld[half], 32 * g)
                nc.vector.tensor_copy(rows_hi[:, half], misc[0:GH * QT, 0:P]).then_inc(rows_step, 1)
                dve.wait_ge(rows_step, 2 * n + 1)
                nc.vector.tensor_tensor(rows_lo[:, half], misc[0:GH * QT, 0:P], f32(rows_hi[:, half]),
                                        ALU.subtract).then_inc(rows_step, 1)

            def normalise(g, half):
                n = 2 * g + half
                o = misc[:].rearrange("p (t c) -> p t c", c=HP)
                dve.wait_ge(out_mm, n + 1)
                nc.vector.reciprocal(rsum[:, half], o[:, :, HD]).then_inc(rsum_ok, 1)
                dve.wait_ge(rsum_ok, n + 1)
                if g >= 1:
                    dve.wait_ge(out_st[half], 16 * g)
                nc.vector.tensor_tensor(o_norm[:, half], o[:, :, 0:HD],
                                        rsum[:, half].unsqueeze(2).broadcast_to([P, QT * GH, HD]),
                                        ALU.mult).then_inc(out_ok, 1)

            for m in range(32):
                maximum(0, m)
            rows(0, 0)

            def group(g, s, has_next, has_after):
                for st in range(STEPS):
                    if has_next:
                        for m in MAX_TILES.get(st, ()):
                            maximum(g + 1, m)
                    if st == ROWS_LAST:
                        rows(g, 1)
                    if st == OUT_FIRST:
                        normalise(g, 0)
                    if st == ROWS_NEXT and has_next:
                        rows(g + 1, 0)
                normalise(g, 1)

            groups(group)

        @block.tensor
        def _(pe):
            pe.sem_inc(pv_free, 2)

            last_use = [None]

            def take_misc(next_use):
                if last_use[0] is not None:
                    s, v = last_use[0]
                    pe.wait_ge(s, v)
                last_use[0] = next_use

            def project(g, u):
                half, a = u // 2, u % 2
                take_misc((proj_f_ok, 4 * g + u + 1))
                if u == 0:
                    pe.wait_ge(w_split, 4 * (g + 1))
                tok = (g // NG) * N + half * HALF
                for i, (xs, xk, ws, wk) in enumerate(PRODUCTS):
                    w = (wqk_hi, wqk_lo)[ws][:, wk, a].rearrange("p h d -> p (h d)")
                    mm = nc.tensor.matmul(misc[:], w, (x_hi, x_lo)[xs][:, xk, tok:tok + HALF],
                                          start=(i == 0), stop=(i == 6))
                mm.then_inc(proj_mm, 1)

            def maximum(g, s, m):
                half, h, qt = max_tile(m)
                n = 32 * g + m
                if m == 0:
                    pe.wait_ge(stack_ld, 16 * 12 * (g + 1))
                pe.wait_ge(max_free, n + 1)
                for kh in range(2):
                    mm = nc.tensor.matmul(m_ps[m % 2][:, kh * HALF:(kh + 1) * HALF],
                                          stack[s][:, h, 0, half, qt * P:(qt + 1) * P], stack[s][:, h, 1, kh],
                                          start=True, stop=True)
                mm.then_inc(max_mm, 1)

            def rows(g, half):
                n = 2 * g + half
                take_misc((rows_step, 2 * (n + 1)))
                pe.wait_ge(max_free, 2 + 32 * g + 16 * (half + 1))
                nc.tensor.transpose(misc[0:GH * QT, 0:P], negmax[:, half, g % 2], ident[:]).then_inc(rows_mm, 1)

            def outputs(g, half):
                n = 2 * g + half
                take_misc((out_ok, n + 1))
                pe.wait_ge(o_evac, n + 1)
                for t in range(QT):
                    mm = nc.tensor.transpose(misc[:, t * P:(t + 1) * P], o_sb[:, half, t * P:(t + 1) * P], ident[:])
                mm.then_inc(out_mm, 1)

            def scores(g, s, st):
                half, kt = st // KT, st % KT
                if kt == 0:
                    pe.wait_ge(rows_ld[half], 32 * (g + 1))
                for h in range(GH):
                    n = 64 * g + 4 * st + h
                    pe.wait_ge(exp_free, n + 1)
                    nc.tensor.matmul(s_ps[h % 2][:], stack[s][:, h, 1, kt // QT, (kt % QT) * P:(kt % QT + 1) * P],
                                     stack[s][:, h, 0, half], start=True, stop=True).then_inc(score_mm, 1)

            def values(g, st):
                half, kt = st // KT, st % KT
                pe.wait_ge(exp_free, 2 + 64 * g + 4 * (st + 1))
                if kt == 0:
                    n = 2 * g + half
                    if isinstance(n, int) and n == 0:
                        pe.wait_ge(zero_ok, 5)
                    else:
                        pe.wait_ge(o_evac, n)
                tile = (g // NG) * KT + kt
                for h in range(GH):
                    mm = nc.tensor.matmul(o_ps[h * HP:h * HP + HA], v_aug[:, tile, (g % NG) * GH + h],
                                          probs[:, st % 2, h], start=(kt == 0), stop=(kt == KT - 1))
                mm.then_inc(pv_free, 1)

            for g in range(2):
                for u in range(4):
                    project(g, u)
            for m in range(32):
                maximum(0, 0, m)
            rows(0, 0)

            def group(g, s, has_next, has_after):
                for st in range(STEPS):
                    scores(g, s, st)
                    if has_next:
                        for m in MAX_TILES.get(st, ()):
                            maximum(g + 1, 1 - s, m)
                    if st >= 1:
                        values(g, st - 1)
                    if st == ROWS_LAST:
                        rows(g, 1)
                    if st == OUT_FIRST:
                        outputs(g, 0)
                    if st == ROWS_NEXT and has_next:
                        rows(g + 1, 0)
                    if has_after and st in PROJ_UNIT:
                        project(g + 2, PROJ_UNIT[st])
                values(g, STEPS - 1)
                outputs(g, 1)

            groups(group)


def experts(nc, sb, pb, sem, xt, ot, o_dram, w_proj, b_proj, w_gate, w1, b1, w2, b2, x_hi, x_lo, mod_late, ident,
            half_neg):
    ctx = ExitStack()
    PIECE = 3 * P
    PIECES = 6
    x1_dram = nc.dram_tensor("x1_scratch", (P, NT, C), F32, kind="Internal").ap()
    with ctx:
        w1_hi = [sb(ctx, "w1_hi0", [P, 3, H], F32R)]
        w1_lo = [sb(ctx, "w1_lo0", [P, 2, H], F32R)]
        w2_hi = [sb(ctx, "w2_hi0", [P, HT, C], F32R)]
        w2_lo = [sb(ctx, "w2_lo0", [P, HT, C], F32R)]
        w_raw = sb(ctx, "w_raw", [P, 2, 3, PIECE])
        b1c = sb(ctx, "b1c", [P, NE, HT])
        b2b = sb(ctx, "b2b", [P, NE, C])
        cw = sb(ctx, "cw", [P, NT, NE])
        piece_ld = [sem(ctx, f"piece_ld{i}") for i in range(2)]
        piece_step = sem(ctx, "piece_step")
        piece_ok = sem(ctx, "piece_ok")
        b1_ld = sem(ctx, "b1_ld")
        b2_ld = sem(ctx, "b2_ld")

        def load_piece(eng, e, i):
            n = PIECES * e + i
            buf = w_raw[:, i % 2]
            if n >= 2:
                eng.wait_ge(piece_ok, n - 1)
            if i < 3:
                c = slice(i * PIECE, (i + 1) * PIECE)
                eng.dma_start(buf[:, 0:2], w1[e, 0:2 * P, c].rearrange("(k p) n -> p k n", p=P))\
                   .then_inc(piece_ld[i % 2], 16)
                for q in range(4):
                    eng.dma_start(buf[q * HP:q * HP + REM, 2], w1[e, 2 * P:C, c]).then_inc(piece_ld[i % 2], 16)
            else:
                r = slice((i - 3) * PIECE, (i - 2) * PIECE)
                eng.dma_start(buf[:, :, 0:C], w2[e, r].rearrange("(k p) n -> p k n", p=P))\
                   .then_inc(piece_ld[i % 2], 16)

        def split_piece(pool, e, i):
            loads = (LOADS, LOADS + LOADS, 2 * LOADS + 1) if i % 2 == 0 else (LOADS, LOADS + 1, LOADS + 2)
            steps = 12 * e + (3 * i if i < 3 else 6 + i)
            pool.wait_ge(piece_ld[i % 2], 16 * (loads[2] * e + loads[i // 2]))
            raw = w_raw[:, i % 2]
            if i < 3:
                hi, lo = w1_hi[e % 2][:, :, i * PIECE:(i + 1) * PIECE], w1_lo[e % 2][:, :, i * PIECE:(i + 1) * PIECE]
                nc.gpsimd.tensor_copy(hi, raw).then_inc(piece_step, 1)
                pool.wait_ge(piece_step, steps + 1)
                nc.gpsimd.tensor_tensor(lo, raw[:, 0:2], f32(hi[:, 0:2]), ALU.subtract).then_inc(piece_step, 1)
                pool.wait_ge(piece_step, steps + 2)
                nc.gpsimd.tensor_tensor(hi[HP:2 * HP, 2], raw[HP:2 * HP, 2], f32(hi[HP:2 * HP, 2]), ALU.subtract)\
                  .then_inc(piece_step, 1)
                pool.wait_ge(piece_step, steps + 3)
                nc.gpsimd.tensor_tensor(hi[3 * HP:P, 2], raw[3 * HP:P, 2], f32(hi[3 * HP:P, 2]), ALU.subtract)\
                  .then_inc(piece_ok, 1)
                pool.wait_ge(piece_ok, PIECES * e + i + 1)
            else:
                hi, lo = (w[e % 2][:, 3 * (i - 3):3 * (i - 2)] for w in (w2_hi, w2_lo))
                nc.gpsimd.tensor_copy(hi, raw[:, :, 0:C]).then_inc(piece_step, 1)
                pool.wait_ge(piece_step, steps + 1)
                nc.gpsimd.tensor_tensor(lo, raw[:, :, 0:C], f32(hi), ALU.subtract).then_inc(piece_ok, 1)

        between(nc, sb, pb, sem, xt, o_dram, w_proj, b_proj, w_gate, b1, b2, x_hi, x_lo, mod_late, ident, half_neg,
                x1_dram, b1c, b2b, cw, b1_ld, b2_ld, load_piece, split_piece, PIECES)
        w1_hi.append(sb(ctx, "w1_hi1", [P, 3, H], F32R))
        w1_lo.append(sb(ctx, "w1_lo1", [P, 2, H], F32R))
        w2_hi.append(sb(ctx, "w2_hi1", [P, HT, C], F32R))
        w2_lo.append(sb(ctx, "w2_lo1", [P, HT, C], F32R))
        mixture(nc, sb, pb, sem, ot, x_hi, x_lo, mod_late, x1_dram, w1_hi, w1_lo, w2_hi, w2_lo, b1c, b2b, cw,
                b1_ld, b2_ld, piece_ok, load_piece, split_piece, PIECES)


def between(nc, sb, pb, sem, xt, o_dram, w_proj, b_proj, w_gate, b1, b2, x_hi, x_lo, mod_late, ident, half_neg,
            x1_dram, b1c, b2b, cw, b1_ld, b2_ld, load_piece, split_piece, PIECES):
    ctx = ExitStack()
    with ctx:
        wp_raw = sb(ctx, "wp_raw", [P, 3, C])
        wp_hi = sb(ctx, "wp_hi", [P, 3, C], F32R)
        wp_lo = sb(ctx, "wp_lo", [P, 2, C], F32R)
        wg_raw = sb(ctx, "wg_raw", [P, 3, NE])
        wg_hi = sb(ctx, "wg_hi", [P, 3, NE], F32R)
        wg_lo = sb(ctx, "wg_lo", [P, 2, NE], F32R)
        bp = sb(ctx, "bp", [P, C])
        o_in = sb(ctx, "o_in", [P, 4, 3 * P])
        x_in = sb(ctx, "xr", [P, 4, C])
        ot_hi = sb(ctx, "ot_hi", [P, 2, 3, P], F32R)
        ot_lo = sb(ctx, "ot_lo", [P, 2, 2, P], F32R)
        y = sb(ctx, "y", [P, 2, C])
        gy = sb(ctx, "gy", [P, 2, C])
        x1 = sb(ctx, "x1", [P, 4, C])
        stats = sb(ctx, "stats2", [P, 2, 6])
        mv = sb(ctx, "mv2", [P, 4, 2])
        veps = sb(ctx, "veps2", [P, NT])
        rstd = sb(ctx, "rstd2", [P, NT])
        xn = sb(ctx, "xn2", [P, 2, C])
        xm = sb(ctx, "xm2", [P, 2, C])
        h = sb(ctx, "h2", [P, 2, 3 * P])
        logits = sb(ctx, "logits", [P, NT, NE])
        rank = sb(ctx, "rank", [P, NT, NE])
        ge = sb(ctx, "ge", [P, 6, NT])
        top = sb(ctx, "top", [P, NT])
        shifted = sb(ctx, "shifted", [P, NT, NE])
        weight = sb(ctx, "weight", [P, NT, NE])
        wsum = sb(ctx, "wsum", [P, NT])

        to_ps = [pb(ctx, f"to_ps{i}", [P, 3, P]) for i in range(2)]
        y_ps = [pb(ctx, f"y_ps{i}", [P, 512]) for i in range(2)]
        tx_ps = [pb(ctx, f"tx_ps{i}", [P, 3, P]) for i in range(2)]
        gate_ps = pb(ctx, "gate_ps", [P, NT, NE])

        wp_ld = sem(ctx, "wp_ld")
        wg_ld = sem(ctx, "wg_ld")
        bp_ld = sem(ctx, "bp_ld")
        wp_ok = sem(ctx, "wp_ok")
        wg_ok = sem(ctx, "wg_ok")
        o_ld = [sem(ctx, f"o_ld{i}") for i in range(4)]
        xr_ld = [sem(ctx, f"xr_ld{i}") for i in range(4)]
        x1_st = [sem(ctx, f"x1_st{i}") for i in range(4)]
        orem_ok = sem(ctx, "orem_ok")
        to_mm = sem(ctx, "to_mm")
        ohi_ok = sem(ctx, "ohi_ok")
        olo_ok = sem(ctx, "olo_ok")
        y_mm = sem(ctx, "y_mm")
        y_ok = sem(ctx, "y_ok")
        gy_ok = sem(ctx, "gy_ok")
        x1_ok = sem(ctx, "x1_ok")
        stat_step = sem(ctx, "stat_step2")
        veps_ok = sem(ctx, "veps_ok2")
        rstd_ok = sem(ctx, "rstd_ok2")
        xn_ok = sem(ctx, "xn_ok2")
        xm_ok = sem(ctx, "xm_ok2")
        h_ok = sem(ctx, "h_ok2")
        rem_ok = sem(ctx, "rem_ok2")
        tx_mm = sem(ctx, "tx_mm")
        hi_ok = sem(ctx, "hi_ok2")
        lo_ok = sem(ctx, "lo_ok2")
        gate_mm = sem(ctx, "gate_mm")
        gate_step = sem(ctx, "gate_step")
        gexp_ok = sem(ctx, "gexp_ok")

        def rounds(*stages):
            for r in range(NT + max(d for d, _ in stages)):
                for d, stage in stages:
                    if 0 <= r - d < NT:
                        stage(r - d)

        block = ctx.enter_context(nc.Block())

        @block.sync
        def _(sp):
            def load(t):
                b, half, qt = t // KT, (t % KT) // QT, t % QT
                if t >= 4:
                    sp.wait_ge(to_mm, t - 3)
                    sp.wait_ge(x1_ok, t - 3)
                sp.dma_start(o_in[:, t % 4, 0:C].rearrange("p (g c) -> p g c", g=NG),
                             o_dram[b * NG:(b + 1) * NG, half, :, qt * GC:(qt + 1) * GC]
                             .rearrange("g p c -> p g c")).then_inc(o_ld[t % 4], 16)
                sp.dma_start(x_in[:, t % 4], xt[:, t]).then_inc(xr_ld[t % 4], 16)

            def store(t):
                sp.wait_ge(x1_ok, t + 1)
                sp.dma_start(x1_dram[:, t], x1[:, t % 4]).then_inc(x1_st[t % 4], 16)

            load_rows(sp, wp_raw, w_proj, wp_ld)
            rounds((0, load), (4, store))
            for i in range(4):
                sp.wait_ge(x1_st[i], 16 * (NT // 4))

        @block.gpsimd
        def _(pool):
            pool.wait_ge(wp_ld, 16 * LOADS)
            split_weights(pool, wp_hi[:], wp_lo[:], wp_raw[:], (wp_ok, 0))
            pool.wait_ge(wg_ld, 16 * LOADS)
            split_weights(pool, wg_hi[:], wg_lo[:], wg_raw[:], (wg_ok, 0))

            def add_x(t):
                pool.wait_ge(xr_ld[t % 4], 16 * (t // 4 + 1))
                pool.wait_ge(gy_ok, t + 1)
                if t >= 4:
                    pool.wait_ge(x1_st[t % 4], 16 * (t // 4))
                    pool.wait_ge(xn_ok, t - 3)
                nc.gpsimd.tensor_tensor(x1[:, t % 4], x_in[:, t % 4], gy[:, t % 2], ALU.add).then_inc(x1_ok, 1)

            def root(t):
                pool.wait_ge(veps_ok, t + 1)
                nc.gpsimd.tensor_tensor(rstd[:, t:t + 1], veps[:, t:t + 1], half_neg[:, t:t + 1], ALU.pow)\
                  .then_inc(rstd_ok, 1)

            def shift(t):
                pool.wait_ge(xm_ok, t + 1)
                if t >= 2:
                    pool.wait_ge(tx_mm, t - 1)
                nc.gpsimd.tensor_tensor(h[:, t % 2, 0:C], xm[:, t % 2], mod_late[:, t // KT, SH_MLP:SH_MLP + C],
                                        ALU.add).then_inc(h_ok, 1)

            rounds((1, add_x), (2, root), (3, shift))
            for i in range(PIECES):
                split_piece(pool, 0, i)

        @block.scalar
        def _(act):
            load_rows(act, wg_raw, w_gate, wg_ld)
            act.dma_start(bp[:], b_proj.rearrange("(a n) -> a n", a=1).broadcast_to([P, C])).then_inc(bp_ld, 16)

            def remainder(src, t, buf):
                rem = src[:, buf, 2 * P:C].unsqueeze(1).broadcast_to([P, 3, REM])
                return nc.scalar.copy(src[:, buf, C:3 * P].rearrange("p (q c) -> p q c", q=3), rem)

            def attn_remainder(t):
                act.wait_ge(o_ld[t % 4], 16 * (t // 4 + 1))
                if t >= 4:
                    act.wait_ge(to_mm, t - 3)
                remainder(o_in, t, t % 4).then_inc(orem_ok, 1)

            def attn_high(t):
                act.wait_ge(to_mm, t + 1)
                if t >= 2:
                    act.wait_ge(y_mm, t - 1)
                nc.scalar.copy(ot_hi[:, t % 2], to_ps[t % 2][:]).then_inc(ohi_ok, 1)

            def x_remainder(t):
                act.wait_ge(h_ok, t + 1)
                remainder(h, t, t % 2).then_inc(rem_ok, 1)

            def x_high(t):
                act.wait_ge(tx_mm, t + 1)
                nc.scalar.copy(x_hi[:, :, t * P:(t + 1) * P], tx_ps[t % 2][:]).then_inc(hi_ok, 1)

            rounds((0, attn_remainder), (0, attn_high), (3, x_remainder), (4, x_high))
            for i in range(3):
                load_piece(act, 0, i)
            act.dma_start(b1c[:], b1.rearrange("e (t p) -> p e t", p=P)).then_inc(b1_ld, 16)
            act.dma_start(b2b[:], b2.rearrange("(a e) n -> a e n", a=1).broadcast_to([P, NE, C])).then_inc(b2_ld, 16)
            for i in range(3, PIECES):
                load_piece(act, 0, i)
            act.wait_ge(gate_step, 1 + 18 + 2)
            nc.scalar.activation(weight[:], shifted[:], ACT.Exp).then_inc(gexp_ok, 1)

        @block.vector
        def _(dve):
            def attn_low(t):
                dve.wait_ge(ohi_ok, t + 1)
                nc.vector.tensor_tensor(ot_lo[:, t % 2], to_ps[t % 2][:, 0:2], f32(ot_hi[:, t % 2, 0:2]), ALU.subtract)
                nc.vector.tensor_tensor(ot_hi[2 * HP:P, t % 2, 2], to_ps[t % 2][2 * HP:P, 2],
                                        f32(ot_hi[2 * HP:P, t % 2, 2]), ALU.subtract).then_inc(olo_ok, 1)

            def bias_and_gate(t):
                dve.wait_ge(y_mm, t + 1)
                if t == 0:
                    dve.wait_ge(bp_ld, 16)
                nc.vector.tensor_tensor(y[:, t % 2], y_ps[t % 2][:, 0:C], bp[:], ALU.add).then_inc(y_ok, 1)
                dve.wait_ge(y_ok, t + 1)
                if t >= 2:
                    dve.wait_ge(x1_ok, t - 1)
                nc.vector.tensor_tensor(gy[:, t % 2], y[:, t % 2], mod_late[:, t // KT, G_MSA:G_MSA + C],
                                        ALU.mult).then_inc(gy_ok, 1)

            def moments(t):
                dve.wait_ge(x1_ok, t + 1)
                nc.vector.bn_stats(stats[:, t % 2], x1[:, t % 4]).then_inc(stat_step, 1)
                dve.wait_ge(stat_step, 2 * t + 1)
                nc.vector.bn_aggr(mv[:, t % 4], stats[:, t % 2]).then_inc(stat_step, 1)
                dve.wait_ge(stat_step, 2 * t + 2)
                nc.vector.tensor_scalar(veps[:, t:t + 1], mv[:, t % 4, 1:2], LN_EPS, None, ALU.add)\
                  .then_inc(veps_ok, 1)

            def normalise(t):
                dve.wait_ge(rstd_ok, t + 1)
                nc.vector.tensor_scalar(xn[:, t % 2], x1[:, t % 4], mv[:, t % 4, 0:1], rstd[:, t:t + 1],
                                        ALU.subtract, ALU.mult).then_inc(xn_ok, 1)
                dve.wait_ge(xn_ok, t + 1)
                if t >= 2:
                    dve.wait_ge(h_ok, t - 1)
                nc.vector.tensor_tensor(xm[:, t % 2], xn[:, t % 2], mod_late[:, t // KT, SC_MLP:SC_MLP + C],
                                        ALU.mult).then_inc(xm_ok, 1)

            def x_low(t):
                s = slice(t * P, (t + 1) * P)
                dve.wait_ge(hi_ok, t + 1)
                nc.vector.tensor_tensor(x_lo[:, :, s], tx_ps[t % 2][:, 0:2], f32(x_hi[:, 0:2, s]), ALU.subtract)
                nc.vector.tensor_tensor(x_hi[2 * HP:P, 2, s], tx_ps[t % 2][2 * HP:P, 2], f32(x_hi[2 * HP:P, 2, s]),
                                        ALU.subtract).then_inc(lo_ok, 1)

            rounds((0, attn_low), (1, bias_and_gate), (2, moments), (3, normalise), (4, x_low))

            step = 0

            def then(instruction):
                nonlocal step
                step += 1
                instruction.then_inc(gate_step, 1)
                dve.wait_ge(gate_step, step)

            dve.wait_ge(gate_mm, NT)
            then(nc.vector.tensor_copy(logits[:], gate_ps[:]))
            for e in range(NE):
                nc.vector.memset(rank[:, :, e], float(NE - 1 - e))
            pairs = [(i, j) for i in range(NE) for j in range(i + 1, NE)]
            for n, (i, j) in enumerate(pairs):
                then(nc.vector.tensor_tensor(ge[:, n], logits[:, :, i], logits[:, :, j], ALU.is_ge))
                then(nc.vector.tensor_tensor(rank[:, :, j], rank[:, :, j], ge[:, n], ALU.add))
                then(nc.vector.tensor_tensor(rank[:, :, i], rank[:, :, i], ge[:, n], ALU.subtract))
            then(nc.vector.tensor_reduce(top[:], logits[:], AX.X, ALU.max))
            then(nc.vector.tensor_tensor(shifted[:], logits[:], top[:].unsqueeze(2).broadcast_to([P, NT, NE]),
                                         ALU.subtract))
            dve.wait_ge(gexp_ok, 1)
            then(nc.vector.scalar_tensor_tensor(out=weight[:], in0=rank[:], scalar=2.0, in1=weight[:],
                                                op0=ALU.is_lt, op1=ALU.mult))
            then(nc.vector.tensor_reduce(wsum[:], weight[:], AX.X, ALU.add))
            then(nc.vector.reciprocal(wsum[:], wsum[:]))
            then(nc.vector.tensor_tensor(cw[:], weight[:], wsum[:].unsqueeze(2).broadcast_to([P, NT, NE]), ALU.mult))

        @block.tensor
        def _(pe):
            def attn_transposes(t):
                pe.wait_ge(orem_ok, t + 1)
                if t >= 2:
                    pe.wait_ge(olo_ok, t - 1)
                for k in range(3):
                    mm = nc.tensor.transpose(to_ps[t % 2][:, k], o_in[:, t % 4, k * P:(k + 1) * P], ident[:])
                mm.then_inc(to_mm, 1)

            def project(t):
                pe.wait_ge(olo_ok, t + 1)
                if t == 0:
                    pe.wait_ge(wp_ok, 4)
                if t >= 2:
                    pe.wait_ge(y_ok, t - 1)
                for i, (xs, xk, ws, wk) in enumerate(PRODUCTS):
                    mm = nc.tensor.matmul(y_ps[t % 2][:, 0:C], (ot_hi, ot_lo)[xs][:, t % 2, xk], (wp_hi, wp_lo)[ws][:, wk],
                                          start=(i == 0), stop=(i == 6))
                mm.then_inc(y_mm, 1)

            def x_transposes(t):
                pe.wait_ge(rem_ok, t + 1)
                if t >= 2:
                    pe.wait_ge(lo_ok, t - 1)
                for k in range(3):
                    mm = nc.tensor.transpose(tx_ps[t % 2][:, k], h[:, t % 2, k * P:(k + 1) * P], ident[:])
                mm.then_inc(tx_mm, 1)

            def gate(t):
                pe.wait_ge(lo_ok, t + 1)
                if t == 0:
                    pe.wait_ge(wg_ok, 4)
                for i, (xs, xk, ws, wk) in enumerate(PRODUCTS):
                    mm = nc.tensor.matmul(gate_ps[:, t], (x_hi, x_lo)[xs][:, xk, t * P:(t + 1) * P],
                                          (wg_hi, wg_lo)[ws][:, wk], start=(i == 0), stop=(i == 6))
                mm.then_inc(gate_mm, 1)

            rounds((0, attn_transposes), (1, project), (4, x_transposes), (5, gate))


def mixture(nc, sb, pb, sem, ot, x_hi, x_lo, mod_late, x1_dram, w1_hi, w1_lo, w2_hi, w2_lo, b1c, b2b, cw,
            b1_ld, b2_ld, piece_ok, load_piece, split_piece, PIECES):
    ctx = ExitStack()
    RING = 3
    LAG = 2
    assert HT % RING == 0
    with ctx:
        hid = sb(ctx, "hid", [P, RING, CH])
        hid_hi = sb(ctx, "hid_hi", [P, RING, CH], F32R)
        hid_lo = sb(ctx, "hid_lo", [P, RING, CH], F32R)
        acc = sb(ctx, "acc", [P, NT, C])
        part = sb(ctx, "part", [P, TCH, C])
        x1 = sb(ctx, "x1_in", [P, 2, C])
        gated = sb(ctx, "gated", [P, 2, C])
        res = sb(ctx, "res", [P, 2, C])
        h_ps = [pb(ctx, f"h_ps{i}", [P, CH]) for i in range(RING)]
        y_ps = [pb(ctx, f"e_ps{i}", [P, 512]) for i in range(TCH)]

        up_mm = sem(ctx, "up_mm")
        gelu_ok = sem(ctx, "gelu_ok")
        hi_ok = sem(ctx, "hid_hi_ok")
        split_ok = sem(ctx, "split_ok")
        down_mm = sem(ctx, "down_mm")
        part_ok = sem(ctx, "part_ok")
        bias_ok = sem(ctx, "bias_ok")
        add_ok = sem(ctx, "add_ok")
        x1_ld = [sem(ctx, f"x1_ld{i}") for i in range(2)]
        gated_ok = sem(ctx, "gated_ok")
        res_ok = sem(ctx, "res_ok")
        out_st = [sem(ctx, f"y_st{i}") for i in range(2)]

        def chunks(eng, e, body):
            if e < NE - 1:
                with eng.Fori(0, NCH) as c:
                    body(c, c + NCH * e)
            else:
                for c in range(NCH):
                    body(c, c + NCH * e)

        block = ctx.enter_context(nc.Block())

        @block.sync
        def _(sp):
            for e in range(1, NE):
                for i in range(PIECES):
                    load_piece(sp, e, i)
            for t in range(NT):
                if t >= 2:
                    sp.wait_ge(res_ok, t - 1)
                sp.dma_start(x1[:, t % 2], x1_dram[:, t]).then_inc(x1_ld[t % 2], 16)
                if t >= 1:
                    sp.wait_ge(res_ok, t)
                    sp.dma_start(ot[:, t - 1], res[:, (t - 1) % 2]).then_inc(out_st[(t - 1) % 2], 16)
            sp.wait_ge(res_ok, NT)
            sp.dma_start(ot[:, NT - 1], res[:, (NT - 1) % 2]).then_inc(out_st[(NT - 1) % 2], 16)
            for i in range(2):
                sp.wait_ge(out_st[i], 16 * NT // 2)

        @block.gpsimd
        def _(pool):
            pool.sem_inc(add_ok, TCH)
            for e in range(NE):
                for c in range(NCH):
                    if e + 1 < NE and c < 3:
                        if c == 0 and e >= 1:
                            pool.wait_ge(down_mm, RING + HT * NCH * e)
                        for i in (2 * c, 2 * c + 1):
                            split_piece(pool, e + 1, i)
                    for t in range(TCH):
                        tile = TCH * c + t
                        n = NT * e + tile
                        pool.wait_ge(bias_ok, n + 1)
                        pool.wait_ge(part_ok, TCH + n + 1)
                        nc.gpsimd.tensor_tensor(acc[:, tile], acc[:, tile], part[:, t], ALU.add).then_inc(add_ok, 1)

        @block.scalar
        def _(act):
            act.sem_inc(gelu_ok, RING)
            act.sem_inc(part_ok, TCH)
            act.wait_ge(b1_ld, 16)

            for e in range(NE):
                def chunk(c, n, e=e):
                    for ht in range(HT):
                        k = n * HT + ht
                        act.wait_ge(up_mm, k + 1)
                        act.wait_ge(split_ok, k + 1)
                        nc.scalar.activation(hid[:, ht % RING], h_ps[ht % RING][:], ACT.Gelu_apprx_tanh,
                                             bias=b1c[:, e, ht:ht + 1]).then_inc(gelu_ok, 1)
                    act.wait_ge(down_mm, RING + (n + 1) * HT)
                    for t in range(TCH):
                        act.wait_ge(add_ok, n * TCH + t + 1)
                        nc.scalar.activation(part[:, t], y_ps[t][:, 0:C], ACT.Copy,
                                             scale=cw[:, c * TCH + t, e:e + 1]).then_inc(part_ok, 1)

                chunks(act, e, chunk)

        @block.vector
        def _(dve):
            dve.sem_inc(split_ok, RING)
            dve.wait_ge(b2_ld, 16)

            def finish(tile):
                n = NT * (NE - 1) + tile
                dve.wait_ge(add_ok, TCH + n + 1)
                nc.vector.tensor_tensor(gated[:, tile % 2], acc[:, tile], mod_late[:, tile // KT, G_MLP:G_MLP + C],
                                        ALU.mult).then_inc(gated_ok, 1)
                dve.wait_ge(gated_ok, tile + 1)
                dve.wait_ge(x1_ld[tile % 2], 16 * (tile // 2 + 1))
                if tile >= 2:
                    dve.wait_ge(out_st[tile % 2], 16 * (tile // 2))
                nc.vector.tensor_tensor(res[:, tile % 2], gated[:, tile % 2], x1[:, tile % 2], ALU.add)\
                  .then_inc(res_ok, 1)

            for e in range(NE):
                def chunk(c, n, e=e):
                    for ht in range(HT):
                        k = n * HT + ht
                        dve.wait_ge(gelu_ok, RING + k + 1)
                        dve.wait_ge(down_mm, k + 1)
                        nc.vector.tensor_copy(hid_hi[:, ht % RING], hid[:, ht % RING]).then_inc(hi_ok, 1)
                        dve.wait_ge(hi_ok, k + 1)
                        nc.vector.tensor_tensor(hid_lo[:, ht % RING], hid[:, ht % RING], f32(hid_hi[:, ht % RING]),
                                                ALU.subtract).then_inc(split_ok, 1)
                        if 3 <= ht < 3 + TCH:
                            t = ht - 3
                            acc_t, cw_t = acc[:, c * TCH + t], cw[:, c * TCH + t, e:e + 1]
                            if e == 0:
                                nc.vector.tensor_scalar(acc_t, b2b[:, e], cw_t, None, ALU.mult).then_inc(bias_ok, 1)
                            else:
                                dve.wait_ge(add_ok, TCH + n * TCH + t + 1 - NT)
                                nc.vector.scalar_tensor_tensor(out=acc_t, in0=b2b[:, e], scalar=cw_t, in1=acc_t,
                                                               op0=ALU.mult, op1=ALU.add).then_inc(bias_ok, 1)
                        if e == NE - 1 and c >= 1 and ht in (2, 4, 6, 8):
                            finish(TCH * (c - 1) + ht // 2 - 1)

                chunks(dve, e, chunk)
            for t in range(NT - TCH, NT):
                finish(t)

        @block.tensor
        def _(pe):
            pe.sem_inc(down_mm, RING)
            for e in range(NE):
                pe.wait_ge(piece_ok, PIECES * (e + 1))

                def chunk(c, n, e=e):
                    w1s, w2s = (w1_hi[e % 2], w1_lo[e % 2]), (w2_hi[e % 2], w2_lo[e % 2])

                    def up(ht):
                        k = n * HT + ht
                        pe.wait_ge(gelu_ok, k + 1)
                        for i, (xs, xk, ws, wk) in enumerate(PRODUCTS):
                            mm = nc.tensor.matmul(h_ps[ht % RING][:], w1s[ws][:, wk, ht * P:(ht + 1) * P],
                                                  (x_hi, x_lo)[xs][:, xk, bass.ds(c * CH, CH)],
                                                  start=(i == 0), stop=(i == 6))
                        mm.then_inc(up_mm, 1)

                    def down(ht):
                        k = n * HT + ht
                        pe.wait_ge(split_ok, RING + k + 1)
                        for t in range(TCH):
                            if ht == 0:
                                pe.wait_ge(part_ok, n * TCH + t + 1)
                            s = slice(t * P, (t + 1) * P)
                            for i, (hs, ws) in enumerate(((hid_hi, 0), (hid_hi, 1), (hid_lo, 0))):
                                mm = nc.tensor.matmul(y_ps[t][:, 0:C], hs[:, ht % RING, s], w2s[ws][:, ht],
                                                      start=(ht == 0 and i == 0), stop=(ht == HT - 1 and i == 2))
                        mm.then_inc(down_mm, 1)

                    for ht in range(HT):
                        up(ht)
                        if ht >= LAG:
                            down(ht - LAG)
                    for ht in range(HT - LAG, HT):
                        down(ht)

                chunks(pe, e, chunk)


_INS = ["x", "cond_1152", "L0_cond_w_adaln", "L0_cond_b_adaln", "L0_cond_w_qkv", "L0_cond_b_qkv", "L0_cond_w_proj",
        "L0_cond_b_proj", "L0_cond_w_gate", "L0_cond_w1", "L0_cond_b1", "L0_cond_w2", "L0_cond_b2"]


def kernel(**inputs):
    import numpy as np
    import concourse.bacc as bacc
    from concourse.bass_utils import run_bass_kernel_spmd

    nc = bacc.Bacc("TRN2", target_bir_lowering=False, num_devices=1)
    arrays, args = {}, []
    for name in _INS:
        a = np.ascontiguousarray(inputs[name])
        arrays[f"in_{name}"] = a
        args.append(nc.dram_tensor(f"in_{name}", a.shape, mybir.dt.from_np(a.dtype), kind="ExternalInput").ap())
    out = nc.dram_tensor("out", (B, N, C), F32, kind="ExternalOutput").ap()
    build_kernel(nc, *args, out)
    r = run_bass_kernel_spmd(nc, [arrays], core_ids=[0])
    return r.results[0]["out"]
```

```python
from contextlib import ExitStack

import concourse.bass as bass
from concourse import mybir

ALU = mybir.AluOpType
ACT = mybir.ActivationFunctionType
AX = mybir.AxisListType
F32 = mybir.dt.float32
F32R = mybir.dt.float32r

P = 128
B, N, C = 2, 1024, 288
T = B * N
NT = T // P
NH, HD = 16, 18
HP = 32
HA = HD + 1
GH = 4
NG = NH // GH
GG = B * NG
GC = GH * HD
HALF = N // 2
KT = N // P
QT = HALF // P
MOD = 6 * C
NE, H = 4, 1152
HT = H // P
CH = 512
NCH = T // CH
TCH = CH // P
REM = C - 2 * P
LN_EPS = 1e-6
SCALE = HD ** -0.5
SH_MSA, SC_MSA = 0, C
G_MSA, SH_MLP, SC_MLP, G_MLP = 0, C, 2 * C, 3 * C

PRODUCTS = [(0, 0, 0, 0), (0, 1, 0, 1), (0, 2, 0, 2), (0, 0, 1, 0), (0, 1, 1, 1), (1, 0, 0, 0), (1, 1, 0, 1)]


def f32(ap):
    return ap.bitcast(F32)


def split_weights(eng, hi, lo, raw, done):
    n = done[1]
    eng.tensor_copy(hi, raw).then_inc(done[0], 1)
    eng.wait_ge(done[0], n + 1)
    eng.tensor_tensor(lo, raw[:, 0:2], f32(hi[:, 0:2]), ALU.subtract).then_inc(done[0], 1)
    for i, q in enumerate((1, 3)):
        s = slice(q * HP, q * HP + REM)
        eng.wait_ge(done[0], n + 2 + i)
        eng.tensor_tensor(hi[s, 2], raw[s, 2], f32(hi[s, 2]), ALU.subtract).then_inc(done[0], 1)
    eng.wait_ge(done[0], n + 4)


def load_rows(eng, dst, w, sem):
    eng.dma_start(dst[:, 0:2], w[0:2 * P].rearrange("(k p) n -> p k n", p=P)).then_inc(sem, 16)
    for q in range(4):
        eng.dma_start(dst[q * HP:q * HP + REM, 2], w[2 * P:C]).then_inc(sem, 16)


LOADS = 5


def rounds(*stages, extra=None):
    for r in range(NT + max(d for d, _ in stages)):
        for d, stage in stages:
            if 0 <= r - d < NT:
                stage(r - d)
        if extra:
            extra(r)


def build_kernel(nc, x, cond, w_adaln, b_adaln, w_qkv, b_qkv, w_proj, b_proj, w_gate, w1, b1, w2, b2, out):
    outer = ExitStack()

    def sb(stack, name, shape, dt=F32):
        return stack.enter_context(nc.sbuf_tensor(name, shape, dt))

    def pb(stack, name, shape, dt=F32):
        return stack.enter_context(nc.psum_tensor(name, shape, dt))

    def sem(stack, name):
        return stack.enter_context(nc.semaphore(name))

    o_dram = nc.dram_tensor("o_scratch", (GG, 2, P, QT * GC), F32, kind="Internal").ap()
    xt = x.rearrange("b (t p) c -> p (b t) c", p=P)
    ot = out.rearrange("b (t p) c -> p (b t) c", p=P)

    outer.enter_context(nc.allow_non_contiguous_dma(reason="biases and the condition are laid out by column"))
    with outer:
        x_hi = sb(outer, "x_hi", [P, 3, T], F32R)
        x_lo = sb(outer, "x_lo", [P, 2, T], F32R)
        mod_late = sb(outer, "mod_late", [P, B, 4 * C])
        ident = sb(outer, "ident", [P, P])
        half_neg = sb(outer, "half_neg", [P, NT])

        setup_and_attention = ExitStack()
        with setup_and_attention:
            v_aug = sb(setup_and_attention, "v_aug", [P, NT, NH, HA])
            wqk = (sb(setup_and_attention, "wqk_raw", [P, 3, 2, GC]),
                   sb(setup_and_attention, "wqk_hi", [P, 3, 2, GH, HP], F32R),
                   sb(setup_and_attention, "wqk_lo", [P, 2, 2, GH, HP], F32R),
                   sb(setup_and_attention, "bqk", [P, GG, 2]),
                   sem(setup_and_attention, "w_ld"), sem(setup_and_attention, "w_split"),
                   sem(setup_and_attention, "bias_ld"))
            setup(nc, sb, pb, sem, xt, cond, w_adaln, b_adaln, w_qkv, b_qkv, x_hi, x_lo, mod_late, ident, half_neg, v_aug,
                  wqk)
            attention(nc, sb, pb, sem, w_qkv, x_hi, x_lo, ident, v_aug, wqk, o_dram)
        experts(nc, sb, pb, sem, xt, ot, o_dram, w_proj, b_proj, w_gate, w1, b1, w2, b2, x_hi, x_lo, mod_late, ident,
                half_neg)


def load_group_weights(sp, w_qkv, wqk_raw, w_ld, g):
    c = (g % NG) * GC
    for k in range(2):
        sp.dma_start(wqk_raw[:, k], w_qkv[k * P:(k + 1) * P, 0:2 * C]
                     .rearrange("p (a n) -> p a n", a=2)[:, :, c:c + GC]).then_inc(w_ld, 16)
    for q in range(4):
        sp.dma_start(wqk_raw[q * HP:q * HP + REM, 2], w_qkv[2 * P:C, 0:2 * C]
                     .rearrange("p (a n) -> p a n", a=2)[:, :, c:c + GC]).then_inc(w_ld, 16)


def split_group_weights(eng, wqk, g):
    wqk_raw, wqk_hi, wqk_lo, _, w_ld, w_split, _ = wqk
    eng.wait_ge(w_ld, 16 * 6 * (g + 1))
    hi = wqk_hi[:, :, :, :, 0:HD].rearrange("p k a h d -> p (k a) h d")
    lo = wqk_lo[:, :, :, :, 0:HD].rearrange("p k a h d -> p (k a) h d")
    raw = wqk_raw[:].rearrange("p k a (h d) -> p (k a) h d", d=HD)
    eng.tensor_copy(hi, raw).then_inc(w_split, 1)
    eng.wait_ge(w_split, 4 * g + 1)
    eng.tensor_tensor(lo, raw[:, 0:4], f32(hi[:, 0:4]), ALU.subtract).then_inc(w_split, 1)
    for i, q in enumerate((1, 3)):
        r = slice(q * HP, q * HP + REM)
        eng.wait_ge(w_split, 4 * g + 2 + i)
        eng.tensor_tensor(hi[r, 4:6], raw[r, 4:6], f32(hi[r, 4:6]), ALU.subtract).then_inc(w_split, 1)
    eng.wait_ge(w_split, 4 * g + 4)


def setup(nc, sb, pb, sem, xt, cond, w_adaln, b_adaln, w_qkv, b_qkv, x_hi, x_lo, mod_late, ident, half_neg, v_aug,
          wqk):
    ctx = ExitStack()
    KC, KN = 96, 3
    wqk_raw, wqk_hi, wqk_lo, bqk, w_ld, _, bias_ld = wqk
    with ctx:
        mod_early = sb(ctx, "mod_early", [P, B, 2 * C])
        x_in = sb(ctx, "x_in", [P, NT, C])
        cond_t = sb(ctx, "cond_t", [KC, KN, B])
        sig = sb(ctx, "sig", [KC, KN, B])
        silu = sb(ctx, "silu", [KC, KN, B])
        silu_b = sb(ctx, "silu_b", [KC + 1, KN, B, P])
        wa = sb(ctx, "wa", [KC + 1, KN, MOD])
        bv = sb(ctx, "bv", [P, C])
        wv_raw = sb(ctx, "wv_raw", [P, 3, C])
        wv_hi = sb(ctx, "wv_hi", [P, 3, C], F32R)
        wv_lo = sb(ctx, "wv_lo", [P, 2, C], F32R)
        stats = sb(ctx, "stats", [P, NT, 6])
        mv = sb(ctx, "mv", [P, NT, 2])
        veps = sb(ctx, "veps", [P, NT])
        rstd = sb(ctx, "rstd", [P, NT])
        shift = sb(ctx, "shift", [P, NT])
        xn = sb(ctx, "xn", [P, 2, C])
        xm = sb(ctx, "xm", [P, 2, C])
        h = sb(ctx, "h", [P, 4, 3 * P])

        mod_ps = [pb(ctx, f"mod_ps{i}", [P, 512]) for i in range(3)]
        t_ps = [pb(ctx, f"t_ps{i}", [P, 3, P]) for i in range(3)]
        v_ps = [pb(ctx, f"v_ps{i}", [P, 512]) for i in range(2)]

        x_ld = [sem(ctx, f"x_ld{i}") for i in range(NT // 4)]
        bias_zero = sem(ctx, "bias_zero")
        cond_ld = sem(ctx, "cond_ld")
        wa_ld = [sem(ctx, f"wa_ld{i}") for i in range(2)]
        bv_ld = sem(ctx, "bv_ld")
        wv_ld = sem(ctx, "wv_ld")
        const_ok = sem(ctx, "const_ok")
        wv_ok = sem(ctx, "wv_ok")
        exp_ok = sem(ctx, "exp_ok")
        silu_step = sem(ctx, "silu_step")
        silu_ok = sem(ctx, "silu_ok")
        mod_mm = sem(ctx, "mod_mm")
        mod_ok = sem(ctx, "mod_ok")
        scale_ok = sem(ctx, "scale_ok")
        stat_ok = sem(ctx, "stat_ok")
        mv_ok = sem(ctx, "mv_ok")
        veps_ok = sem(ctx, "veps_ok")
        rstd_ok = sem(ctx, "rstd_ok")
        shift_ok = sem(ctx, "shift_ok")
        xn_ok = sem(ctx, "xn_ok")
        xm_ok = sem(ctx, "xm_ok")
        h_ok = sem(ctx, "h_ok")
        rem_ok = sem(ctx, "rem_ok")
        t_ok = sem(ctx, "t_ok")
        hi_ok = sem(ctx, "hi_ok")
        lo_ok = sem(ctx, "lo_ok")
        v_mm = sem(ctx, "v_mm")
        v_ok = sem(ctx, "v_ok")

        MOD_BLOCKS = [(b, j) for b in range(B) for j in (1, 0)] + [(b, j) for b in range(B) for j in range(2, 6)]
        EARLY = 2 * C

        block = ctx.enter_context(nc.Block())

        @block.sync
        def _(sp):
            for b in range(B):
                sp.dma_start(cond_t[:, :, b], cond[b].rearrange("(k p) -> p k", p=KC)).then_inc(cond_ld, 16)
            for part, cols in enumerate((slice(0, EARLY), slice(EARLY, MOD))):
                sp.dma_start(wa[0:KC, :, cols], w_adaln[:, cols].rearrange("(k p) n -> p k n", p=KC))\
                  .then_inc(wa_ld[part], 16)
                sp.dma_start(wa[KC:KC + 1, KN - 1, cols], b_adaln[cols].rearrange("(a n) -> a n", a=1))\
                  .then_inc(wa_ld[part], 16)
                if part == 0:
                    for i in range(0, NT, 4):
                        sp.dma_start(x_in[:, i:i + 4], xt[:, i:i + 4]).then_inc(x_ld[i // 4], 16)
            load_group_weights(sp, w_qkv, wqk_raw, w_ld, 0)
            sp.wait_ge(bias_zero, 2)
            for h in range(GH):
                for a in range(2):
                    for b in range(B):
                        sp.dma_start(bqk[h * HP:h * HP + HD, b * NG:(b + 1) * NG, a],
                                     b_qkv[a * C:(a + 1) * C].rearrange("(g h d) -> h d g", h=GH, d=HD)[h])\
                          .then_inc(bias_ld, 16)

        @block.gpsimd
        def _(pool):
            nc.gpsimd.memset(ident[:], 0.0).then_inc(const_ok, 1)
            nc.gpsimd.memset(half_neg[:], -0.5).then_inc(const_ok, 1)
            pool.wait_ge(const_ok, 2)
            nc.gpsimd.affine_select(out=ident[:], in_=ident[:], compare_op=ALU.not_equal, fill=1.0, base=0,
                                    pattern=[[-1, P]], channel_multiplier=1).then_inc(const_ok, 1)
            pool.wait_ge(wv_ld, 16 * LOADS)
            split_weights(pool, wv_hi[:], wv_lo[:], wv_raw[:], (wv_ok, 0))
            nc.gpsimd.memset(bqk[:, :, 0], 0.0).then_inc(bias_zero, 1)
            nc.gpsimd.memset(bqk[:, :, 1], 1.0).then_inc(bias_zero, 1)
            nc.gpsimd.memset(f32(wqk_hi[:]), 0.0).then_inc(bias_zero, 1)
            nc.gpsimd.memset(f32(wqk_lo[:]), 0.0).then_inc(bias_zero, 1)
            for b in range(B):
                s = slice(b * KT, (b + 1) * KT)
                pool.wait_ge(veps_ok, b + 1)
                nc.gpsimd.tensor_tensor(rstd[:, s], veps[:, s], half_neg[:, s], ALU.pow).then_inc(rstd_ok, 1)

            def add_shift(t):
                pool.wait_ge(xm_ok, t + 1)
                if t >= 4:
                    pool.wait_ge(t_ok, t - 3)
                nc.gpsimd.tensor_tensor(h[:, t % 4, 0:C], xm[:, t % 2], mod_early[:, t // KT, SH_MSA:SH_MSA + C],
                                        ALU.add).then_inc(h_ok, 1)

            rounds((2, add_shift))
            pool.wait_ge(bias_zero, 4)
            split_group_weights(pool, wqk, 0)

        @block.scalar
        def _(act):
            load_rows(act, wv_raw, w_qkv[:, 2 * C:3 * C], wv_ld)
            act.dma_start(bv[:], b_qkv[2 * C:3 * C].rearrange("(a n) -> a n", a=1).broadcast_to([P, C]))\
               .then_inc(bv_ld, 16)
            act.wait_ge(cond_ld, 32)
            nc.scalar.activation(sig[:], cond_t[:], ACT.Exp, scale=-1.0).then_inc(exp_ok, 1)

            def normalise(t):
                act.wait_ge(shift_ok, 2 * (t // KT) + 2)
                if t >= 2:
                    act.wait_ge(xm_ok, t - 1)
                nc.scalar.activation(xn[:, t % 2], x_in[:, t], ACT.Identity, scale=rstd[:, t:t + 1],
                                     bias=shift[:, t:t + 1]).then_inc(xn_ok, 1)

            def remainder(t):
                act.wait_ge(h_ok, t + 1)
                rem = h[:, t % 4, 2 * P:C].unsqueeze(1).broadcast_to([P, 3, REM])
                nc.scalar.copy(h[:, t % 4, C:3 * P].rearrange("p (q c) -> p q c", q=3), rem).then_inc(rem_ok, 1)

            def high_part(t):
                act.wait_ge(t_ok, t + 1)
                nc.scalar.copy(x_hi[:, :, t * P:(t + 1) * P], t_ps[t % 3][:]).then_inc(hi_ok, 1)

            rounds((5, high_part), (3, remainder), (0, normalise))

        @block.vector
        def _(dve):
            nc.vector.memset(silu_b[KC:KC + 1, KN - 1], 1.0).then_inc(silu_ok, 1)
            nc.vector.memset(v_aug[:, :, :, HD:HA], 1.0)
            dve.wait_ge(exp_ok, 1)
            nc.vector.tensor_scalar(sig[:], sig[:], 1.0, None, ALU.add).then_inc(silu_step, 1)
            dve.wait_ge(silu_step, 1)
            nc.vector.reciprocal(sig[:], sig[:]).then_inc(silu_step, 1)
            dve.wait_ge(silu_step, 2)
            nc.vector.tensor_tensor(silu[:], cond_t[:], sig[:], ALU.mult).then_inc(silu_step, 1)
            dve.wait_ge(silu_step, 3)
            for k in range(KN):
                nc.vector.tensor_copy(silu_b[0:KC, k], silu[:, k].unsqueeze(2).broadcast_to([KC, B, P]))\
                  .then_inc(silu_ok, 1)

            def moments(b):
                for t in range(b * KT, (b + 1) * KT):
                    dve.wait_ge(x_ld[t // 4], 16)
                    nc.vector.bn_stats(stats[:, t], x_in[:, t]).then_inc(stat_ok, 1)
                for t in range(b * KT, (b + 1) * KT):
                    dve.wait_ge(stat_ok, t + 1)
                    nc.vector.bn_aggr(mv[:, t], stats[:, t]).then_inc(mv_ok, 1)
                s = slice(b * KT, (b + 1) * KT)
                dve.wait_ge(mv_ok, (b + 1) * KT)
                nc.vector.tensor_scalar(veps[:, s], mv[:, s, 1], LN_EPS, None, ALU.add).then_inc(veps_ok, 1)

            def shifts(b):
                s = slice(b * KT, (b + 1) * KT)
                dve.wait_ge(rstd_ok, b + 1)
                nc.vector.tensor_tensor(shift[:, s], mv[:, s, 0], rstd[:, s], ALU.mult).then_inc(shift_ok, 1)
                dve.wait_ge(shift_ok, 2 * b + 1)
                nc.vector.tensor_scalar(shift[:, s], shift[:, s], -1.0, None, ALU.mult).then_inc(shift_ok, 1)

            def modulation(i):
                b, j = MOD_BLOCKS[i]
                dve.wait_ge(mod_mm, i + 1)
                dst = mod_early[:, b, j * C:(j + 1) * C] if j < 2 else mod_late[:, b, (j - 2) * C:(j - 1) * C]
                nc.vector.tensor_scalar(dst, mod_ps[i % 3][:, 0:C], 1.0 if j in (1, 4) else 0.0, None, ALU.add)\
                  .then_inc(mod_ok, 1)

            moments(0)
            shifts(0)
            for i in range(2 * B):
                modulation(i)
            moments(1)
            shifts(1)
            dve.wait_ge(mod_ok, 2 * B)
            dve.wait_ge(bv_ld, 16)

            def scale(t):
                dve.wait_ge(xn_ok, t + 1)
                if t >= 2:
                    dve.wait_ge(h_ok, t - 1)
                nc.vector.tensor_tensor(xm[:, t % 2], xn[:, t % 2], mod_early[:, t // KT, SC_MSA:SC_MSA + C],
                                        ALU.mult).then_inc(xm_ok, 1)

            def low_parts(t):
                s = slice(t * P, (t + 1) * P)
                dve.wait_ge(hi_ok, t + 1)
                nc.vector.tensor_tensor(x_lo[:, :, s], t_ps[t % 3][:, 0:2], f32(x_hi[:, 0:2, s]), ALU.subtract)
                nc.vector.tensor_tensor(x_hi[2 * HP:P, 2, s], t_ps[t % 3][2 * HP:P, 2], f32(x_hi[2 * HP:P, 2, s]),
                                        ALU.subtract).then_inc(lo_ok, 1)

            def values(t):
                dve.wait_ge(v_mm, t + 1)
                nc.vector.tensor_tensor(v_aug[:, t, :, 0:HD], v_ps[t % 2][:, 0:C].rearrange("p (h d) -> p h d", d=HD),
                                        bv[:].rearrange("p (h d) -> p h d", d=HD), ALU.add).then_inc(v_ok, 1)

            def late_modulation(r):
                if 2 * B + r < len(MOD_BLOCKS):
                    modulation(2 * B + r)

            rounds((8, values), (6, low_parts), (1, scale), extra=late_modulation)

        @block.tensor
        def _(pe):
            def modulation(i):
                b, j = MOD_BLOCKS[i]
                if i in (0, 2 * B):
                    pe.wait_ge(wa_ld[i // (2 * B)], 32)
                if i >= 3:
                    pe.wait_ge(mod_ok, i - 2)
                for k in range(KN):
                    rows = slice(0, KC + (k == KN - 1))
                    mm = nc.tensor.matmul(mod_ps[i % 3][:, 0:C], silu_b[rows, k, b], wa[rows, k, j * C:(j + 1) * C],
                                          start=(k == 0), stop=(k == KN - 1))
                mm.then_inc(mod_mm, 1)

            pe.wait_ge(silu_ok, KN + 1)
            for i in range(2 * B):
                modulation(i)
            pe.wait_ge(const_ok, 3)
            pe.wait_ge(wv_ok, 4)

            def transposes(t):
                pe.wait_ge(rem_ok, t + 1)
                if t >= 3:
                    pe.wait_ge(lo_ok, t - 2)
                for k in range(3):
                    mm = nc.tensor.transpose(t_ps[t % 3][:, k], h[:, t % 4, k * P:(k + 1) * P], ident[:])
                mm.then_inc(t_ok, 1)

            def values(t):
                pe.wait_ge(lo_ok, t + 1)
                if t >= 2:
                    pe.wait_ge(v_ok, t - 1)
                for i, (xs, xk, ws, wk) in enumerate(PRODUCTS):
                    mm = nc.tensor.matmul(v_ps[t % 2][:, 0:C], (x_hi, x_lo)[xs][:, xk, t * P:(t + 1) * P],
                                          (wv_hi, wv_lo)[ws][:, wk], start=(i == 0), stop=(i == 6))
                mm.then_inc(v_mm, 1)

            def late_modulation(r):
                if 2 * B + r < len(MOD_BLOCKS):
                    modulation(2 * B + r)

            rounds((7, values), (4, transposes), extra=late_modulation)


STEPS = 2 * KT
MAXIMA = GH * QT


def plan(g):
    tiles, proj, rows, outs = ([[] for _ in range(STEPS)] for _ in range(4))

    def spread(group, first_tile, first_step, counts):
        for st, n in enumerate(counts, first_step):
            tiles[st] += [(group, first_tile + i) for i in range(n)]
            first_tile += n

    if g == 0:
        spread(0, MAXIMA, 0, (3, 3, 3, 3, 2, 2))
        spread(1, 0, 7, (4, 4, 4, 4, 4, 3, 3, 3, 3))
        rows[5], rows[11], outs[12] = [(0, 1)], [(1, 0)], [(0, 0)]
        for u, st in enumerate((0, 1, 2, 3)):
            proj[st] = [(1, u)]
        for u, st in enumerate((9, 10, 13, 14)):
            proj[st] = [(2, u)]
    else:
        outs[2], outs[10], rows[1] = [(g - 1, 1)], [(g, 0)], [(g, 1)]
        if g + 1 < GG:
            spread(g + 1, 0, 2, (3, 3, 2, 3, 2, 3, 2, 2, 2, 2, 2, 2, 2, 2))
            rows[9] = [(g + 1, 0)]
        if g + 2 < GG:
            for u, st in enumerate((4, 6, 8, 11)):
                proj[st] = [(g + 2, u)]
    return tiles, proj, rows, outs


def attention(nc, sb, pb, sem, w_qkv, x_hi, x_lo, ident, v_aug, wqk, o_dram):
    ctx = ExitStack()
    with ctx:
        wqk_raw, wqk_hi, wqk_lo, bqk, w_ld, w_split, bias_ld = wqk
        proj_f = sb(ctx, "proj_f", [P, 2, HALF])
        parts = sb(ctx, "parts", [P, 4, 2, HALF], F32R)
        Q_LO, Q_HI, K_HI, K_LO = range(4)
        rows_dram = nc.dram_tensor("rows_scratch", (GG, 2, 2, GH * QT, P), F32, kind="Internal").ap()
        stack = [sb(ctx, f"stack{i}", [3 * HP, GH, 2, 2, HALF], F32R) for i in range(2)]
        negmax = sb(ctx, "negmax", [P, 2, 2, GH * QT])
        rows_hi = sb(ctx, "rows_hi", [GH * QT, 2, P], F32R)
        rows_lo = sb(ctx, "rows_lo", [GH * QT, 2, P], F32R)
        probs = sb(ctx, "probs", [P, 2, GH, HALF])
        o_sb = sb(ctx, "o_sb", [P, 2, HALF])
        rsum = sb(ctx, "rsum", [P, 2, QT * GH])
        o_norm = sb(ctx, "o_norm", [P, 2, QT * GH, HD])

        s_ps = [pb(ctx, f"s_ps{i}", [P, HALF]) for i in range(2)]
        m_ps = [pb(ctx, f"m_ps{i}", [P, N]) for i in range(2)]
        o_ps = pb(ctx, "o_ps", [P, HALF])
        misc = pb(ctx, "misc", [P, HALF])

        zero_ok = sem(ctx, "zero_ok")
        proj_mm = sem(ctx, "proj_mm")
        proj_ok = sem(ctx, "proj_ok")
        parts_ok = sem(ctx, "parts_ok")
        stack_ld = [sem(ctx, f"stack_ld{h}") for h in range(GH)]
        max_mm = sem(ctx, "max_mm")
        max_free = sem(ctx, "max_free")
        rows_mm = sem(ctx, "rows_mm")
        rows_step = sem(ctx, "rows_step")
        rows_ld = [sem(ctx, f"rows_ld{i}") for i in range(2)]
        rows_st = [sem(ctx, f"rows_st{i}") for i in range(2)]
        score_mm = sem(ctx, "score_mm")
        exp_free = sem(ctx, "exp_free")
        pv_free = sem(ctx, "pv_free")
        o_evac = sem(ctx, "o_evac")
        out_mm = sem(ctx, "out_mm")
        rsum_ok = sem(ctx, "rsum_ok")
        out_ok = sem(ctx, "out_ok")
        out_st = [sem(ctx, f"out_st{i}") for i in range(2)]

        block = ctx.enter_context(nc.Block())

        def low_part(eng, g, u):
            n = 4 * g + u
            half, a = u // 2, u % 2
            eng.wait_ge(proj_ok, n + 1)
            eng.tensor_tensor(parts[:, (Q_LO, K_LO)[a], half], proj_f[:, u % 2], f32(parts[:, (Q_HI, K_HI)[a], half]),
                              ALU.subtract).then_inc(parts_ok, 1)

        def max_tile(m):
            return m // MAXIMA, (m // QT) % GH, m % QT

        @block.sync
        def _(sp):
            def load_w(g):
                if g < GG:
                    sp.wait_ge(w_split, 4 * g)
                    load_group_weights(sp, w_qkv, wqk_raw, w_ld, g)

            def load_stack(g):
                s = g % 2
                sp.wait_ge(parts_ok, 4 * (g + 1))
                if g >= 2:
                    sp.wait_ge(score_mm, 64 * (g - 1))
                n = HP if g < 2 else HA
                for h in range(GH):
                    for q, kinds in enumerate((slice(Q_HI, K_HI + 1), slice(Q_HI, K_LO + 1, 2), slice(Q_LO, K_HI + 1, 2))):
                        sp.dma_start(f32(stack[s][q * HP:q * HP + n, h]).rearrange("p a b n -> p a (b n)"),
                                     f32(parts[h * HP:h * HP + n, kinds]).rearrange("p a b n -> p a (b n)"))\
                          .then_inc(stack_ld[h], 16)

            def load_rows_of_max(g, half):
                n, s = 2 * g + half, g % 2
                sp.wait_ge(rows_step, 2 * (n + 1))
                for part, rows in enumerate((rows_hi, rows_lo)):
                    sp.dma_start(rows_dram[g, half, part], f32(rows[:, half])).then_inc(rows_st[half], 16)
                sp.wait_ge(rows_st[half], 32 * (g + 1))
                for part, q in enumerate((0, 2)):
                    sp.dma_start(f32(stack[s][q * HP + HD:q * HP + HA, :, 0, half]),
                                 rows_dram[g, half, part].rearrange("(a h t) n -> a h (t n)", a=1, h=GH))\
                      .then_inc(rows_ld[half], 16)

            def store(g, half):
                n = 2 * g + half
                sp.wait_ge(out_ok, n + 1)
                sp.dma_start(o_dram[g, half], o_norm[:, half].rearrange("p t d -> p (t d)")).then_inc(out_st[half], 16)

            load_w(1)
            load_stack(0)
            load_rows_of_max(0, 0)
            for g in range(GG):
                if g + 1 < GG:
                    load_stack(g + 1)
                if g == 0:
                    load_rows_of_max(0, 1)
                    load_w(2)
                else:
                    load_rows_of_max(g, 1)
                    store(g - 1, 1)
                if g + 1 < GG:
                    load_rows_of_max(g + 1, 0)
                store(g, 0)
                load_w(g + 3)
            store(GG - 1, 1)
            for half in range(2):
                sp.wait_ge(out_st[half], 16 * GG)

        @block.gpsimd
        def _(pool):
            def split_w(g):
                if g < GG:
                    pool.wait_ge(proj_mm, 4 * g)
                    split_group_weights(pool, wqk, g)

            split_w(1)
            for g in range(GG):
                for st in range(STEPS):
                    for unit in plan(g)[1][st]:
                        low_part(pool, *unit)
                        if unit[1] == 3:
                            split_w(unit[0] + 1)

        @block.scalar
        def _(act):
            act.sem_inc(exp_free, 2)
            act.wait_ge(bias_ld, 16 * 16)

            def project(g, u):
                n = 4 * g + u
                half, a = u // 2, u % 2
                act.wait_ge(proj_mm, n + 1)
                if u == 0:
                    for h in range(GH):
                        act.wait_ge(stack_ld[h], 48 * g)
                if n >= 2:
                    act.wait_ge(parts_ok, n - 1)
                nc.scalar.activation(parts[:, (Q_HI, K_HI)[a], half], misc[:], ACT.Identity, bias=bqk[:, g, a:a + 1])
                nc.scalar.activation(proj_f[:, u % 2], misc[:], ACT.Identity, bias=bqk[:, g, a:a + 1])\
                  .then_inc(proj_ok, 1)

            def out_of_bank(g, half):
                n = 2 * g + half
                act.wait_ge(pv_free, 2 + 16 * g + KT * (half + 1))
                if n >= 2:
                    act.wait_ge(out_mm, n - 1)
                nc.scalar.copy(o_sb[:, half], o_ps[:]).then_inc(o_evac, 1)

            for u in range(4):
                project(0, u)
            for g in range(GG):
                for st in range(STEPS):
                    for h in range(GH):
                        n = 64 * g + 4 * st + h
                        if h == 2:
                            if st == 0 and g >= 1:
                                out_of_bank(g - 1, 1)
                            if st == KT:
                                out_of_bank(g, 0)
                            if st >= 1:
                                for unit in plan(g)[1][st - 1]:
                                    project(*unit)
                        act.wait_ge(score_mm, n + 1)
                        if h == 0:
                            act.wait_ge(pv_free, 16 * g + st + 1)
                        nc.scalar.activation(probs[:, st % 2, h], s_ps[h % 2][:], ACT.Exp, scale=SCALE)\
                          .then_inc(exp_free, 1)
            out_of_bank(GG - 1, 1)

        @block.vector
        def _(dve):
            nc.vector.memset(o_ps[:], 0.0).then_inc(zero_ok, 1)
            dve.sem_inc(max_free, 2)

            def maximum(g, m):
                half = m // 16
                n = 32 * g + m
                dve.wait_ge(max_mm, n + 1)
                nc.vector.tensor_reduce(negmax[:, half, g % 2, m % 16:m % 16 + 1],
                                        m_ps[m % 2][:], AX.X, ALU.max, negate=True).then_inc(max_free, 1)

            def rows(g, half):
                n = 2 * g + half
                dve.wait_ge(rows_mm, n + 1)
                if g >= 1:
                    dve.wait_ge(rows_ld[half], 32 * g)
                nc.vector.tensor_copy(rows_hi[:, half], misc[0:GH * QT, 0:P]).then_inc(rows_step, 1)
                dve.wait_ge(rows_step, 2 * n + 1)
                nc.vector.tensor_tensor(rows_lo[:, half], misc[0:GH * QT, 0:P], f32(rows_hi[:, half]),
                                        ALU.subtract).then_inc(rows_step, 1)

            def normalise(g, half):
                n = 2 * g + half
                o = misc[:].rearrange("p (t c) -> p t c", c=HP)
                dve.wait_ge(out_mm, n + 1)
                nc.vector.reciprocal(rsum[:, half], o[:, :, HD]).then_inc(rsum_ok, 1)
                dve.wait_ge(rsum_ok, n + 1)
                if g >= 1:
                    dve.wait_ge(out_st[half], 16 * g)
                nc.vector.tensor_tensor(o_norm[:, half], o[:, :, 0:HD],
                                        rsum[:, half].unsqueeze(2).broadcast_to([P, QT * GH, HD]),
                                        ALU.mult).then_inc(out_ok, 1)

            for u in range(4):
                low_part(dve, 0, u)
            for m in range(MAXIMA):
                maximum(0, m)
            rows(0, 0)
            for g in range(GG):
                for tiles, _, row_turns, out_turns in zip(*plan(g)):
                    for tile in tiles:
                        maximum(*tile)
                    for turn in row_turns:
                        rows(*turn)
                    for turn in out_turns:
                        normalise(*turn)
            normalise(GG - 1, 1)

        @block.tensor
        def _(pe):
            pe.sem_inc(pv_free, 2)

            last_use = [None]

            def take_misc(next_use):
                if last_use[0] is not None:
                    s, v = last_use[0]
                    pe.wait_ge(s, v)
                last_use[0] = next_use

            def project(g, u):
                half, a = u // 2, u % 2
                take_misc((proj_ok, 4 * g + u + 1))
                if u == 0:
                    pe.wait_ge(w_split, 4 * (g + 1))
                tok = (g // NG) * N + half * HALF
                for i, (xs, xk, ws, wk) in enumerate(PRODUCTS):
                    w = (wqk_hi, wqk_lo)[ws][:, wk, a].rearrange("p h d -> p (h d)")
                    mm = nc.tensor.matmul(misc[:], w, (x_hi, x_lo)[xs][:, xk, tok:tok + HALF],
                                          start=(i == 0), stop=(i == 6))
                mm.then_inc(proj_mm, 1)

            def maximum(g, m):
                half, h, qt = max_tile(m)
                n, s = 32 * g + m, g % 2
                if half == 0 and qt == 0:
                    pe.wait_ge(stack_ld[h], 48 * (g + 1))
                pe.wait_ge(max_free, n + 1)
                for kh in range(2):
                    mm = nc.tensor.matmul(m_ps[m % 2][:, kh * HALF:(kh + 1) * HALF],
                                          stack[s][:, h, 0, half, qt * P:(qt + 1) * P], stack[s][:, h, 1, kh],
                                          start=True, stop=True)
                mm.then_inc(max_mm, 1)

            def rows(g, half):
                n = 2 * g + half
                take_misc((rows_step, 2 * (n + 1)))
                pe.wait_ge(max_free, 2 + 32 * g + 16 * (half + 1))
                nc.tensor.transpose(misc[0:GH * QT, 0:P], negmax[:, half, g % 2], ident[:]).then_inc(rows_mm, 1)

            def outputs(g, half):
                n = 2 * g + half
                take_misc((out_ok, n + 1))
                pe.wait_ge(o_evac, n + 1)
                for t in range(QT):
                    mm = nc.tensor.transpose(misc[:, t * P:(t + 1) * P], o_sb[:, half, t * P:(t + 1) * P], ident[:])
                mm.then_inc(out_mm, 1)

            def scores(g, st, heads):
                half, kt, s = st // KT, st % KT, g % 2
                if kt == 0:
                    pe.wait_ge(rows_ld[half], 32 * (g + 1))
                for h in heads:
                    n = 64 * g + 4 * st + h
                    pe.wait_ge(exp_free, n + 1)
                    nc.tensor.matmul(s_ps[h % 2][:], stack[s][:, h, 1, kt // QT, (kt % QT) * P:(kt % QT + 1) * P],
                                     stack[s][:, h, 0, half], start=True, stop=True).then_inc(score_mm, 1)

            def values(g, st):
                half, kt = st // KT, st % KT
                pe.wait_ge(exp_free, 2 + 64 * g + 4 * (st + 1))
                if kt == 0:
                    n = 2 * g + half
                    if isinstance(n, int) and n == 0:
                        pe.wait_ge(zero_ok, 1)
                    else:
                        pe.wait_ge(o_evac, n)
                tile = (g // NG) * KT + kt
                for h in range(GH):
                    mm = nc.tensor.matmul(o_ps[h * HP:h * HP + HA], v_aug[:, tile, (g % NG) * GH + h],
                                          probs[:, st % 2, h], start=(kt == 0), stop=(kt == KT - 1))
                mm.then_inc(pv_free, 1)

            for u in range(4):
                project(0, u)
            for m in range(MAXIMA):
                maximum(0, m)
            rows(0, 0)
            for g in range(GG):
                for st, (tiles, units, row_turns, out_turns) in enumerate(zip(*plan(g))):
                    scores(g, st, (0, 1))
                    for tile in tiles[:1]:
                        maximum(*tile)
                    if st >= 1:
                        values(g, st - 1)
                    elif g >= 1:
                        values(g - 1, STEPS - 1)
                    for tile in tiles[1:2]:
                        maximum(*tile)
                    scores(g, st, (2, 3))
                    for tile in tiles[2:]:
                        maximum(*tile)
                    for turn in row_turns:
                        rows(*turn)
                    for turn in out_turns:
                        outputs(*turn)
                    for unit in units:
                        project(*unit)
            values(GG - 1, STEPS - 1)
            outputs(GG - 1, 1)


def experts(nc, sb, pb, sem, xt, ot, o_dram, w_proj, b_proj, w_gate, w1, b1, w2, b2, x_hi, x_lo, mod_late, ident,
            half_neg):
    ctx = ExitStack()
    PIECE = 3 * P
    PIECES = 6
    x1_dram = nc.dram_tensor("x1_scratch", (P, NT, C), F32, kind="Internal").ap()
    with ctx:
        w1_hi = [sb(ctx, "w1_hi0", [P, 3, H], F32R)]
        w1_lo = [sb(ctx, "w1_lo0", [P, 2, H], F32R)]
        w2_hi = [sb(ctx, "w2_hi0", [P, HT, C], F32R)]
        w2_lo = [sb(ctx, "w2_lo0", [P, HT, C], F32R)]
        w_raw = sb(ctx, "w_raw", [P, 2, 3, PIECE])
        b1c = sb(ctx, "b1c", [P, NE, HT])
        b2b = sb(ctx, "b2b", [P, NE, C])
        cw = sb(ctx, "cw", [P, NT, NE])
        piece_ld = [sem(ctx, f"piece_ld{i}") for i in range(2)]
        piece_step = sem(ctx, "piece_step")
        piece_ok = sem(ctx, "piece_ok")
        b1_ld = sem(ctx, "b1_ld")
        b2_ld = sem(ctx, "b2_ld")

        def load_piece(eng, e, i):
            n = PIECES * e + i
            buf = w_raw[:, i % 2]
            if n >= 2:
                eng.wait_ge(piece_ok, n - 1)
            if i < 3:
                c = slice(i * PIECE, (i + 1) * PIECE)
                eng.dma_start(buf[:, 0:2], w1[e, 0:2 * P, c].rearrange("(k p) n -> p k n", p=P))\
                   .then_inc(piece_ld[i % 2], 16)
                for q in range(4):
                    eng.dma_start(buf[q * HP:q * HP + REM, 2], w1[e, 2 * P:C, c]).then_inc(piece_ld[i % 2], 16)
            else:
                r = slice((i - 3) * PIECE, (i - 2) * PIECE)
                eng.dma_start(buf[:, :, 0:C], w2[e, r].rearrange("(k p) n -> p k n", p=P))\
                   .then_inc(piece_ld[i % 2], 16)

        def split_piece(pool, e, i):
            loads = (LOADS, LOADS + LOADS, 2 * LOADS + 1) if i % 2 == 0 else (LOADS, LOADS + 1, LOADS + 2)
            steps = 12 * e + (3 * i if i < 3 else 6 + i)
            pool.wait_ge(piece_ld[i % 2], 16 * (loads[2] * e + loads[i // 2]))
            raw = w_raw[:, i % 2]
            if i < 3:
                hi, lo = w1_hi[e % 2][:, :, i * PIECE:(i + 1) * PIECE], w1_lo[e % 2][:, :, i * PIECE:(i + 1) * PIECE]
                nc.gpsimd.tensor_copy(hi, raw).then_inc(piece_step, 1)
                pool.wait_ge(piece_step, steps + 1)
                nc.gpsimd.tensor_tensor(lo, raw[:, 0:2], f32(hi[:, 0:2]), ALU.subtract).then_inc(piece_step, 1)
                pool.wait_ge(piece_step, steps + 2)
                nc.gpsimd.tensor_tensor(hi[HP:2 * HP, 2], raw[HP:2 * HP, 2], f32(hi[HP:2 * HP, 2]), ALU.subtract)\
                  .then_inc(piece_step, 1)
                pool.wait_ge(piece_step, steps + 3)
                nc.gpsimd.tensor_tensor(hi[3 * HP:P, 2], raw[3 * HP:P, 2], f32(hi[3 * HP:P, 2]), ALU.subtract)\
                  .then_inc(piece_ok, 1)
                pool.wait_ge(piece_ok, PIECES * e + i + 1)
            else:
                hi, lo = (w[e % 2][:, 3 * (i - 3):3 * (i - 2)] for w in (w2_hi, w2_lo))
                nc.gpsimd.tensor_copy(hi, raw[:, :, 0:C]).then_inc(piece_step, 1)
                pool.wait_ge(piece_step, steps + 1)
                nc.gpsimd.tensor_tensor(lo, raw[:, :, 0:C], f32(hi), ALU.subtract).then_inc(piece_ok, 1)

        between(nc, sb, pb, sem, xt, o_dram, w_proj, b_proj, w_gate, b1, b2, x_hi, x_lo, mod_late, ident, half_neg,
                x1_dram, b1c, b2b, cw, b1_ld, b2_ld, load_piece, split_piece, PIECES)
        w1_hi.append(sb(ctx, "w1_hi1", [P, 3, H], F32R))
        w1_lo.append(sb(ctx, "w1_lo1", [P, 2, H], F32R))
        w2_hi.append(sb(ctx, "w2_hi1", [P, HT, C], F32R))
        w2_lo.append(sb(ctx, "w2_lo1", [P, HT, C], F32R))
        mixture(nc, sb, pb, sem, ot, x_hi, x_lo, mod_late, x1_dram, w1_hi, w1_lo, w2_hi, w2_lo, b1c, b2b, cw,
                b1_ld, b2_ld, piece_ok, load_piece, split_piece, PIECES)


def between(nc, sb, pb, sem, xt, o_dram, w_proj, b_proj, w_gate, b1, b2, x_hi, x_lo, mod_late, ident, half_neg,
            x1_dram, b1c, b2b, cw, b1_ld, b2_ld, load_piece, split_piece, PIECES):
    ctx = ExitStack()
    with ctx:
        wp_raw = sb(ctx, "wp_raw", [P, 3, C])
        wp_hi = sb(ctx, "wp_hi", [P, 3, C], F32R)
        wp_lo = sb(ctx, "wp_lo", [P, 2, C], F32R)
        wg_raw = sb(ctx, "wg_raw", [P, 3, NE])
        wg_hi = sb(ctx, "wg_hi", [P, 3, NE], F32R)
        wg_lo = sb(ctx, "wg_lo", [P, 2, NE], F32R)
        bp = sb(ctx, "bp", [P, C])
        o_in = sb(ctx, "o_in", [P, 4, 3 * P])
        x_in = sb(ctx, "xr", [P, 4, C])
        ot_hi = sb(ctx, "ot_hi", [P, 2, 3, P], F32R)
        ot_lo = sb(ctx, "ot_lo", [P, 2, 2, P], F32R)
        y = sb(ctx, "y", [P, 2, C])
        gy = sb(ctx, "gy", [P, 2, C])
        x1 = sb(ctx, "x1", [P, 4, C])
        stats = sb(ctx, "stats2", [P, 2, 6])
        mv = sb(ctx, "mv2", [P, 4, 2])
        veps = sb(ctx, "veps2", [P, NT])
        rstd = sb(ctx, "rstd2", [P, NT])
        xn = sb(ctx, "xn2", [P, 2, C])
        xm = sb(ctx, "xm2", [P, 2, C])
        h = sb(ctx, "h2", [P, 2, 3 * P])
        logits = sb(ctx, "logits", [P, NT, NE])
        rank = sb(ctx, "rank", [P, NT, NE])
        ge = sb(ctx, "ge", [P, 6, NT])
        top = sb(ctx, "top", [P, NT])
        shifted = sb(ctx, "shifted", [P, NT, NE])
        weight = sb(ctx, "weight", [P, NT, NE])
        wsum = sb(ctx, "wsum", [P, NT])

        to_ps = [pb(ctx, f"to_ps{i}", [P, 3, P]) for i in range(2)]
        y_ps = [pb(ctx, f"y_ps{i}", [P, 512]) for i in range(2)]
        tx_ps = [pb(ctx, f"tx_ps{i}", [P, 3, P]) for i in range(2)]
        gate_ps = pb(ctx, "gate_ps", [P, NT, NE])

        wp_ld = sem(ctx, "wp_ld")
        wg_ld = sem(ctx, "wg_ld")
        bp_ld = sem(ctx, "bp_ld")
        wp_ok = sem(ctx, "wp_ok")
        wg_ok = sem(ctx, "wg_ok")
        o_ld = [sem(ctx, f"o_ld{i}") for i in range(4)]
        xr_ld = [sem(ctx, f"xr_ld{i}") for i in range(4)]
        x1_st = [sem(ctx, f"x1_st{i}") for i in range(4)]
        orem_ok = sem(ctx, "orem_ok")
        to_mm = sem(ctx, "to_mm")
        ohi_ok = sem(ctx, "ohi_ok")
        olo_ok = sem(ctx, "olo_ok")
        y_mm = sem(ctx, "y_mm")
        y_ok = sem(ctx, "y_ok")
        gy_ok = sem(ctx, "gy_ok")
        x1_ok = sem(ctx, "x1_ok")
        stat_step = sem(ctx, "stat_step2")
        veps_ok = sem(ctx, "veps_ok2")
        rstd_ok = sem(ctx, "rstd_ok2")
        xn_ok = sem(ctx, "xn_ok2")
        xm_ok = sem(ctx, "xm_ok2")
        h_ok = sem(ctx, "h_ok2")
        rem_ok = sem(ctx, "rem_ok2")
        tx_mm = sem(ctx, "tx_mm")
        hi_ok = sem(ctx, "hi_ok2")
        lo_ok = sem(ctx, "lo_ok2")
        gate_mm = sem(ctx, "gate_mm")
        gate_step = sem(ctx, "gate_step")
        gexp_ok = sem(ctx, "gexp_ok")

        block = ctx.enter_context(nc.Block())

        @block.sync
        def _(sp):
            def load(t):
                b, half, qt = t // KT, (t % KT) // QT, t % QT
                if t >= 4:
                    sp.wait_ge(to_mm, t - 3)
                    sp.wait_ge(x1_ok, t - 3)
                sp.dma_start(o_in[:, t % 4, 0:C].rearrange("p (g c) -> p g c", g=NG),
                             o_dram[b * NG:(b + 1) * NG, half, :, qt * GC:(qt + 1) * GC]
                             .rearrange("g p c -> p g c")).then_inc(o_ld[t % 4], 16)
                sp.dma_start(x_in[:, t % 4], xt[:, t]).then_inc(xr_ld[t % 4], 16)

            def store(t):
                sp.wait_ge(x1_ok, t + 1)
                sp.dma_start(x1_dram[:, t], x1[:, t % 4]).then_inc(x1_st[t % 4], 16)

            load_rows(sp, wp_raw, w_proj, wp_ld)
            rounds((0, load), (4, store))
            for i in range(4):
                sp.wait_ge(x1_st[i], 16 * (NT // 4))

        @block.gpsimd
        def _(pool):
            pool.wait_ge(wp_ld, 16 * LOADS)
            split_weights(pool, wp_hi[:], wp_lo[:], wp_raw[:], (wp_ok, 0))
            pool.wait_ge(wg_ld, 16 * LOADS)
            split_weights(pool, wg_hi[:], wg_lo[:], wg_raw[:], (wg_ok, 0))

            def add_x(t):
                pool.wait_ge(xr_ld[t % 4], 16 * (t // 4 + 1))
                pool.wait_ge(gy_ok, t + 1)
                if t >= 4:
                    pool.wait_ge(x1_st[t % 4], 16 * (t // 4))
                    pool.wait_ge(xn_ok, t - 3)
                nc.gpsimd.tensor_tensor(x1[:, t % 4], x_in[:, t % 4], gy[:, t % 2], ALU.add).then_inc(x1_ok, 1)

            def root(t):
                pool.wait_ge(veps_ok, t + 1)
                nc.gpsimd.tensor_tensor(rstd[:, t:t + 1], veps[:, t:t + 1], half_neg[:, t:t + 1], ALU.pow)\
                  .then_inc(rstd_ok, 1)

            def shift(t):
                pool.wait_ge(xm_ok, t + 1)
                if t >= 2:
                    pool.wait_ge(tx_mm, t - 1)
                nc.gpsimd.tensor_tensor(h[:, t % 2, 0:C], xm[:, t % 2], mod_late[:, t // KT, SH_MLP:SH_MLP + C],
                                        ALU.add).then_inc(h_ok, 1)

            rounds((1, add_x), (2, root), (3, shift))
            for i in range(PIECES):
                split_piece(pool, 0, i)

        @block.scalar
        def _(act):
            load_rows(act, wg_raw, w_gate, wg_ld)
            act.dma_start(bp[:], b_proj.rearrange("(a n) -> a n", a=1).broadcast_to([P, C])).then_inc(bp_ld, 16)

            def remainder(src, t, buf):
                rem = src[:, buf, 2 * P:C].unsqueeze(1).broadcast_to([P, 3, REM])
                return nc.scalar.copy(src[:, buf, C:3 * P].rearrange("p (q c) -> p q c", q=3), rem)

            def attn_remainder(t):
                act.wait_ge(o_ld[t % 4], 16 * (t // 4 + 1))
                if t >= 4:
                    act.wait_ge(to_mm, t - 3)
                remainder(o_in, t, t % 4).then_inc(orem_ok, 1)

            def attn_high(t):
                act.wait_ge(to_mm, t + 1)
                if t >= 2:
                    act.wait_ge(y_mm, t - 1)
                nc.scalar.copy(ot_hi[:, t % 2], to_ps[t % 2][:]).then_inc(ohi_ok, 1)

            def x_remainder(t):
                act.wait_ge(h_ok, t + 1)
                remainder(h, t, t % 2).then_inc(rem_ok, 1)

            def x_high(t):
                act.wait_ge(tx_mm, t + 1)
                nc.scalar.copy(x_hi[:, :, t * P:(t + 1) * P], tx_ps[t % 2][:]).then_inc(hi_ok, 1)

            rounds((0, attn_remainder), (0, attn_high), (3, x_remainder), (4, x_high))
            for i in range(3):
                load_piece(act, 0, i)
            act.dma_start(b1c[:], b1.rearrange("e (t p) -> p e t", p=P)).then_inc(b1_ld, 16)
            act.dma_start(b2b[:], b2.rearrange("(a e) n -> a e n", a=1).broadcast_to([P, NE, C])).then_inc(b2_ld, 16)
            for i in range(3, PIECES):
                load_piece(act, 0, i)
            act.wait_ge(gate_step, 1 + 18 + 2)
            nc.scalar.activation(weight[:], shifted[:], ACT.Exp).then_inc(gexp_ok, 1)

        @block.vector
        def _(dve):
            def attn_low(t):
                dve.wait_ge(ohi_ok, t + 1)
                nc.vector.tensor_tensor(ot_lo[:, t % 2], to_ps[t % 2][:, 0:2], f32(ot_hi[:, t % 2, 0:2]), ALU.subtract)
                nc.vector.tensor_tensor(ot_hi[2 * HP:P, t % 2, 2], to_ps[t % 2][2 * HP:P, 2],
                                        f32(ot_hi[2 * HP:P, t % 2, 2]), ALU.subtract).then_inc(olo_ok, 1)

            def bias_and_gate(t):
                dve.wait_ge(y_mm, t + 1)
                if t == 0:
                    dve.wait_ge(bp_ld, 16)
                nc.vector.tensor_tensor(y[:, t % 2], y_ps[t % 2][:, 0:C], bp[:], ALU.add).then_inc(y_ok, 1)
                dve.wait_ge(y_ok, t + 1)
                if t >= 2:
                    dve.wait_ge(x1_ok, t - 1)
                nc.vector.tensor_tensor(gy[:, t % 2], y[:, t % 2], mod_late[:, t // KT, G_MSA:G_MSA + C],
                                        ALU.mult).then_inc(gy_ok, 1)

            def moments(t):
                dve.wait_ge(x1_ok, t + 1)
                nc.vector.bn_stats(stats[:, t % 2], x1[:, t % 4]).then_inc(stat_step, 1)
                dve.wait_ge(stat_step, 2 * t + 1)
                nc.vector.bn_aggr(mv[:, t % 4], stats[:, t % 2]).then_inc(stat_step, 1)
                dve.wait_ge(stat_step, 2 * t + 2)
                nc.vector.tensor_scalar(veps[:, t:t + 1], mv[:, t % 4, 1:2], LN_EPS, None, ALU.add)\
                  .then_inc(veps_ok, 1)

            def normalise(t):
                dve.wait_ge(rstd_ok, t + 1)
                nc.vector.tensor_scalar(xn[:, t % 2], x1[:, t % 4], mv[:, t % 4, 0:1], rstd[:, t:t + 1],
                                        ALU.subtract, ALU.mult).then_inc(xn_ok, 1)
                dve.wait_ge(xn_ok, t + 1)
                if t >= 2:
                    dve.wait_ge(h_ok, t - 1)
                nc.vector.tensor_tensor(xm[:, t % 2], xn[:, t % 2], mod_late[:, t // KT, SC_MLP:SC_MLP + C],
                                        ALU.mult).then_inc(xm_ok, 1)

            def x_low(t):
                s = slice(t * P, (t + 1) * P)
                dve.wait_ge(hi_ok, t + 1)
                nc.vector.tensor_tensor(x_lo[:, :, s], tx_ps[t % 2][:, 0:2], f32(x_hi[:, 0:2, s]), ALU.subtract)
                nc.vector.tensor_tensor(x_hi[2 * HP:P, 2, s], tx_ps[t % 2][2 * HP:P, 2], f32(x_hi[2 * HP:P, 2, s]),
                                        ALU.subtract).then_inc(lo_ok, 1)

            rounds((0, attn_low), (1, bias_and_gate), (2, moments), (3, normalise), (4, x_low))

            step = 0

            def then(instruction):
                nonlocal step
                step += 1
                instruction.then_inc(gate_step, 1)
                dve.wait_ge(gate_step, step)

            dve.wait_ge(gate_mm, NT)
            then(nc.vector.tensor_copy(logits[:], gate_ps[:]))
            for e in range(NE):
                nc.vector.memset(rank[:, :, e], float(NE - 1 - e))
            pairs = [(i, j) for i in range(NE) for j in range(i + 1, NE)]
            for n, (i, j) in enumerate(pairs):
                then(nc.vector.tensor_tensor(ge[:, n], logits[:, :, i], logits[:, :, j], ALU.is_ge))
                then(nc.vector.tensor_tensor(rank[:, :, j], rank[:, :, j], ge[:, n], ALU.add))
                then(nc.vector.tensor_tensor(rank[:, :, i], rank[:, :, i], ge[:, n], ALU.subtract))
            then(nc.vector.tensor_reduce(top[:], logits[:], AX.X, ALU.max))
            then(nc.vector.tensor_tensor(shifted[:], logits[:], top[:].unsqueeze(2).broadcast_to([P, NT, NE]),
                                         ALU.subtract))
            dve.wait_ge(gexp_ok, 1)
            then(nc.vector.scalar_tensor_tensor(out=weight[:], in0=rank[:], scalar=2.0, in1=weight[:],
                                                op0=ALU.is_lt, op1=ALU.mult))
            then(nc.vector.tensor_reduce(wsum[:], weight[:], AX.X, ALU.add))
            then(nc.vector.reciprocal(wsum[:], wsum[:]))
            then(nc.vector.tensor_tensor(cw[:], weight[:], wsum[:].unsqueeze(2).broadcast_to([P, NT, NE]), ALU.mult))

        @block.tensor
        def _(pe):
            def attn_transposes(t):
                pe.wait_ge(orem_ok, t + 1)
                if t >= 2:
                    pe.wait_ge(olo_ok, t - 1)
                for k in range(3):
                    mm = nc.tensor.transpose(to_ps[t % 2][:, k], o_in[:, t % 4, k * P:(k + 1) * P], ident[:])
                mm.then_inc(to_mm, 1)

            def project(t):
                pe.wait_ge(olo_ok, t + 1)
                if t == 0:
                    pe.wait_ge(wp_ok, 4)
                if t >= 2:
                    pe.wait_ge(y_ok, t - 1)
                for i, (xs, xk, ws, wk) in enumerate(PRODUCTS):
                    mm = nc.tensor.matmul(y_ps[t % 2][:, 0:C], (ot_hi, ot_lo)[xs][:, t % 2, xk], (wp_hi, wp_lo)[ws][:, wk],
                                          start=(i == 0), stop=(i == 6))
                mm.then_inc(y_mm, 1)

            def x_transposes(t):
                pe.wait_ge(rem_ok, t + 1)
                if t >= 2:
                    pe.wait_ge(lo_ok, t - 1)
                for k in range(3):
                    mm = nc.tensor.transpose(tx_ps[t % 2][:, k], h[:, t % 2, k * P:(k + 1) * P], ident[:])
                mm.then_inc(tx_mm, 1)

            def gate(t):
                pe.wait_ge(lo_ok, t + 1)
                if t == 0:
                    pe.wait_ge(wg_ok, 4)
                for i, (xs, xk, ws, wk) in enumerate(PRODUCTS):
                    mm = nc.tensor.matmul(gate_ps[:, t], (x_hi, x_lo)[xs][:, xk, t * P:(t + 1) * P],
                                          (wg_hi, wg_lo)[ws][:, wk], start=(i == 0), stop=(i == 6))
                mm.then_inc(gate_mm, 1)

            rounds((0, attn_transposes), (1, project), (4, x_transposes), (5, gate))


def mixture(nc, sb, pb, sem, ot, x_hi, x_lo, mod_late, x1_dram, w1_hi, w1_lo, w2_hi, w2_lo, b1c, b2b, cw,
            b1_ld, b2_ld, piece_ok, load_piece, split_piece, PIECES):
    ctx = ExitStack()
    RING = 3
    LAG = 2
    assert HT % RING == 0
    with ctx:
        hid = sb(ctx, "hid", [P, RING, CH])
        hid_hi = sb(ctx, "hid_hi", [P, RING, CH], F32R)
        hid_lo = sb(ctx, "hid_lo", [P, RING, CH], F32R)
        acc = sb(ctx, "acc", [P, NT, C])
        part = sb(ctx, "part", [P, TCH, C])
        x1 = sb(ctx, "x1_in", [P, 2, C])
        gated = sb(ctx, "gated", [P, 2, C])
        res = sb(ctx, "res", [P, 2, C])
        h_ps = [pb(ctx, f"h_ps{i}", [P, CH]) for i in range(RING)]
        y_ps = [pb(ctx, f"e_ps{i}", [P, 512]) for i in range(TCH)]

        up_mm = sem(ctx, "up_mm")
        gelu_ok = sem(ctx, "gelu_ok")
        hi_ok = sem(ctx, "hid_hi_ok")
        split_ok = sem(ctx, "split_ok")
        down_mm = sem(ctx, "down_mm")
        part_ok = sem(ctx, "part_ok")
        bias_ok = sem(ctx, "bias_ok")
        add_ok = sem(ctx, "add_ok")
        x1_ld = [sem(ctx, f"x1_ld{i}") for i in range(2)]
        gated_ok = sem(ctx, "gated_ok")
        res_ok = sem(ctx, "res_ok")
        out_st = [sem(ctx, f"y_st{i}") for i in range(2)]

        def chunks(eng, e, body):
            if e < NE - 1:
                with eng.Fori(0, NCH) as c:
                    body(c, c + NCH * e)
            else:
                for c in range(NCH):
                    body(c, c + NCH * e)

        block = ctx.enter_context(nc.Block())

        @block.sync
        def _(sp):
            for e in range(1, NE):
                for i in range(PIECES):
                    load_piece(sp, e, i)
            for t in range(NT):
                if t >= 2:
                    sp.wait_ge(res_ok, t - 1)
                sp.dma_start(x1[:, t % 2], x1_dram[:, t]).then_inc(x1_ld[t % 2], 16)
                if t >= 1:
                    sp.wait_ge(res_ok, t)
                    sp.dma_start(ot[:, t - 1], res[:, (t - 1) % 2]).then_inc(out_st[(t - 1) % 2], 16)
            sp.wait_ge(res_ok, NT)
            sp.dma_start(ot[:, NT - 1], res[:, (NT - 1) % 2]).then_inc(out_st[(NT - 1) % 2], 16)
            for i in range(2):
                sp.wait_ge(out_st[i], 16 * NT // 2)

        @block.gpsimd
        def _(pool):
            pool.sem_inc(add_ok, TCH)
            for e in range(NE):
                for c in range(NCH):
                    if e + 1 < NE and c < 3:
                        if c == 0 and e >= 1:
                            pool.wait_ge(down_mm, RING + HT * NCH * e)
                        for i in (2 * c, 2 * c + 1):
                            split_piece(pool, e + 1, i)
                    for t in range(TCH):
                        tile = TCH * c + t
                        n = NT * e + tile
                        pool.wait_ge(bias_ok, n + 1)
                        pool.wait_ge(part_ok, TCH + n + 1)
                        nc.gpsimd.tensor_tensor(acc[:, tile], acc[:, tile], part[:, t], ALU.add).then_inc(add_ok, 1)

        @block.scalar
        def _(act):
            act.sem_inc(gelu_ok, RING)
            act.sem_inc(part_ok, TCH)
            act.wait_ge(b1_ld, 16)

            for e in range(NE):
                def chunk(c, n, e=e):
                    for ht in range(HT):
                        k = n * HT + ht
                        act.wait_ge(up_mm, k + 1)
                        act.wait_ge(split_ok, k + 1)
                        nc.scalar.activation(hid[:, ht % RING], h_ps[ht % RING][:], ACT.Gelu_apprx_tanh,
                                             bias=b1c[:, e, ht:ht + 1]).then_inc(gelu_ok, 1)
                    act.wait_ge(down_mm, RING + (n + 1) * HT)
                    for t in range(TCH):
                        act.wait_ge(add_ok, n * TCH + t + 1)
                        nc.scalar.activation(part[:, t], y_ps[t][:, 0:C], ACT.Copy,
                                             scale=cw[:, c * TCH + t, e:e + 1]).then_inc(part_ok, 1)

                chunks(act, e, chunk)

        @block.vector
        def _(dve):
            dve.sem_inc(split_ok, RING)
            dve.wait_ge(b2_ld, 16)

            def finish(tile):
                n = NT * (NE - 1) + tile
                dve.wait_ge(add_ok, TCH + n + 1)
                nc.vector.tensor_tensor(gated[:, tile % 2], acc[:, tile], mod_late[:, tile // KT, G_MLP:G_MLP + C],
                                        ALU.mult).then_inc(gated_ok, 1)
                dve.wait_ge(gated_ok, tile + 1)
                dve.wait_ge(x1_ld[tile % 2], 16 * (tile // 2 + 1))
                if tile >= 2:
                    dve.wait_ge(out_st[tile % 2], 16 * (tile // 2))
                nc.vector.tensor_tensor(res[:, tile % 2], gated[:, tile % 2], x1[:, tile % 2], ALU.add)\
                  .then_inc(res_ok, 1)

            for e in range(NE):
                def chunk(c, n, e=e):
                    for ht in range(HT):
                        k = n * HT + ht
                        dve.wait_ge(gelu_ok, RING + k + 1)
                        dve.wait_ge(down_mm, k + 1)
                        nc.vector.tensor_copy(hid_hi[:, ht % RING], hid[:, ht % RING]).then_inc(hi_ok, 1)
                        dve.wait_ge(hi_ok, k + 1)
                        nc.vector.tensor_tensor(hid_lo[:, ht % RING], hid[:, ht % RING], f32(hid_hi[:, ht % RING]),
                                                ALU.subtract).then_inc(split_ok, 1)
                        if 3 <= ht < 3 + TCH:
                            t = ht - 3
                            acc_t, cw_t = acc[:, c * TCH + t], cw[:, c * TCH + t, e:e + 1]
                            if e == 0:
                                nc.vector.tensor_scalar(acc_t, b2b[:, e], cw_t, None, ALU.mult).then_inc(bias_ok, 1)
                            else:
                                dve.wait_ge(add_ok, TCH + n * TCH + t + 1 - NT)
                                nc.vector.scalar_tensor_tensor(out=acc_t, in0=b2b[:, e], scalar=cw_t, in1=acc_t,
                                                               op0=ALU.mult, op1=ALU.add).then_inc(bias_ok, 1)
                        if e == NE - 1 and c >= 1 and ht in (2, 4, 6, 8):
                            finish(TCH * (c - 1) + ht // 2 - 1)

                chunks(dve, e, chunk)
            for t in range(NT - TCH, NT):
                finish(t)

        @block.tensor
        def _(pe):
            pe.sem_inc(down_mm, RING)
            for e in range(NE):
                pe.wait_ge(piece_ok, PIECES * (e + 1))

                def chunk(c, n, e=e):
                    w1s, w2s = (w1_hi[e % 2], w1_lo[e % 2]), (w2_hi[e % 2], w2_lo[e % 2])

                    def up(ht):
                        k = n * HT + ht
                        pe.wait_ge(gelu_ok, k + 1)
                        for i, (xs, xk, ws, wk) in enumerate(PRODUCTS):
                            mm = nc.tensor.matmul(h_ps[ht % RING][:], w1s[ws][:, wk, ht * P:(ht + 1) * P],
                                                  (x_hi, x_lo)[xs][:, xk, bass.ds(c * CH, CH)],
                                                  start=(i == 0), stop=(i == 6))
                        mm.then_inc(up_mm, 1)

                    def down(ht):
                        k = n * HT + ht
                        pe.wait_ge(split_ok, RING + k + 1)
                        for t in range(TCH):
                            if ht == 0:
                                pe.wait_ge(part_ok, n * TCH + t + 1)
                            s = slice(t * P, (t + 1) * P)
                            for i, (hs, ws) in enumerate(((hid_hi, 0), (hid_hi, 1), (hid_lo, 0))):
                                mm = nc.tensor.matmul(y_ps[t][:, 0:C], hs[:, ht % RING, s], w2s[ws][:, ht],
                                                      start=(ht == 0 and i == 0), stop=(ht == HT - 1 and i == 2))
                        mm.then_inc(down_mm, 1)

                    for ht in range(HT):
                        up(ht)
                        if ht >= LAG:
                            down(ht - LAG)
                    for ht in range(HT - LAG, HT):
                        down(ht)

                chunks(pe, e, chunk)


_INS = ["x", "cond_1152", "L0_cond_w_adaln", "L0_cond_b_adaln", "L0_cond_w_qkv", "L0_cond_b_qkv", "L0_cond_w_proj",
        "L0_cond_b_proj", "L0_cond_w_gate", "L0_cond_w1", "L0_cond_b1", "L0_cond_w2", "L0_cond_b2"]


def kernel(**inputs):
    import numpy as np
    import concourse.bacc as bacc
    from concourse.bass_utils import run_bass_kernel_spmd

    nc = bacc.Bacc("TRN2", target_bir_lowering=False, num_devices=1)
    arrays, args = {}, []
    for name in _INS:
        a = np.ascontiguousarray(inputs[name])
        arrays[f"in_{name}"] = a
        args.append(nc.dram_tensor(f"in_{name}", a.shape, mybir.dt.from_np(a.dtype), kind="ExternalInput").ap())
    out = nc.dram_tensor("out", (B, N, C), F32, kind="ExternalOutput").ap()
    build_kernel(nc, *args, out)
    r = run_bass_kernel_spmd(nc, [arrays], core_ids=[0])
    return r.results[0]["out"]
```

```python
from contextlib import ExitStack

import concourse.bass as bass
from concourse import mybir

ALU = mybir.AluOpType
ACT = mybir.ActivationFunctionType
AX = mybir.AxisListType
F32 = mybir.dt.float32
F32R = mybir.dt.float32r

P = 128
B, N, C = 2, 1024, 288
T = B * N
NT = T // P
NH, HD = 16, 18
HP = 32
HA = HD + 1
GH = 4
NG = NH // GH
GG = B * NG
GC = GH * HD
HALF = N // 2
KT = N // P
QT = HALF // P
MOD = 6 * C
NE, H = 4, 1152
HT = H // P
CH = 512
NCH = T // CH
TCH = CH // P
EXPERT_WORDS = (3 + 2) * H + 2 * HT * C
REM = C - 2 * P
LN_EPS = 1e-6
SCALE = HD ** -0.5
SH_MSA, SC_MSA = 0, C
G_MSA, SH_MLP, SC_MLP, G_MLP = 0, C, 2 * C, 3 * C

PRODUCTS = [(0, 0, 0, 0), (0, 1, 0, 1), (0, 2, 0, 2), (0, 0, 1, 0), (0, 1, 1, 1), (1, 0, 0, 0), (1, 1, 0, 1)]


def f32(ap):
    return ap.bitcast(F32)


def split_weights(eng, hi, lo, raw, done):
    n = done[1]
    eng.tensor_copy(hi, raw).then_inc(done[0], 1)
    eng.wait_ge(done[0], n + 1)
    eng.tensor_tensor(lo, raw[:, 0:2], f32(hi[:, 0:2]), ALU.subtract).then_inc(done[0], 1)
    for i, q in enumerate((1, 3)):
        s = slice(q * HP, q * HP + REM)
        eng.wait_ge(done[0], n + 2 + i)
        eng.tensor_tensor(hi[s, 2], raw[s, 2], f32(hi[s, 2]), ALU.subtract).then_inc(done[0], 1)
    eng.wait_ge(done[0], n + 4)


def load_rows(eng, dst, w, sem):
    eng.dma_start(dst[:, 0:2], w[0:2 * P].rearrange("(k p) n -> p k n", p=P)).then_inc(sem, 16)
    for q in range(4):
        eng.dma_start(dst[q * HP:q * HP + REM, 2], w[2 * P:C]).then_inc(sem, 16)


LOADS = 5


def rounds(*stages, extra=None):
    for r in range(min(0, *(d for d, _ in stages)), NT + max(d for d, _ in stages)):
        for d, stage in stages:
            if 0 <= r - d < NT:
                stage(r - d)
        if extra:
            extra(r)


def build_kernel(nc, x, cond, w_adaln, b_adaln, w_qkv, b_qkv, w_proj, b_proj, w_gate, w1, b1, w2, b2, out):
    outer = ExitStack()

    def sb(stack, name, shape, dt=F32):
        return stack.enter_context(nc.sbuf_tensor(name, shape, dt))

    def pb(stack, name, shape, dt=F32):
        return stack.enter_context(nc.psum_tensor(name, shape, dt))

    def sem(stack, name):
        return stack.enter_context(nc.semaphore(name))

    o_dram = nc.dram_tensor("o_scratch", (B, 2, P, QT, C), F32, kind="Internal").ap()
    xt = x.rearrange("b (t p) c -> p (b t) c", p=P)
    ot = out.rearrange("b (t p) c -> p (b t) c", p=P)

    outer.enter_context(nc.allow_non_contiguous_dma(reason="biases and the condition are laid out by column"))
    with outer:
        stretch = sb(outer, "stretch", [P, max(5 * T, EXPERT_WORDS)], F32R)
        x_hi = stretch[:, 0:3 * T].rearrange("p (k t) -> p k t", k=3)
        x_lo = stretch[:, 3 * T:5 * T].rearrange("p (k t) -> p k t", k=2)
        late = LateWeights(nc, sb, sem, outer, w_proj, b_proj, w_gate, w1, b1, w2, stretch)
        mod_late = sb(outer, "mod_late", [P, B, 4 * C])
        ident = sb(outer, "ident", [P, P])
        half_neg = sb(outer, "half_neg", [P, NT])

        outputs_in = OutputTiles(sb, sem, outer, o_dram)
        setup_and_attention = ExitStack()
        with setup_and_attention:
            v_aug = sb(setup_and_attention, "v_aug", [P, NT, NH, HA])
            wqk = (sb(setup_and_attention, "wqk_raw", [P, 3, 2, GC]),
                   sb(setup_and_attention, "wqk_hi", [P, 3, 2, GH, HP], F32R),
                   sb(setup_and_attention, "wqk_lo", [P, 2, 2, GH, HP], F32R),
                   sb(setup_and_attention, "bqk", [P, GG, 2]),
                   sem(setup_and_attention, "w_ld"), sem(setup_and_attention, "w_split"),
                   sem(setup_and_attention, "bias_ld"))
            heads = HeadParts(nc, sb, sem, setup_and_attention, x_hi, x_lo, wqk)
            late.stage_in(heads.parts)
            setup(nc, sb, pb, sem, xt, cond, w_adaln, b_adaln, w_qkv, b_qkv, x_hi, x_lo, mod_late, ident, half_neg, v_aug,
                  wqk, heads, outputs_in.tiles)
            attention(nc, sb, pb, sem, w_qkv, ident, v_aug, wqk, heads, o_dram, late, outputs_in)
        experts(nc, sb, pb, sem, xt, ot, b2, mod_late, ident, half_neg, late, outputs_in)


class OutputTiles:
    BUFS = 4

    def __init__(self, sb, sem, stack, o_dram):
        self.o_dram = o_dram
        self.tiles = sb(stack, "o_in", [P, self.BUFS, 3 * P])
        self.stored = [sem(stack, f"out_st{i}") for i in range(2)]
        self.loaded = [sem(stack, f"o_ld{i}") for i in range(self.BUFS)]

    def load(self, sp, t):
        b, half, qt = t // KT, (t % KT) // QT, t % QT
        sp.dma_start(self.tiles[:, t % self.BUFS, 0:C], self.o_dram[b, half, :, qt])\
          .then_inc(self.loaded[t % self.BUFS], 16)

    def wait(self, eng, t):
        eng.wait_ge(self.loaded[t % self.BUFS], 16 * (t // self.BUFS + 1))


def split_tiles(flat, hi_tiles, lo_tiles, n, at):
    mid, end = at + hi_tiles * n, at + (hi_tiles + lo_tiles) * n
    return (flat[:, at:mid].rearrange("p (k n) -> p k n", k=hi_tiles),
            flat[:, mid:end].rearrange("p (k n) -> p k n", k=lo_tiles))


class LateWeights:
    PIECE = 3 * P
    PIECES = 6

    def __init__(self, nc, sb, sem, outer, w_proj, b_proj, w_gate, w1, b1, w2, stretch):
        self.nc, self.w_proj, self.b_proj, self.w_gate, self.w1, self.b1, self.w2 = \
            nc, w_proj, b_proj, w_gate, w1, b1, w2
        self.wp_hi = sb(outer, "wp_hi", [P, 3, C], F32R)
        self.wp_lo = sb(outer, "wp_lo", [P, 2, C], F32R)
        self.wg_hi = sb(outer, "wg_hi", [P, 3, NE], F32R)
        self.wg_lo = sb(outer, "wg_lo", [P, 2, NE], F32R)
        self.bp_raw = sb(outer, "bp_raw", [2 * HP, C])
        self.bp = sb(outer, "bp", [2 * HP, C], F32R)
        self.ones = sb(outer, "ones", [2 * HP, P], F32R)
        self.b1c = sb(outer, "b1c", [P, NE, HT])
        self.b1_ld = sem(outer, "b1_ld")
        self.bp_zero = sem(outer, "bp_zero")
        self.bp_ld = sem(outer, "bp_ld")
        self.bp_ok = sem(outer, "bp_ok")
        self.wp_ld = sem(outer, "wp_ld")
        self.wg_ld = sem(outer, "wg_ld")
        self.wp_ok = sem(outer, "wp_ok")
        self.wg_ok = sem(outer, "wg_ok")
        self.piece_ld = [sem(outer, f"piece_ld{i}") for i in range(2)]
        self.piece_hi = sem(outer, "piece_hi")
        self.piece_step = sem(outer, "piece_step")
        self.piece_ok = sem(outer, "piece_ok")
        self.places = []
        self.add_place(stretch)

    def add_place(self, flat):
        self.places.append((split_tiles(flat, 3, 2, H, 0), split_tiles(flat, HT, HT, C, 5 * H)))

    def stage_in(self, parts):
        words = f32(parts[:].rearrange("p a b n -> p (a b n)"))
        n = 3 * self.PIECE
        self.raw0 = [words[:, i * n:(i + 1) * n].rearrange("p (k n) -> p k n", k=3) for i in range(2)]
        self.wp_raw = words[:, 2 * n:2 * n + 3 * C].rearrange("p (k n) -> p k n", k=3)
        self.wg_raw = words[:, 2 * n + 3 * C:2 * n + 3 * (C + NE)].rearrange("p (k n) -> p k n", k=3)

    def raw(self, e, i):
        return self.raw0[i % 2] if e == 0 else self.w_raw[:, i % 2]

    def load_biases(self, eng):
        eng.dma_start(self.b1c[:], self.b1.rearrange("e (t p) -> p e t", p=P)).then_inc(self.b1_ld, 16)

    def load_projections(self, eng):
        eng.wait_ge(self.bp_zero, 1)
        for q in range(2):
            eng.dma_start(self.bp_raw[q * HP:q * HP + 1], self.b_proj.rearrange("(a n) -> a n", a=1))\
               .then_inc(self.bp_ld, 16)
        load_rows(eng, self.wp_raw, self.w_proj, self.wp_ld)
        load_rows(eng, self.wg_raw, self.w_gate, self.wg_ld)

    def clear_bias_rows(self, eng):
        eng.memset(self.bp_raw[:], 0.0).then_inc(self.bp_zero, 1)

    def split_projections(self, eng):
        eng.memset(f32(self.ones[:]), 1.0).then_inc(self.bp_ok, 1)
        eng.wait_ge(self.bp_ld, 32)
        eng.wait_ge(self.bp_ok, 1)
        eng.tensor_copy(self.bp[:], self.bp_raw[:]).then_inc(self.bp_ok, 1)
        eng.wait_ge(self.bp_ok, 2)
        eng.tensor_tensor(self.bp[HP:HP + 1], self.bp_raw[HP:HP + 1], f32(self.bp[HP:HP + 1]), ALU.subtract)\
           .then_inc(self.bp_ok, 1)
        eng.wait_ge(self.bp_ok, 3)
        eng.tensor_copy(self.ones[:], f32(self.ones[:])).then_inc(self.bp_ok, 1)
        eng.wait_ge(self.bp_ok, 4)
        eng.wait_ge(self.wp_ld, 16 * LOADS)
        split_weights(eng, self.wp_hi[:], self.wp_lo[:], self.wp_raw, (self.wp_ok, 0))
        eng.wait_ge(self.wg_ld, 16 * LOADS)
        split_weights(eng, self.wg_hi[:], self.wg_lo[:], self.wg_raw, (self.wg_ok, 0))

    def load_piece(self, eng, e, i):
        n = self.PIECES * e + i
        buf = self.raw(e, i)
        if n >= 2:
            eng.wait_ge(self.piece_ok, n - 1)
        if i < 3:
            c = slice(i * self.PIECE, (i + 1) * self.PIECE)
            eng.dma_start(buf[:, 0:2], self.w1[e, 0:2 * P, c].rearrange("(k p) n -> p k n", p=P))\
               .then_inc(self.piece_ld[i % 2], 16)
            for q in range(4):
                eng.dma_start(buf[q * HP:q * HP + REM, 2], self.w1[e, 2 * P:C, c]).then_inc(self.piece_ld[i % 2], 16)
        else:
            r = slice((i - 3) * self.PIECE, (i - 2) * self.PIECE)
            eng.dma_start(buf[:, :, 0:C], self.w2[e, r].rearrange("(k p) n -> p k n", p=P))\
               .then_inc(self.piece_ld[i % 2], 16)

    def split_piece(self, pool, e, i):
        nc, (w1s, w2s), raw = self.nc, self.places[e % 2], self.raw(e, i)
        if i < 3:
            c = slice(i * self.PIECE, (i + 1) * self.PIECE)
            hi, lo = (w[:, :, c] for w in w1s)
        else:
            r = slice(3 * (i - 3), 3 * (i - 2))
            raw, hi, lo = raw[:, :, 0:C], w2s[0][:, r], w2s[1][:, r]
        loads = (LOADS, 2 * LOADS, 2 * LOADS + 1) if i % 2 == 0 else (LOADS, LOADS + 1, LOADS + 2)
        pool.wait_ge(self.piece_ld[i % 2], 16 * (loads[2] * e + loads[i // 2]))
        nc.gpsimd.tensor_copy(hi, raw).then_inc(self.piece_hi, 1)
        pool.wait_ge(self.piece_hi, self.PIECES * e + i + 1)
        if i >= 3:
            nc.gpsimd.tensor_tensor(lo, raw, f32(hi), ALU.subtract).then_inc(self.piece_ok, 1)
            return
        steps = 6 * e + 2 * i
        nc.gpsimd.tensor_tensor(lo, raw[:, 0:2], f32(hi[:, 0:2]), ALU.subtract).then_inc(self.piece_step, 1)
        pool.wait_ge(self.piece_step, steps + 1)
        nc.gpsimd.tensor_tensor(hi[HP:2 * HP, 2], raw[HP:2 * HP, 2], f32(hi[HP:2 * HP, 2]), ALU.subtract)\
          .then_inc(self.piece_step, 1)
        pool.wait_ge(self.piece_step, steps + 2)
        nc.gpsimd.tensor_tensor(hi[3 * HP:P, 2], raw[3 * HP:P, 2], f32(hi[3 * HP:P, 2]), ALU.subtract)\
          .then_inc(self.piece_ok, 1)
        pool.wait_ge(self.piece_ok, self.PIECES * e + i + 1)


def load_group_weights(sp, w_qkv, wqk_raw, w_ld, g):
    c = (g % NG) * GC
    for k in range(2):
        sp.dma_start(wqk_raw[:, k], w_qkv[k * P:(k + 1) * P, 0:2 * C]
                     .rearrange("p (a n) -> p a n", a=2)[:, :, c:c + GC]).then_inc(w_ld, 16)
    for q in range(4):
        sp.dma_start(wqk_raw[q * HP:q * HP + REM, 2], w_qkv[2 * P:C, 0:2 * C]
                     .rearrange("p (a n) -> p a n", a=2)[:, :, c:c + GC]).then_inc(w_ld, 16)


def split_group_weights(eng, wqk, g):
    wqk_raw, wqk_hi, wqk_lo, _, w_ld, w_split, _ = wqk
    eng.wait_ge(w_ld, 16 * 6 * (g + 1))
    hi = wqk_hi[:, :, :, :, 0:HD].rearrange("p k a h d -> p (k a) h d")
    lo = wqk_lo[:, :, :, :, 0:HD].rearrange("p k a h d -> p (k a) h d")
    raw = wqk_raw[:].rearrange("p k a (h d) -> p (k a) h d", d=HD)
    eng.tensor_copy(hi, raw).then_inc(w_split, 1)
    eng.wait_ge(w_split, 4 * g + 1)
    eng.tensor_tensor(lo, raw[:, 0:4], f32(hi[:, 0:4]), ALU.subtract).then_inc(w_split, 1)
    for i, q in enumerate((1, 3)):
        r = slice(q * HP, q * HP + REM)
        eng.wait_ge(w_split, 4 * g + 2 + i)
        eng.tensor_tensor(hi[r, 4:6], raw[r, 4:6], f32(hi[r, 4:6]), ALU.subtract).then_inc(w_split, 1)
    eng.wait_ge(w_split, 4 * g + 4)


class HeadParts:
    Q_LO, Q_HI, K_HI, K_LO = range(4)

    def __init__(self, nc, sb, sem, stack, x_hi, x_lo, wqk):
        self.nc, self.x, self.wqk = nc, (x_hi, x_lo), wqk
        self.parts = sb(stack, "parts", [P, 4, 2, HALF], F32R)
        self.proj_f = sb(stack, "proj_f", [P, 2, HALF])
        self.stacks = [sb(stack, "stack0", [3 * HP, GH, 2, 2, HALF], F32R)]
        self.proj_mm = sem(stack, "proj_mm")
        self.proj_ok = sem(stack, "proj_ok")
        self.parts_ok = sem(stack, "parts_ok")
        self.stack_ld = [sem(stack, f"stack_ld{h}") for h in range(GH)]

    def multiply(self, g, u, bank):
        nc, half, a = self.nc, u // 2, u % 2
        tok = (g // NG) * N + half * HALF
        for i, (xs, xk, ws, wk) in enumerate(PRODUCTS):
            w = self.wqk[1 + ws][:, wk, a].rearrange("p h d -> p (h d)")
            mm = nc.tensor.matmul(bank[:], w, self.x[xs][:, xk, tok:tok + HALF], start=(i == 0), stop=(i == 6))
        mm.then_inc(self.proj_mm, 1)

    def high(self, act, g, u, bank):
        half, a = u // 2, u % 2
        act.wait_ge(self.proj_mm, 4 * g + u + 1)
        if u == 0 and g >= 1:
            for h in range(GH):
                act.wait_ge(self.stack_ld[h], 48 * g)
        self.nc.scalar.activation(self.parts[:, (self.Q_HI, self.K_HI)[a], half], bank[:], ACT.Identity,
                                  bias=self.wqk[3][:, g, a:a + 1])

    def whole(self, act, g, u, bank):
        n, a = 4 * g + u, u % 2
        if n >= 2:
            act.wait_ge(self.parts_ok, n - 1)
        self.nc.scalar.activation(self.proj_f[:, u % 2], bank[:], ACT.Identity, bias=self.wqk[3][:, g, a:a + 1])\
            .then_inc(self.proj_ok, 1)

    def low(self, pool, g, u):
        half, a = u // 2, u % 2
        pool.wait_ge(self.proj_ok, 4 * g + u + 1)
        pool.tensor_tensor(self.parts[:, (self.Q_LO, self.K_LO)[a], half], self.proj_f[:, u % 2],
                           f32(self.parts[:, (self.Q_HI, self.K_HI)[a], half]), ALU.subtract).then_inc(self.parts_ok, 1)

    def load_stack(self, sp, g):
        sp.wait_ge(self.parts_ok, 4 * (g + 1))
        n = HP if g < 2 else HA
        kinds = (slice(self.Q_HI, self.K_HI + 1), slice(self.Q_HI, self.K_LO + 1, 2), slice(self.Q_LO, self.K_HI + 1, 2))
        for h in range(GH):
            for q, kind in enumerate(kinds):
                sp.dma_start(f32(self.stacks[g % 2][q * HP:q * HP + n, h]).rearrange("p a b n -> p a (b n)"),
                             f32(self.parts[h * HP:h * HP + n, kind]).rearrange("p a b n -> p a (b n)"))\
                  .then_inc(self.stack_ld[h], 16)


def setup(nc, sb, pb, sem, xt, cond, w_adaln, b_adaln, w_qkv, b_qkv, x_hi, x_lo, mod_late, ident, half_neg, v_aug,
          wqk, heads, h):
    ctx = ExitStack()
    KC, KN = 96, 3
    wqk_raw, wqk_hi, wqk_lo, bqk, w_ld, w_split, bias_ld = wqk
    with ctx:
        mod_early = sb(ctx, "mod_early", [P, B, 2 * C])
        x_in = sb(ctx, "x_in", [P, NT, C])
        cond_t = sb(ctx, "cond_t", [KC, KN, B])
        sig = sb(ctx, "sig", [KC, KN, B])
        silu = sb(ctx, "silu", [KC, KN, B])
        silu_b = sb(ctx, "silu_b", [KC + 1, KN, B, P])
        wa = sb(ctx, "wa", [KC + 1, KN, MOD])
        bv = sb(ctx, "bv", [P, C])
        wv_raw = sb(ctx, "wv_raw", [P, 3, C])
        wv_hi = sb(ctx, "wv_hi", [P, 3, C], F32R)
        wv_lo = sb(ctx, "wv_lo", [P, 2, C], F32R)
        stats = sb(ctx, "stats", [P, NT, 6])
        mv = sb(ctx, "mv", [P, NT, 2])
        veps = sb(ctx, "veps", [P, NT])
        rstd = sb(ctx, "rstd", [P, NT])
        shift = sb(ctx, "shift", [P, NT])
        xn = sb(ctx, "xn", [P, 2, C])
        xm = sb(ctx, "xm", [P, 2, C])

        mod_ps = [pb(ctx, f"mod_ps{i}", [P, 512]) for i in range(3)]
        t_ps = [pb(ctx, f"t_ps{i}", [P, 3, P]) for i in range(3)]
        v_ps = [pb(ctx, f"v_ps{i}", [P, 512]) for i in range(2)]

        x_ld = [sem(ctx, f"x_ld{i}") for i in range(NT // 4)]
        bias_zero = sem(ctx, "bias_zero")
        cond_ld = sem(ctx, "cond_ld")
        wa_ld = [sem(ctx, f"wa_ld{i}") for i in range(2)]
        bv_ld = sem(ctx, "bv_ld")
        wv_ld = sem(ctx, "wv_ld")
        const_ok = sem(ctx, "const_ok")
        wv_ok = sem(ctx, "wv_ok")
        exp_ok = sem(ctx, "exp_ok")
        silu_step = sem(ctx, "silu_step")
        silu_ok = sem(ctx, "silu_ok")
        mod_mm = sem(ctx, "mod_mm")
        mod_ok = sem(ctx, "mod_ok")
        scale_ok = sem(ctx, "scale_ok")
        stat_ok = sem(ctx, "stat_ok")
        mv_ok = sem(ctx, "mv_ok")
        veps_ok = sem(ctx, "veps_ok")
        rstd_ok = sem(ctx, "rstd_ok")
        shift_ok = sem(ctx, "shift_ok")
        xn_ok = sem(ctx, "xn_ok")
        xm_ok = sem(ctx, "xm_ok")
        h_ok = sem(ctx, "h_ok")
        rem_ok = sem(ctx, "rem_ok")
        t_ok = sem(ctx, "t_ok")
        hi_ok = sem(ctx, "hi_ok")
        lo_ok = sem(ctx, "lo_ok")
        v_mm = sem(ctx, "v_mm")
        v_ok = sem(ctx, "v_ok")

        MOD_BLOCKS = [(b, j) for b in range(B) for j in (1, 0)] + [(b, j) for b in range(B) for j in range(2, 6)]
        EARLY = 2 * C
        UNITS_AT = (9, 11, 13, 15)

        block = ctx.enter_context(nc.Block())

        @block.sync
        def _(sp):
            for b in range(B):
                sp.dma_start(cond_t[:, :, b], cond[b].rearrange("(k p) -> p k", p=KC)).then_inc(cond_ld, 16)
            for part, cols in enumerate((slice(0, EARLY), slice(EARLY, MOD))):
                sp.dma_start(wa[0:KC, :, cols], w_adaln[:, cols].rearrange("(k p) n -> p k n", p=KC))\
                  .then_inc(wa_ld[part], 16)
                sp.dma_start(wa[KC:KC + 1, KN - 1, cols], b_adaln[cols].rearrange("(a n) -> a n", a=1))\
                  .then_inc(wa_ld[part], 16)
                if part == 0:
                    for i in range(0, NT, 4):
                        sp.dma_start(x_in[:, i:i + 4], xt[:, i:i + 4]).then_inc(x_ld[i // 4], 16)
            load_group_weights(sp, w_qkv, wqk_raw, w_ld, 0)
            sp.wait_ge(bias_zero, 2)
            for h in range(GH):
                for a in range(2):
                    for b in range(B):
                        sp.dma_start(bqk[h * HP:h * HP + HD, b * NG:(b + 1) * NG, a],
                                     b_qkv[a * C:(a + 1) * C].rearrange("(g h d) -> h d g", h=GH, d=HD)[h])\
                          .then_inc(bias_ld, 16)
            sp.wait_ge(w_split, 4)
            load_group_weights(sp, w_qkv, wqk_raw, w_ld, 1)
            heads.load_stack(sp, 0)

        @block.gpsimd
        def _(pool):
            nc.gpsimd.memset(ident[:], 0.0).then_inc(const_ok, 1)
            nc.gpsimd.memset(half_neg[:], -0.5).then_inc(const_ok, 1)
            pool.wait_ge(const_ok, 2)
            nc.gpsimd.affine_select(out=ident[:], in_=ident[:], compare_op=ALU.not_equal, fill=1.0, base=0,
                                    pattern=[[-1, P]], channel_multiplier=1).then_inc(const_ok, 1)
            pool.wait_ge(wv_ld, 16 * LOADS)
            split_weights(pool, wv_hi[:], wv_lo[:], wv_raw[:], (wv_ok, 0))
            nc.gpsimd.memset(bqk[:, :, 0], 0.0).then_inc(bias_zero, 1)
            nc.gpsimd.memset(bqk[:, :, 1], 1.0).then_inc(bias_zero, 1)
            nc.gpsimd.memset(f32(wqk_hi[:]), 0.0).then_inc(bias_zero, 1)
            nc.gpsimd.memset(f32(wqk_lo[:]), 0.0).then_inc(bias_zero, 1)
            def roots(b):
                s = slice(b * KT, (b + 1) * KT)
                pool.wait_ge(veps_ok, b + 1)
                nc.gpsimd.tensor_tensor(rstd[:, s], veps[:, s], half_neg[:, s], ALU.pow).then_inc(rstd_ok, 1)

            roots(0)

            def add_shift(t):
                pool.wait_ge(xm_ok, t + 1)
                if t >= 4:
                    pool.wait_ge(t_ok, t - 3)
                nc.gpsimd.tensor_tensor(h[:, t % 4, 0:C], xm[:, t % 2], mod_early[:, t // KT, SH_MSA:SH_MSA + C],
                                        ALU.add).then_inc(h_ok, 1)

            def first_group(r):
                if r == 0:
                    pool.wait_ge(bias_zero, 4)
                    split_group_weights(pool, wqk, 0)
                if r == 5:
                    roots(1)
                if r - 2 in UNITS_AT:
                    heads.low(pool, 0, UNITS_AT.index(r - 2))

            rounds((2, add_shift), extra=first_group)

        @block.scalar
        def _(act):
            load_rows(act, wv_raw, w_qkv[:, 2 * C:3 * C], wv_ld)
            act.dma_start(bv[:], b_qkv[2 * C:3 * C].rearrange("(a n) -> a n", a=1).broadcast_to([P, C]))\
               .then_inc(bv_ld, 16)
            act.wait_ge(cond_ld, 32)
            nc.scalar.activation(sig[:], cond_t[:], ACT.Exp, scale=-1.0).then_inc(exp_ok, 1)

            def normalise(t):
                act.wait_ge(shift_ok, 2 * (t // KT) + 2)
                if t >= 2:
                    act.wait_ge(xm_ok, t - 1)
                nc.scalar.activation(xn[:, t % 2], x_in[:, t], ACT.Identity, scale=rstd[:, t:t + 1],
                                     bias=shift[:, t:t + 1]).then_inc(xn_ok, 1)

            def remainder(t):
                act.wait_ge(h_ok, t + 1)
                rem = h[:, t % 4, 2 * P:C].unsqueeze(1).broadcast_to([P, 3, REM])
                nc.scalar.copy(h[:, t % 4, C:3 * P].rearrange("p (q c) -> p q c", q=3), rem).then_inc(rem_ok, 1)

            def high_part(t):
                act.wait_ge(t_ok, t + 1)
                nc.scalar.copy(x_hi[:, :, t * P:(t + 1) * P], t_ps[t % 3][:]).then_inc(hi_ok, 1)

            def first_group(r):
                if r - 1 in UNITS_AT:
                    u = UNITS_AT.index(r - 1)
                    if u == 0:
                        act.wait_ge(bias_ld, 16 * 16)
                    heads.high(act, 0, u, mod_ps[u % 2])
                    heads.whole(act, 0, u, mod_ps[u % 2])

            rounds((5, high_part), (3, remainder), (0, normalise), extra=first_group)

        @block.vector
        def _(dve):
            nc.vector.memset(silu_b[KC:KC + 1, KN - 1], 1.0).then_inc(silu_ok, 1)
            nc.vector.memset(v_aug[:, :, :, HD:HA], 1.0)
            dve.wait_ge(exp_ok, 1)
            nc.vector.tensor_scalar(sig[:], sig[:], 1.0, None, ALU.add).then_inc(silu_step, 1)
            dve.wait_ge(silu_step, 1)
            nc.vector.reciprocal(sig[:], sig[:]).then_inc(silu_step, 1)
            dve.wait_ge(silu_step, 2)
            nc.vector.tensor_tensor(silu[:], cond_t[:], sig[:], ALU.mult).then_inc(silu_step, 1)
            dve.wait_ge(silu_step, 3)
            for k in range(KN):
                nc.vector.tensor_copy(silu_b[0:KC, k], silu[:, k].unsqueeze(2).broadcast_to([KC, B, P]))\
                  .then_inc(silu_ok, 1)

            def tile_stats(t):
                dve.wait_ge(x_ld[t // 4], 16)
                nc.vector.bn_stats(stats[:, t], x_in[:, t]).then_inc(stat_ok, 1)

            def tile_moments(t):
                dve.wait_ge(stat_ok, t + 1)
                nc.vector.bn_aggr(mv[:, t], stats[:, t]).then_inc(mv_ok, 1)

            def variances(b):
                s = slice(b * KT, (b + 1) * KT)
                dve.wait_ge(mv_ok, (b + 1) * KT)
                nc.vector.tensor_scalar(veps[:, s], mv[:, s, 1], LN_EPS, None, ALU.add).then_inc(veps_ok, 1)

            def shifts(b):
                s = slice(b * KT, (b + 1) * KT)
                dve.wait_ge(rstd_ok, b + 1)
                nc.vector.tensor_tensor(shift[:, s], mv[:, s, 0], rstd[:, s], ALU.mult).then_inc(shift_ok, 1)
                dve.wait_ge(shift_ok, 2 * b + 1)
                nc.vector.tensor_scalar(shift[:, s], shift[:, s], -1.0, None, ALU.mult).then_inc(shift_ok, 1)

            def modulation(i):
                b, j = MOD_BLOCKS[i]
                dve.wait_ge(mod_mm, i + 1)
                dst = mod_early[:, b, j * C:(j + 1) * C] if j < 2 else mod_late[:, b, (j - 2) * C:(j - 1) * C]
                nc.vector.tensor_scalar(dst, mod_ps[i % 3][:, 0:C], 1.0 if j in (1, 4) else 0.0, None, ALU.add)\
                  .then_inc(mod_ok, 1)

            for t in range(KT):
                tile_stats(t)
            for t in range(KT):
                tile_moments(t)
            variances(0)
            for i in range(2 * B):
                modulation(i)
            shifts(0)
            dve.wait_ge(mod_ok, 2 * B)
            dve.wait_ge(bv_ld, 16)

            def scale(t):
                dve.wait_ge(xn_ok, t + 1)
                if t >= 2:
                    dve.wait_ge(h_ok, t - 1)
                nc.vector.tensor_tensor(xm[:, t % 2], xn[:, t % 2], mod_early[:, t // KT, SC_MSA:SC_MSA + C],
                                        ALU.mult).then_inc(xm_ok, 1)

            def low_parts(t):
                s = slice(t * P, (t + 1) * P)
                dve.wait_ge(hi_ok, t + 1)
                nc.vector.tensor_tensor(x_lo[:, :, s], t_ps[t % 3][:, 0:2], f32(x_hi[:, 0:2, s]), ALU.subtract)
                nc.vector.tensor_tensor(x_hi[2 * HP:P, 2, s], t_ps[t % 3][2 * HP:P, 2], f32(x_hi[2 * HP:P, 2, s]),
                                        ALU.subtract).then_inc(lo_ok, 1)

            def values(t):
                dve.wait_ge(v_mm, t + 1)
                nc.vector.tensor_tensor(v_aug[:, t, :, 0:HD], v_ps[t % 2][:, 0:C].rearrange("p (h d) -> p h d", d=HD),
                                        bv[:].rearrange("p (h d) -> p h d", d=HD), ALU.add).then_inc(v_ok, 1)

            def beside(r):
                if 2 * B + r < len(MOD_BLOCKS):
                    modulation(2 * B + r)
                for i in (2 * r, 2 * r + 1):
                    if i < KT:
                        tile_stats(KT + i)
                    if 0 <= i - 2 < KT:
                        tile_moments(KT + i - 2)
                if r == 5:
                    variances(1)
                if r == 6:
                    shifts(1)

            rounds((12, values), (6, low_parts), (1, scale), extra=beside)

        @block.tensor
        def _(pe):
            def modulation(i):
                b, j = MOD_BLOCKS[i]
                if i in (0, 2 * B):
                    pe.wait_ge(wa_ld[i // (2 * B)], 32)
                if i >= 3:
                    pe.wait_ge(mod_ok, i - 2)
                for k in range(KN):
                    rows = slice(0, KC + (k == KN - 1))
                    mm = nc.tensor.matmul(mod_ps[i % 3][:, 0:C], silu_b[rows, k, b], wa[rows, k, j * C:(j + 1) * C],
                                          start=(k == 0), stop=(k == KN - 1))
                mm.then_inc(mod_mm, 1)

            pe.wait_ge(silu_ok, KN + 1)
            for i in range(2 * B):
                modulation(i)
            pe.wait_ge(const_ok, 3)
            pe.wait_ge(wv_ok, 4)

            def transposes(t):
                pe.wait_ge(rem_ok, t + 1)
                if t >= 3:
                    pe.wait_ge(lo_ok, t - 2)
                for k in range(3):
                    mm = nc.tensor.transpose(t_ps[t % 3][:, k], h[:, t % 4, k * P:(k + 1) * P], ident[:])
                mm.then_inc(t_ok, 1)

            def values(t):
                pe.wait_ge(lo_ok, t + 1)
                if t >= 2:
                    pe.wait_ge(v_ok, t - 1)
                for i, (xs, xk, ws, wk) in enumerate(PRODUCTS):
                    mm = nc.tensor.matmul(v_ps[t % 2][:, 0:C], (x_hi, x_lo)[xs][:, xk, t * P:(t + 1) * P],
                                          (wv_hi, wv_lo)[ws][:, wk], start=(i == 0), stop=(i == 6))
                mm.then_inc(v_mm, 1)

            def beside(r):
                if 2 * B + r < len(MOD_BLOCKS):
                    modulation(2 * B + r)
                if r in UNITS_AT:
                    u = UNITS_AT.index(r)
                    if u == 0:
                        pe.wait_ge(w_split, 4)
                        pe.wait_ge(mod_ok, len(MOD_BLOCKS))
                    if u >= 2:
                        pe.wait_ge(heads.proj_ok, u - 1)
                    pe.wait_ge(lo_ok, QT * (u // 2 + 1))
                    heads.multiply(0, u, mod_ps[u % 2])

            rounds((11, values), (4, transposes), extra=beside)


STEPS = 2 * KT
MAXIMA = GH * QT
LATE = 4
WIDE = 3
AHEAD = 24


def plan(g):
    tiles, proj, rows, outs = ([[] for _ in range(STEPS)] for _ in range(4))

    def spread(group, first_tile, first_step, counts):
        for st, n in enumerate(counts, first_step):
            tiles[st] += [(group, first_tile + i) for i in range(n)]
            first_tile += n

    if g == 0:
        spread(0, AHEAD, 0, (2, 2, 2, 2))
        spread(1, 0, 5, (3, 3, 3, 3, 3, 3, 2, 2, 2, 2, 2))
        rows[4], rows[10], outs[11] = [(0, 1)], [(1, 0)], [(0, 0)]
        for u, st in enumerate((1, 3, 6, 8)):
            proj[st] = [(2, u)]
    else:
        outs[1], outs[11], rows[2] = [(g - 1, 1)], [(g, 0)], [(g, 1)]
        spread(g, 2 * MAXIMA - LATE, 0, (2, 2))
        if g + 1 < GG:
            spread(g + 1, 0, 2, (2, 2, 2, 2, 2, 2, 2, 2, 2, 2, 2, 2, 2, 2))
            rows[10] = [(g + 1, 0)]
        if g + 2 < GG:
            for u, st in enumerate((4, 6, 8, 13)):
                proj[st] = [(g + 2, u)]
    return tiles, proj, rows, outs


def attention(nc, sb, pb, sem, w_qkv, ident, v_aug, wqk, heads, o_dram, late, outputs_in):
    ctx = ExitStack()
    with ctx:
        wqk_raw, _, _, _, w_ld, w_split, _ = wqk
        proj_mm, proj_ok, stack_ld = heads.proj_mm, heads.proj_ok, heads.stack_ld
        rows_dram = nc.dram_tensor("rows_scratch", (GG, 2, 2, GH * QT, P), F32, kind="Internal").ap()
        heads.stacks.append(sb(ctx, "stack1", [3 * HP, GH, 2, 2, HALF], F32R))
        stack = heads.stacks
        negmax = sb(ctx, "negmax", [P, 2, 2, GH * QT])
        rows_hi = sb(ctx, "rows_hi", [GH * QT, 2, P], F32R)
        rows_lo = sb(ctx, "rows_lo", [GH * QT, 2, P], F32R)
        probs = sb(ctx, "probs", [P, 2, GH, HALF])
        o_sb = sb(ctx, "o_sb", [P, 2, HALF])
        rsum = sb(ctx, "rsum", [P, 2, QT * GH])
        o_norm = sb(ctx, "o_norm", [P, 2, QT * GH, HD])

        s_ps = [pb(ctx, f"s_ps{i}", [P, HALF]) for i in range(2)]
        m_ps = [pb(ctx, f"m_ps{i}", [P, N]) for i in range(2)]
        o_ps = pb(ctx, "o_ps", [P, HALF])
        misc = pb(ctx, "misc", [P, HALF])

        zero_ok = sem(ctx, "zero_ok")
        max_mm = sem(ctx, "max_mm")
        max_free = sem(ctx, "max_free")
        rows_mm = sem(ctx, "rows_mm")
        rows_step = sem(ctx, "rows_step")
        rows_ld = [sem(ctx, f"rows_ld{i}") for i in range(2)]
        rows_st = [sem(ctx, f"rows_st{i}") for i in range(2)]
        score_mm = sem(ctx, "score_mm")
        exp_free = sem(ctx, "exp_free")
        pv_free = sem(ctx, "pv_free")
        o_evac = sem(ctx, "o_evac")
        out_mm = sem(ctx, "out_mm")
        rsum_ok = sem(ctx, "rsum_ok")
        out_ok = sem(ctx, "out_ok")
        out_st = outputs_in.stored

        def four_banks(g, st):
            return g == GG - 1 and st >= WIDE

        def score_bank(g, st, h):
            return m_ps[h - 2][:, 0:HALF] if four_banks(g, st) and h >= 2 else s_ps[h % 2][:]

        block = ctx.enter_context(nc.Block())

        def max_tile(m):
            return m // MAXIMA, (m // QT) % GH, m % QT

        @block.sync
        def _(sp):
            def load_w(g):
                if g < GG:
                    sp.wait_ge(w_split, 4 * g)
                    load_group_weights(sp, w_qkv, wqk_raw, w_ld, g)

            def load_stack(g):
                if g >= 2:
                    sp.wait_ge(score_mm, 64 * (g - 1))
                heads.load_stack(sp, g)

            def load_rows_of_max(g, half):
                n, s = 2 * g + half, g % 2
                sp.wait_ge(rows_step, 2 * (n + 1))
                for part, rows in enumerate((rows_hi, rows_lo)):
                    sp.dma_start(rows_dram[g, half, part], f32(rows[:, half])).then_inc(rows_st[half], 16)
                sp.wait_ge(rows_st[half], 32 * (g + 1))
                for part, q in enumerate((0, 2)):
                    sp.dma_start(f32(stack[s][q * HP + HD:q * HP + HA, :, 0, half]),
                                 rows_dram[g, half, part].rearrange("(a h t) n -> a h (t n)", a=1, h=GH))\
                      .then_inc(rows_ld[half], 16)

            def store(g, half):
                n = 2 * g + half
                sp.wait_ge(out_ok, n + 1)
                c = (g % NG) * GC
                sp.dma_start(o_dram[g // NG, half, :, :, c:c + GC],
                             o_norm[:, half].rearrange("p (t h) d -> p t (h d)", h=GH)).then_inc(out_st[half], 16)

            load_w(2)
            load_rows_of_max(0, 0)
            for g in range(GG):
                if g + 1 < GG:
                    load_stack(g + 1)
                if g == 0:
                    load_rows_of_max(0, 1)
                else:
                    load_rows_of_max(g, 1)
                    store(g - 1, 1)
                if g == 2:
                    late.load_biases(sp)
                if g == GG - 2:
                    for h in range(GH):
                        sp.wait_ge(stack_ld[h], 48 * GG)
                    late.load_projections(sp)
                    for i in (0, 1):
                        late.load_piece(sp, 0, i)
                if g == GG - 1:
                    for i in (4, 5):
                        late.load_piece(sp, 0, i)
                if g + 1 < GG:
                    load_rows_of_max(g + 1, 0)
                store(g, 0)
                if g == GG - 2:
                    for i in (2, 3):
                        late.load_piece(sp, 0, i)
                load_w(g + 3)
            for half in range(2):
                sp.wait_ge(out_st[half], 16 * (GG - 1))
            for t in range(outputs_in.BUFS):
                outputs_in.load(sp, t)
            store(GG - 1, 1)

        @block.gpsimd
        def _(pool):
            def split_w(g):
                if g < GG:
                    pool.wait_ge(proj_mm, 4 * g)
                    split_group_weights(pool, wqk, g)

            split_w(1)
            late.clear_bias_rows(nc.gpsimd)
            for u in range(4):
                heads.low(pool, 1, u)
            split_w(2)
            for g in range(GG):
                for st in range(STEPS):
                    for unit in plan(g)[1][st]:
                        heads.low(pool, *unit)
                        if unit[1] == 3:
                            split_w(unit[0] + 1)
            pool.wait_ge(proj_mm, 4 * GG)
            late.split_projections(nc.gpsimd)
            for i in range(late.PIECES):
                late.split_piece(pool, 0, i)

        @block.scalar
        def _(act):
            act.sem_inc(exp_free, 2)

            def out_of_bank(g, half):
                n = 2 * g + half
                act.wait_ge(pv_free, 2 + 16 * g + KT * (half + 1))
                if n >= 2:
                    act.wait_ge(out_mm, n - 1)
                nc.scalar.copy(o_sb[:, half], o_ps[:]).then_inc(o_evac, 1)

            for u in range(4):
                heads.high(act, 1, u, misc)
                heads.whole(act, 1, u, misc)
            for g in range(GG):
                for st in range(STEPS):
                    units = plan(g)[1][st - 1] if st >= 1 else []
                    for unit in units:
                        heads.high(act, *unit, misc)
                    for h in range(GH):
                        n = 64 * g + 4 * st + h
                        if h == 1:
                            for unit in units:
                                heads.whole(act, *unit, misc)
                        if h == 2:
                            if st == 0 and g >= 1:
                                out_of_bank(g - 1, 1)
                            if st == KT:
                                out_of_bank(g, 0)
                        act.wait_ge(score_mm, n + 1)
                        if h == 0:
                            act.wait_ge(pv_free, 16 * g + st + 1)
                        nc.scalar.activation(probs[:, st % 2, h], score_bank(g, st, h), ACT.Exp, scale=SCALE)\
                          .then_inc(exp_free, 1)
            out_of_bank(GG - 1, 1)

        @block.vector
        def _(dve):
            nc.vector.memset(o_ps[:], 0.0).then_inc(zero_ok, 1)
            dve.sem_inc(max_free, 2)

            def maximum(g, m):
                half = m // 16
                n = 32 * g + m
                dve.wait_ge(max_mm, n + 1)
                nc.vector.tensor_reduce(negmax[:, half, g % 2, m % 16:m % 16 + 1],
                                        m_ps[m % 2][:], AX.X, ALU.max, negate=True).then_inc(max_free, 1)

            def rows(g, half):
                n = 2 * g + half
                dve.wait_ge(rows_mm, n + 1)
                if g >= 1:
                    dve.wait_ge(rows_ld[half], 32 * g)
                nc.vector.tensor_copy(rows_hi[:, half], misc[0:GH * QT, 0:P]).then_inc(rows_step, 1)
                dve.wait_ge(rows_step, 2 * n + 1)
                nc.vector.tensor_tensor(rows_lo[:, half], misc[0:GH * QT, 0:P], f32(rows_hi[:, half]),
                                        ALU.subtract).then_inc(rows_step, 1)

            def normalise(g, half):
                n = 2 * g + half
                o = misc[:].rearrange("p (t c) -> p t c", c=HP)
                dve.wait_ge(out_mm, n + 1)
                nc.vector.reciprocal(rsum[:, half], o[:, :, HD]).then_inc(rsum_ok, 1)
                dve.wait_ge(rsum_ok, n + 1)
                if g >= 1:
                    dve.wait_ge(out_st[half], 16 * g)
                nc.vector.tensor_tensor(o_norm[:, half], o[:, :, 0:HD],
                                        rsum[:, half].unsqueeze(2).broadcast_to([P, QT * GH, HD]),
                                        ALU.mult).then_inc(out_ok, 1)

            for m in range(MAXIMA):
                maximum(0, m)
            rows(0, 0)
            for m in range(MAXIMA, AHEAD):
                maximum(0, m)
            for g in range(GG):
                for tiles, _, row_turns, out_turns in zip(*plan(g)):
                    for tile in tiles:
                        maximum(*tile)
                    for turn in row_turns:
                        rows(*turn)
                    for turn in out_turns:
                        normalise(*turn)
            normalise(GG - 1, 1)

        @block.tensor
        def _(pe):
            pe.sem_inc(pv_free, 2)

            last_use = [None]

            def take_misc(next_use):
                if last_use[0] is not None:
                    s, v = last_use[0]
                    pe.wait_ge(s, v)
                last_use[0] = next_use

            def project(g, u):
                take_misc((proj_ok, 4 * g + u + 1))
                if u == 0:
                    pe.wait_ge(w_split, 4 * (g + 1))
                heads.multiply(g, u, misc)

            def maximum(g, m):
                half, h, qt = max_tile(m)
                n, s = 32 * g + m, g % 2
                if half == 0 and qt == 0:
                    pe.wait_ge(stack_ld[h], 48 * (g + 1))
                pe.wait_ge(max_free, n + 1)
                for kh in range(2):
                    mm = nc.tensor.matmul(m_ps[m % 2][:, kh * HALF:(kh + 1) * HALF],
                                          stack[s][:, h, 0, half, qt * P:(qt + 1) * P], stack[s][:, h, 1, kh],
                                          start=True, stop=True)
                mm.then_inc(max_mm, 1)

            def rows(g, half):
                n = 2 * g + half
                take_misc((rows_step, 2 * (n + 1)))
                pe.wait_ge(max_free, 2 + 32 * g + 16 * (half + 1))
                nc.tensor.transpose(misc[0:GH * QT, 0:P], negmax[:, half, g % 2], ident[:]).then_inc(rows_mm, 1)

            def outputs(g, half):
                n = 2 * g + half
                take_misc((out_ok, n + 1))
                pe.wait_ge(o_evac, n + 1)
                for t in range(QT):
                    mm = nc.tensor.transpose(misc[:, t * P:(t + 1) * P], o_sb[:, half, t * P:(t + 1) * P], ident[:])
                mm.then_inc(out_mm, 1)

            def scores(g, st, heads):
                half, kt, s = st // KT, st % KT, g % 2
                if kt == 0:
                    pe.wait_ge(rows_ld[half], 32 * (g + 1))
                for h in heads:
                    n = 64 * g + 4 * st + h
                    if not four_banks(g, st) or (st == WIDE and h < 2):
                        pe.wait_ge(exp_free, n + 1)
                    elif st == WIDE:
                        pe.wait_ge(max_free, 2 + 32 * GG)
                    else:
                        pe.wait_ge(exp_free, n - 1)
                    nc.tensor.matmul(score_bank(g, st, h), stack[s][:, h, 1, kt // QT, (kt % QT) * P:(kt % QT + 1) * P],
                                     stack[s][:, h, 0, half], start=True, stop=True).then_inc(score_mm, 1)

            def values(g, st):
                half, kt = st // KT, st % KT
                pe.wait_ge(exp_free, 2 + 64 * g + 4 * (st + 1))
                if kt == 0:
                    n = 2 * g + half
                    if n == 0:
                        pe.wait_ge(zero_ok, 1)
                    else:
                        pe.wait_ge(o_evac, n)
                tile = (g // NG) * KT + kt
                for h in range(GH):
                    mm = nc.tensor.matmul(o_ps[h * HP:h * HP + HA], v_aug[:, tile, (g % NG) * GH + h],
                                          probs[:, st % 2, h], start=(kt == 0), stop=(kt == KT - 1))
                mm.then_inc(pv_free, 1)

            for m in range(MAXIMA):
                maximum(0, m)
                if m % 4 == 3:
                    project(1, m // 4)
            rows(0, 0)
            for m in range(MAXIMA, AHEAD):
                maximum(0, m)
            for g in range(GG):
                for st, (tiles, units, row_turns, out_turns) in enumerate(zip(*plan(g))):
                    if four_banks(g, st):
                        scores(g, st, range(GH))
                        values(g, st - 1)
                        for turn in out_turns:
                            outputs(*turn)
                        continue
                    scores(g, st, (0,))
                    for tile in tiles[:1]:
                        maximum(*tile)
                    scores(g, st, (1,))
                    if st >= 1:
                        values(g, st - 1)
                    elif g >= 1:
                        values(g - 1, STEPS - 1)
                    scores(g, st, (2,))
                    for tile in tiles[1:2]:
                        maximum(*tile)
                    scores(g, st, (3,))
                    for tile in tiles[2:]:
                        maximum(*tile)
                    for turn in row_turns:
                        rows(*turn)
                    for turn in out_turns:
                        outputs(*turn)
                    for unit in units:
                        project(*unit)
            values(GG - 1, STEPS - 1)
            outputs(GG - 1, 1)


def experts(nc, sb, pb, sem, xt, ot, b2, mod_late, ident, half_neg, late, outputs_in):
    ctx = ExitStack()
    x1_dram = nc.dram_tensor("x1_scratch", (P, NT, C), F32, kind="Internal").ap()
    with ctx:
        late.w_raw = sb(ctx, "w_raw", [P, 2, 3, late.PIECE])
        x_hi = sb(ctx, "x2_hi", [P, 3, T], F32R)
        x_lo = sb(ctx, "x2_lo", [P, 2, T], F32R)
        b2b = sb(ctx, "b2b", [P, NE, C])
        gate_ps = pb(ctx, "gate_ps", [P, NT, NE])
        b2_ld = sem(ctx, "b2_ld")

        between(nc, sb, pb, sem, xt, outputs_in, b2, x_hi, x_lo, mod_late, ident, half_neg, x1_dram, b2b,
                b2_ld, gate_ps, late)
        late.add_place(sb(ctx, "place1", [P, EXPERT_WORDS], F32R))
        mixture(nc, sb, pb, sem, ot, x_hi, x_lo, mod_late, x1_dram, b2b, b2_ld, gate_ps, late,
                outputs_in.tiles)


def between(nc, sb, pb, sem, xt, outputs_in, b2, x_hi, x_lo, mod_late, ident, half_neg, x1_dram, b2b,
            b2_ld, gate_ps, late):
    ctx = ExitStack()
    DEEP = 6
    with ctx:
        o_in = outputs_in.tiles
        x_in = sb(ctx, "xr", [P, DEEP, C])
        ot_hi = sb(ctx, "ot_hi", [P, 3, 3, P], F32R)
        ot_lo = sb(ctx, "ot_lo", [P, 3, 2, P], F32R)
        gy = sb(ctx, "gy", [P, 2, C])
        x1 = sb(ctx, "x1", [P, DEEP, C])
        stats = sb(ctx, "stats2", [P, 2, 6])
        mv = sb(ctx, "mv2", [P, 4, 2])
        veps = sb(ctx, "veps2", [P, NT])
        rstd = sb(ctx, "rstd2", [P, NT])
        xc = sb(ctx, "xc", [P, 3, C])
        xs = sb(ctx, "xs", [P, 3, C])
        h = sb(ctx, "h2", [P, 4, 3 * P])

        to_ps = [pb(ctx, f"to_ps{i}", [P, 3, P]) for i in range(3)]
        y_ps = [pb(ctx, f"y_ps{i}", [P, 512]) for i in range(2)]
        tx_ps = [pb(ctx, f"tx_ps{i}", [P, 3, P]) for i in range(2)]

        xr_ld = [sem(ctx, f"xr_ld{i}") for i in range(DEEP)]
        x1_st = [sem(ctx, f"x1_st{i}") for i in range(DEEP)]
        orem_ok = sem(ctx, "orem_ok")
        to_mm = sem(ctx, "to_mm")
        ohi_ok = sem(ctx, "ohi_ok")
        olo_ok = sem(ctx, "olo_ok")
        y_mm = sem(ctx, "y_mm")
        gy_ok = sem(ctx, "gy_ok")
        x1_ok = sem(ctx, "x1_ok")
        stat_ok = sem(ctx, "stat_ok2")
        mv_ok = sem(ctx, "mv_ok2")
        veps_ok = sem(ctx, "veps_ok2")
        rstd_ok = sem(ctx, "rstd_ok2")
        xc_ok = sem(ctx, "xc_ok")
        xs_ok = sem(ctx, "xs_ok")
        h_ok = sem(ctx, "h_ok2")
        rem_ok = sem(ctx, "rem_ok2")
        tx_mm = sem(ctx, "tx_mm")
        hi_ok = sem(ctx, "hi_ok2")
        lo_ok = sem(ctx, "lo_ok2")
        gate_mm = sem(ctx, "gate_mm")

        block = ctx.enter_context(nc.Block())

        @block.sync
        def _(sp):
            def load(t):
                if t >= 4:
                    sp.wait_ge(to_mm, t - 3)
                    if t == KT:
                        for half in range(2):
                            sp.wait_ge(outputs_in.stored[half], 16 * GG)
                    outputs_in.load(sp, t)

            def load_x(t):
                if t >= DEEP:
                    sp.wait_ge(x1_ok, t - DEEP + 1)
                sp.dma_start(x_in[:, t % DEEP], xt[:, t]).then_inc(xr_ld[t % DEEP], 16)

            def store(t):
                sp.wait_ge(x1_ok, t + 1)
                sp.dma_start(x1_dram[:, t], x1[:, t % DEEP]).then_inc(x1_st[t % DEEP], 16)

            rounds((9, store), (2, load_x), (-2, load))
            sp.dma_start(b2b[:], b2.rearrange("(a e) n -> a e n", a=1).broadcast_to([P, NE, C])).then_inc(b2_ld, 16)
            for i in range(DEEP):
                sp.wait_ge(x1_st[i], 16 * len(range(i, NT, DEEP)))

        @block.gpsimd
        def _(pool):
            def add_x(t):
                pool.wait_ge(gy_ok, t + 1)
                pool.wait_ge(xr_ld[t % DEEP], 16 * (t // DEEP + 1))
                if t >= DEEP:
                    pool.wait_ge(x1_st[t % DEEP], 16 * (t // DEEP))
                    pool.wait_ge(xc_ok, t - DEEP + 1)
                nc.gpsimd.tensor_tensor(x1[:, t % DEEP], x_in[:, t % DEEP], gy[:, t % 2], ALU.add).then_inc(x1_ok, 1)

            def root(t):
                pool.wait_ge(veps_ok, t + 1)
                nc.gpsimd.tensor_tensor(rstd[:, t:t + 1], veps[:, t:t + 1], half_neg[:, t:t + 1], ALU.pow)\
                  .then_inc(rstd_ok, 1)

            def add_shift(t):
                pool.wait_ge(xs_ok, t + 1)
                if t >= 4:
                    pool.wait_ge(tx_mm, t - 3)
                nc.gpsimd.tensor_tensor(h[:, t % 4, 0:C], xs[:, t % 3], mod_late[:, t // KT, SH_MLP:SH_MLP + C],
                                        ALU.add).then_inc(h_ok, 1)

            rounds((12, add_shift), (10, root), (6, add_x))

        @block.scalar
        def _(act):
            def remainder(src, buf):
                rem = src[:, buf, 2 * P:C].unsqueeze(1).broadcast_to([P, 3, REM])
                return nc.scalar.copy(src[:, buf, C:3 * P].rearrange("p (q c) -> p q c", q=3), rem)

            def attn_remainder(t):
                outputs_in.wait(act, t)
                remainder(o_in, t % 4).then_inc(orem_ok, 1)

            def attn_high(t):
                act.wait_ge(to_mm, t + 1)
                if t >= 3:
                    act.wait_ge(y_mm, t - 2)
                nc.scalar.copy(ot_hi[:, t % 3], to_ps[t % 3][:]).then_inc(ohi_ok, 1)

            def scale(t):
                act.wait_ge(xc_ok, t + 1)
                act.wait_ge(rstd_ok, t + 1)
                if t >= 3:
                    act.wait_ge(h_ok, t - 2)
                nc.scalar.activation(xs[:, t % 3], xc[:, t % 3], ACT.Copy, scale=rstd[:, t:t + 1]).then_inc(xs_ok, 1)

            def x_remainder(t):
                act.wait_ge(h_ok, t + 1)
                remainder(h, t % 4).then_inc(rem_ok, 1)

            def x_high(t):
                act.wait_ge(tx_mm, t + 1)
                nc.scalar.copy(x_hi[:, :, t * P:(t + 1) * P], tx_ps[t % 2][:]).then_inc(hi_ok, 1)

            rounds((15, x_high), (13, x_remainder), (11, scale), (2, attn_high), (0, attn_remainder))

        @block.vector
        def _(dve):
            def attn_low(t):
                dve.wait_ge(ohi_ok, t + 1)
                nc.vector.tensor_tensor(ot_lo[:, t % 3], to_ps[t % 3][:, 0:2], f32(ot_hi[:, t % 3, 0:2]), ALU.subtract)
                nc.vector.tensor_tensor(ot_hi[2 * HP:P, t % 3, 2], to_ps[t % 3][2 * HP:P, 2],
                                        f32(ot_hi[2 * HP:P, t % 3, 2]), ALU.subtract).then_inc(olo_ok, 1)

            def gate(t):
                dve.wait_ge(y_mm, t + 1)
                if t >= 2:
                    dve.wait_ge(x1_ok, t - 1)
                nc.vector.tensor_tensor(gy[:, t % 2], y_ps[t % 2][:, 0:C], mod_late[:, t // KT, G_MSA:G_MSA + C],
                                        ALU.mult).then_inc(gy_ok, 1)

            def moments(t):
                dve.wait_ge(x1_ok, t + 1)
                nc.vector.bn_stats(stats[:, t % 2], x1[:, t % DEEP]).then_inc(stat_ok, 1)

            def mean_and_variance(t):
                dve.wait_ge(stat_ok, t + 1)
                nc.vector.bn_aggr(mv[:, t % 4], stats[:, t % 2]).then_inc(mv_ok, 1)

            def variance_and_centre(t):
                dve.wait_ge(mv_ok, t + 1)
                if t >= 3:
                    dve.wait_ge(xs_ok, t - 2)
                nc.vector.tensor_scalar(veps[:, t:t + 1], mv[:, t % 4, 1:2], LN_EPS, None, ALU.add)\
                  .then_inc(veps_ok, 1)
                nc.vector.scalar_tensor_tensor(out=xc[:, t % 3], in0=x1[:, t % DEEP], scalar=mv[:, t % 4, 0:1],
                                               in1=mod_late[:, t // KT, SC_MLP:SC_MLP + C],
                                               op0=ALU.subtract, op1=ALU.mult).then_inc(xc_ok, 1)

            def x_low(t):
                s = slice(t * P, (t + 1) * P)
                dve.wait_ge(hi_ok, t + 1)
                nc.vector.tensor_tensor(x_lo[:, :, s], tx_ps[t % 2][:, 0:2], f32(x_hi[:, 0:2, s]), ALU.subtract)
                nc.vector.tensor_tensor(x_hi[2 * HP:P, 2, s], tx_ps[t % 2][2 * HP:P, 2], f32(x_hi[2 * HP:P, 2, s]),
                                        ALU.subtract).then_inc(lo_ok, 1)

            rounds((16, x_low), (9, variance_and_centre), (8, mean_and_variance), (7, moments),
                   (5, gate), (3, attn_low))

        @block.tensor
        def _(pe):
            def attn_transposes(t):
                pe.wait_ge(orem_ok, t + 1)
                if t >= 3:
                    pe.wait_ge(olo_ok, t - 2)
                for k in range(3):
                    mm = nc.tensor.transpose(to_ps[t % 3][:, k], o_in[:, t % 4, k * P:(k + 1) * P], ident[:])
                mm.then_inc(to_mm, 1)

            def project(t):
                pe.wait_ge(olo_ok, t + 1)
                if t == 0:
                    pe.wait_ge(late.wp_ok, 4)
                    pe.wait_ge(late.bp_ok, 4)
                if t >= 2:
                    pe.wait_ge(gy_ok, t - 1)
                nc.tensor.matmul(y_ps[t % 2][:, 0:C], late.ones[:], late.bp[:], start=True, stop=False)
                for i, (xs, xk, ws, wk) in enumerate(PRODUCTS):
                    mm = nc.tensor.matmul(y_ps[t % 2][:, 0:C], (ot_hi, ot_lo)[xs][:, t % 3, xk],
                                          (late.wp_hi, late.wp_lo)[ws][:, wk],
                                          start=False, stop=(i == 6))
                mm.then_inc(y_mm, 1)

            def x_transposes(t):
                pe.wait_ge(rem_ok, t + 1)
                if t >= 2:
                    pe.wait_ge(lo_ok, t - 1)
                for k in range(3):
                    mm = nc.tensor.transpose(tx_ps[t % 2][:, k], h[:, t % 4, k * P:(k + 1) * P], ident[:])
                mm.then_inc(tx_mm, 1)

            def gate(t):
                pe.wait_ge(lo_ok, t + 1)
                if t == 0:
                    pe.wait_ge(late.wg_ok, 4)
                for i, (xs, xk, ws, wk) in enumerate(PRODUCTS):
                    mm = nc.tensor.matmul(gate_ps[:, t], (x_hi, x_lo)[xs][:, xk, t * P:(t + 1) * P],
                                          (late.wg_hi, late.wg_lo)[ws][:, wk], start=(i == 0), stop=(i == 6))
                mm.then_inc(gate_mm, 1)

            rounds((17, gate), (14, x_transposes), (4, project), (1, attn_transposes))


def mixture(nc, sb, pb, sem, ot, x_hi, x_lo, mod_late, x1_dram, b2b, b2_ld, gate_ps, late, rows):
    ctx = ExitStack()
    RING = 3
    LAG = 2
    assert HT % RING == 0
    with ctx:
        hid = sb(ctx, "hid", [P, RING, CH])
        hid_hi = sb(ctx, "hid_hi", [P, RING, CH], F32R)
        hid_lo = sb(ctx, "hid_lo", [P, RING, CH], F32R)
        acc = sb(ctx, "acc", [P, NT, C])
        part = sb(ctx, "part", [P, TCH, C])
        OUT = 4
        spare = late.w_raw[:].rearrange("p i k n -> p (i k n)")
        x1 = spare[:, 0:OUT * C].rearrange("p (b n) -> p b n", b=OUT)
        res = spare[:, OUT * C:2 * OUT * C].rearrange("p (b n) -> p b n", b=OUT)
        words = rows[:].rearrange("p b n -> p (b n)")
        gated = words[:, 0:2 * C].rearrange("p (b n) -> p b n", b=2)
        beats = words[:, 2 * C:2 * C + NT * NE * NE].rearrange("p (t j i) -> p t j i", j=NE, i=NE)
        logits = sb(ctx, "logits", [P, NT, NE])
        rank = sb(ctx, "rank", [P, NT, NE])
        top = sb(ctx, "top", [P, NT])
        shifted = sb(ctx, "shifted", [P, NT, NE])
        weight = sb(ctx, "weight", [P, NT, NE])
        kept = sb(ctx, "kept", [P, NT, NE])
        wsum = sb(ctx, "wsum", [P, NT])
        winv = sb(ctx, "winv", [P, NT])
        cw = sb(ctx, "cw", [P, NT, NE])
        h_ps = [pb(ctx, f"h_ps{i}", [P, CH]) for i in range(RING)]
        y_ps = [pb(ctx, f"e_ps{i}", [P, 512]) for i in range(TCH)]

        logits_ok = sem(ctx, "logits_ok")
        top_ok = sem(ctx, "top_ok")
        shifted_ok = sem(ctx, "shifted_ok")
        gexp_ok = sem(ctx, "gexp_ok")
        beats_ok = sem(ctx, "beats_ok")
        rank_ok = sem(ctx, "rank_ok")
        kept_ok = sem(ctx, "kept_ok")
        wsum_ok = sem(ctx, "wsum_ok")
        winv_ok = sem(ctx, "winv_ok")
        cw_ok = sem(ctx, "cw_ok")
        up_mm = sem(ctx, "up_mm")
        gelu_ok = sem(ctx, "gelu_ok")
        hi_ok = sem(ctx, "hid_hi_ok")
        split_ok = sem(ctx, "split_ok")
        down_mm = sem(ctx, "down_mm")
        part_ok = sem(ctx, "part_ok")
        bias_ok = sem(ctx, "bias_ok")
        add_ok = sem(ctx, "add_ok")
        x1_ld = [sem(ctx, f"x1_ld{i}") for i in range(OUT)]
        gated_ok = sem(ctx, "gated_ok")
        res_ok = sem(ctx, "res_ok")
        out_st = [sem(ctx, f"y_st{i}") for i in range(OUT)]

        def chunks(eng, e, body):
            if e < NE - 1:
                with eng.Fori(0, NCH) as c:
                    body(c, c + NCH * e)
            else:
                for c in range(NCH):
                    body(c, c + NCH * e)

        block = ctx.enter_context(nc.Block())

        @block.sync
        def _(sp):
            for e in range(1, NE):
                for i in range(late.PIECES):
                    late.load_piece(sp, e, i)

            def load_x1(t):
                sp.dma_start(x1[:, t % OUT], x1_dram[:, t]).then_inc(x1_ld[t % OUT], 16)

            sp.wait_ge(late.piece_ok, late.PIECES * NE)
            for t in range(OUT - 1):
                load_x1(t)
            for t in range(NT):
                sp.wait_ge(res_ok, t + 1)
                sp.dma_start(ot[:, t], res[:, t % OUT]).then_inc(out_st[t % OUT], 16)
                if t + OUT - 1 < NT:
                    load_x1(t + OUT - 1)
            for i in range(OUT):
                sp.wait_ge(out_st[i], 16 * NT // OUT)

        @block.gpsimd
        def _(pool):
            pool.sem_inc(add_ok, TCH)
            for e in range(NE):
                for c in range(NCH):
                    if e + 1 < NE and c < 3:
                        if c == 0 and e >= 1:
                            pool.wait_ge(down_mm, RING + HT * NCH * e)
                        for i in (2 * c, 2 * c + 1):
                            late.split_piece(pool, e + 1, i)
                    for t in range(TCH):
                        tile = TCH * c + t
                        n = NT * e + tile
                        pool.wait_ge(bias_ok, n + 1)
                        pool.wait_ge(part_ok, TCH + n + 1)
                        nc.gpsimd.tensor_tensor(acc[:, tile], acc[:, tile], part[:, t], ALU.add).then_inc(add_ok, 1)

        @block.scalar
        def _(act):
            act.sem_inc(gelu_ok, RING)
            act.sem_inc(part_ok, TCH)
            act.wait_ge(shifted_ok, 1)
            nc.scalar.activation(weight[:], shifted[:], ACT.Exp).then_inc(gexp_ok, 1)
            act.wait_ge(late.b1_ld, 16)
            act.wait_ge(cw_ok, 1)

            for e in range(NE):
                def chunk(c, n, e=e):
                    for ht in range(HT):
                        k = n * HT + ht
                        act.wait_ge(up_mm, k + 1)
                        act.wait_ge(split_ok, k + 1)
                        nc.scalar.activation(hid[:, ht % RING], h_ps[ht % RING][:], ACT.Gelu_apprx_tanh,
                                             bias=late.b1c[:, e, ht:ht + 1]).then_inc(gelu_ok, 1)
                    act.wait_ge(down_mm, RING + (n + 1) * HT)
                    for t in range(TCH):
                        act.wait_ge(add_ok, n * TCH + t + 1)
                        nc.scalar.activation(part[:, t], y_ps[t][:, 0:C], ACT.Copy,
                                             scale=cw[:, c * TCH + t, e:e + 1]).then_inc(part_ok, 1)

                chunks(act, e, chunk)

        @block.vector
        def _(dve):
            dve.sem_inc(split_ok, RING)

            nc.vector.tensor_copy(logits[:], gate_ps[:]).then_inc(logits_ok, 1)
            for e in range(NE):
                nc.vector.memset(beats[:, :, e, e], 0.0)
            dve.wait_ge(logits_ok, 1)
            nc.vector.tensor_reduce(top[:], logits[:], AX.X, ALU.max).then_inc(top_ok, 1)
            compared = 0
            for i in range(NE):
                for js, beat in ((slice(0, i), ALU.is_gt), (slice(i + 1, NE), ALU.is_ge)):
                    if js.stop > js.start:
                        nc.vector.tensor_tensor(beats[:, :, js, i],
                                                logits[:, :, i:i + 1].broadcast_to([P, NT, js.stop - js.start]),
                                                logits[:, :, js], beat).then_inc(beats_ok, 1)
                        compared += 1
            dve.wait_ge(top_ok, 1)
            nc.vector.tensor_tensor(shifted[:], logits[:], top[:].unsqueeze(2).broadcast_to([P, NT, NE]),
                                    ALU.subtract).then_inc(shifted_ok, 1)
            dve.wait_ge(beats_ok, compared)
            nc.vector.tensor_reduce(rank[:], beats, AX.X, ALU.add).then_inc(rank_ok, 1)
            dve.wait_ge(rank_ok, 1)
            dve.wait_ge(gexp_ok, 1)
            nc.vector.scalar_tensor_tensor(out=kept[:], in0=rank[:], scalar=2.0, in1=weight[:], op0=ALU.is_lt,
                                           op1=ALU.mult).then_inc(kept_ok, 1)
            dve.wait_ge(kept_ok, 1)
            nc.vector.tensor_reduce(wsum[:], kept[:], AX.X, ALU.add).then_inc(wsum_ok, 1)
            dve.wait_ge(wsum_ok, 1)
            nc.vector.reciprocal(winv[:], wsum[:]).then_inc(winv_ok, 1)
            dve.wait_ge(winv_ok, 1)
            nc.vector.tensor_tensor(cw[:], kept[:], winv[:].unsqueeze(2).broadcast_to([P, NT, NE]),
                                    ALU.mult).then_inc(cw_ok, 1)
            dve.wait_ge(cw_ok, 1)
            dve.wait_ge(b2_ld, 16)

            def finish(tile):
                n = NT * (NE - 1) + tile
                dve.wait_ge(add_ok, TCH + n + 1)
                nc.vector.tensor_tensor(gated[:, tile % 2], acc[:, tile], mod_late[:, tile // KT, G_MLP:G_MLP + C],
                                        ALU.mult).then_inc(gated_ok, 1)
                dve.wait_ge(gated_ok, tile + 1)
                dve.wait_ge(x1_ld[tile % OUT], 16 * (tile // OUT + 1))
                if tile >= OUT:
                    dve.wait_ge(out_st[tile % OUT], 16 * (tile // OUT))
                nc.vector.tensor_tensor(res[:, tile % OUT], gated[:, tile % 2], x1[:, tile % OUT], ALU.add)\
                  .then_inc(res_ok, 1)

            for e in range(NE):
                def chunk(c, n, e=e):
                    for ht in range(HT):
                        k = n * HT + ht
                        dve.wait_ge(gelu_ok, RING + k + 1)
                        dve.wait_ge(down_mm, k + 1)
                        nc.vector.tensor_copy(hid_hi[:, ht % RING], hid[:, ht % RING]).then_inc(hi_ok, 1)
                        dve.wait_ge(hi_ok, k + 1)
                        nc.vector.tensor_tensor(hid_lo[:, ht % RING], hid[:, ht % RING], f32(hid_hi[:, ht % RING]),
                                                ALU.subtract).then_inc(split_ok, 1)
                        if 3 <= ht < 3 + TCH:
                            t = ht - 3
                            acc_t, cw_t = acc[:, c * TCH + t], cw[:, c * TCH + t, e:e + 1]
                            if e == 0:
                                nc.vector.tensor_scalar(acc_t, b2b[:, e], cw_t, None, ALU.mult).then_inc(bias_ok, 1)
                            else:
                                dve.wait_ge(add_ok, TCH + n * TCH + t + 1 - NT)
                                nc.vector.scalar_tensor_tensor(out=acc_t, in0=b2b[:, e], scalar=cw_t, in1=acc_t,
                                                               op0=ALU.mult, op1=ALU.add).then_inc(bias_ok, 1)
                        if e == NE - 1 and c >= 1 and ht in (2, 4, 6, 8):
                            finish(TCH * (c - 1) + ht // 2 - 1)

                chunks(dve, e, chunk)
            for t in range(NT - TCH, NT):
                finish(t)

        @block.tensor
        def _(pe):
            pe.sem_inc(down_mm, RING)
            for e in range(NE):
                pe.wait_ge(late.piece_ok, late.PIECES * (e + 1))

                def chunk(c, n, e=e):
                    w1s, w2s = late.places[e % 2]

                    def up(ht):
                        k = n * HT + ht
                        pe.wait_ge(gelu_ok, k + 1)
                        for i, (xs, xk, ws, wk) in enumerate(PRODUCTS):
                            mm = nc.tensor.matmul(h_ps[ht % RING][:], w1s[ws][:, wk, ht * P:(ht + 1) * P],
                                                  (x_hi, x_lo)[xs][:, xk, bass.ds(c * CH, CH)],
                                                  start=(i == 0), stop=(i == 6))
                        mm.then_inc(up_mm, 1)

                    def down(ht):
                        k = n * HT + ht
                        pe.wait_ge(split_ok, RING + k + 1)
                        for t in range(TCH):
                            if ht == 0:
                                pe.wait_ge(part_ok, n * TCH + t + 1)
                            s = slice(t * P, (t + 1) * P)
                            for i, (hs, ws) in enumerate(((hid_hi, 0), (hid_hi, 1), (hid_lo, 0))):
                                mm = nc.tensor.matmul(y_ps[t][:, 0:C], hs[:, ht % RING, s], w2s[ws][:, ht],
                                                      start=(ht == 0 and i == 0), stop=(ht == HT - 1 and i == 2))
                        mm.then_inc(down_mm, 1)

                    for ht in range(HT):
                        up(ht)
                        if ht >= LAG:
                            down(ht - LAG)
                    for ht in range(HT - LAG, HT):
                        down(ht)

                chunks(pe, e, chunk)


_INS = ["x", "cond_1152", "L0_cond_w_adaln", "L0_cond_b_adaln", "L0_cond_w_qkv", "L0_cond_b_qkv", "L0_cond_w_proj",
        "L0_cond_b_proj", "L0_cond_w_gate", "L0_cond_w1", "L0_cond_b1", "L0_cond_w2", "L0_cond_b2"]


def kernel(**inputs):
    import numpy as np
    import concourse.bacc as bacc
    from concourse.bass_utils import run_bass_kernel_spmd

    nc = bacc.Bacc("TRN2", target_bir_lowering=False, num_devices=1)
    arrays, args = {}, []
    for name in _INS:
        a = np.ascontiguousarray(inputs[name])
        arrays[f"in_{name}"] = a
        args.append(nc.dram_tensor(f"in_{name}", a.shape, mybir.dt.from_np(a.dtype), kind="ExternalInput").ap())
    out = nc.dram_tensor("out", (B, N, C), F32, kind="ExternalOutput").ap()
    build_kernel(nc, *args, out)
    r = run_bass_kernel_spmd(nc, [arrays], core_ids=[0])
    return r.results[0]["out"]
```
